# Optimizing a Trainium2 kernel written in Bass

```python
import numpy as np
import jax
import jax.numpy as jnp

def _softmax(x, axis=-1):
    return jax.nn.softmax(x, axis=axis)

def _gelu(x):
    return jax.nn.gelu(x, approximate=True)

def _silu(x):
    return jax.nn.silu(x)

def _sigmoid(x):
    return jax.nn.sigmoid(x)

def _layernorm(x, axis=-1, eps=1e-05):
    m = jnp.mean(x, axis=axis, keepdims=True)
    v = jnp.var(x, axis=axis, keepdims=True)
    return (x - m) / jnp.sqrt(v + eps)

def _scatter_add(tgt, idx, src, axis=0):
    return tgt.at[idx].add(src)

def _segment_sum(src, seg, n):
    return jax.ops.segment_sum(src, seg, n)
kernel_name = 'mk_audio_tower_d1_tok_audfeat512_r4_b992f4'

def setup_inputs(seed: int=0):
    np.random.seed(seed)
    _w = jnp.asarray

    def _rec_inputs():
        import jax
        import jax.numpy as jnp
        _rk = jax.random.key(seed)
        x = 7.22013e-05 + 1.00017 * jax.random.normal(jax.random.fold_in(_rk, 1), (16, 750, 128), jnp.float32)
        return x
    x = _rec_inputs()

    def _L0_tok_setup():
        import jax, jax.numpy as jnp
        import numpy as np
        H = 8
        TOP_FRAC = 0.2
        EPS = 1e-05

        def _layernorm(x, g, b):
            mu = jnp.mean(x, axis=-1, keepdims=True)
            var = jnp.mean((x - mu) ** 2, axis=-1, keepdims=True)
            return (x - mu) * jax.lax.rsqrt(var + EPS) * g + b
        key = jax.random.key(seed)
        ks = jax.random.split(key, 8)
        B, L, D, F = (8, 512, 128, 512)
        s = 0.02
        return {'x': jax.random.normal(ks[0], (B, L, D), jnp.float32), 'q_w': jax.random.normal(ks[1], (D, D), jnp.float32) * s, 'q_b': jnp.zeros((D,), jnp.float32), 'k_w': jax.random.normal(ks[2], (D, D), jnp.float32) * s, 'k_b': jnp.zeros((D,), jnp.float32), 'v_w': jax.random.normal(ks[3], (D, D), jnp.float32) * s, 'v_b': jnp.zeros((D,), jnp.float32), 'o_w': jax.random.normal(ks[4], (D, D), jnp.float32) * s, 'o_b': jnp.zeros((D,), jnp.float32), 'ln1_g': jnp.ones((D,), jnp.float32), 'ln1_b': jnp.zeros((D,), jnp.float32), 'f1_w': jax.random.normal(ks[5], (D, F), jnp.float32) * s, 'f1_b': jnp.zeros((F,), jnp.float32), 'f2_w': jax.random.normal(ks[6], (F, D), jnp.float32) * s, 'f2_b': jnp.zeros((D,), jnp.float32), 'ln2_g': jnp.ones((D,), jnp.float32), 'ln2_b': jnp.zeros((D,), jnp.float32), 'conv_w': jax.random.normal(ks[7], (D, D, 3), jnp.float32) * s, 'conv_b': jnp.zeros((D,), jnp.float32)}
    _L0_tok_all = _L0_tok_setup()
    _L0_tok_in = {k: v for k, v in _L0_tok_all.items() if k in ('q_w', 'q_b', 'k_w', 'k_b', 'v_w', 'v_b', 'o_w', 'o_b', 'ln1_g', 'ln1_b', 'f1_w', 'f1_b', 'f2_w', 'f2_b', 'ln2_g', 'ln2_b', 'conv_w', 'conv_b')}
    del _L0_tok_all

    def _L0_attn_setup():
        import jax, jax.numpy as jnp
        import numpy as np
        B, S, D = (8, 512, 128)
        key = jax.random.key(seed)
        k1, k2 = jax.random.split(key)
        lstm_out = jax.random.normal(k1, (B, S, D), dtype=jnp.float32)
        limit = float(np.sqrt(6.0 / (D + D)))
        attention_weights = jax.random.uniform(k2, (D, D), dtype=jnp.float32, minval=-limit, maxval=limit)
        return {'lstm_out': lstm_out, 'attention_weights': attention_weights}
    _L0_attn_all = _L0_attn_setup()
    _L0_attn_in = {k: v for k, v in _L0_attn_all.items() if k in ('attention_weights',)}
    del _L0_attn_all

    def _L0_ffn_setup():
        import jax, jax.numpy as jnp
        import numpy as np
        B, S, D = (8, 1024, 128)
        H = 512
        O = 128
        E = 8
        TOP_K = 1
        key = jax.random.key(seed)
        ks = jax.random.split(key, 8)
        sc = 0.02
        return {'x': jax.random.normal(ks[0], (B, S, D), dtype=jnp.float32), 'Wr': jax.random.normal(ks[1], (D, E), dtype=jnp.float32) * sc, 'br': jnp.zeros((E,), dtype=jnp.float32), 'W1': jax.random.normal(ks[2], (E, D, H), dtype=jnp.float32) * sc, 'b1': jnp.zeros((E, H), dtype=jnp.float32), 'W2': jax.random.normal(ks[3], (E, H, O), dtype=jnp.float32) * sc, 'b2': jnp.zeros((E, O), dtype=jnp.float32)}
    _L0_ffn_all = _L0_ffn_setup()
    _L0_ffn_in = {k: v for k, v in _L0_ffn_all.items() if k in ('Wr', 'br', 'W1', 'b1', 'W2', 'b2')}
    del _L0_ffn_all
    return {'x': x, 'L0_tok_q_w': _L0_tok_in['q_w'], 'L0_tok_q_b': _L0_tok_in['q_b'], 'L0_tok_k_w': _L0_tok_in['k_w'], 'L0_tok_k_b': _L0_tok_in['k_b'], 'L0_tok_v_w': _L0_tok_in['v_w'], 'L0_tok_v_b': _L0_tok_in['v_b'], 'L0_tok_o_w': _L0_tok_in['o_w'], 'L0_tok_o_b': _L0_tok_in['o_b'], 'L0_tok_ln1_g': _L0_tok_in['ln1_g'], 'L0_tok_ln1_b': _L0_tok_in['ln1_b'], 'L0_tok_f1_w': _L0_tok_in['f1_w'], 'L0_tok_f1_b': _L0_tok_in['f1_b'], 'L0_tok_f2_w': _L0_tok_in['f2_w'], 'L0_tok_f2_b': _L0_tok_in['f2_b'], 'L0_tok_ln2_g': _L0_tok_in['ln2_g'], 'L0_tok_ln2_b': _L0_tok_in['ln2_b'], 'L0_tok_conv_w': _L0_tok_in['conv_w'], 'L0_tok_conv_b': _L0_tok_in['conv_b'], 'L0_attn_attention_weights': _L0_attn_in['attention_weights'], 'L0_ffn_Wr': _L0_ffn_in['Wr'], 'L0_ffn_br': _L0_ffn_in['br'], 'L0_ffn_W1': _L0_ffn_in['W1'], 'L0_ffn_b1': _L0_ffn_in['b1'], 'L0_ffn_W2': _L0_ffn_in['W2'], 'L0_ffn_b2': _L0_ffn_in['b2']}

def reference(x, L0_tok_q_w, L0_tok_q_b, L0_tok_k_w, L0_tok_k_b, L0_tok_v_w, L0_tok_v_b, L0_tok_o_w, L0_tok_o_b, L0_tok_ln1_g, L0_tok_ln1_b, L0_tok_f1_w, L0_tok_f1_b, L0_tok_f2_w, L0_tok_f2_b, L0_tok_ln2_g, L0_tok_ln2_b, L0_tok_conv_w, L0_tok_conv_b, L0_attn_attention_weights, L0_ffn_Wr, L0_ffn_br, L0_ffn_W1, L0_ffn_b1, L0_ffn_W2, L0_ffn_b2):
    import jax
    import jax.numpy as jnp

    def _L0_tok_ref(x, q_w, q_b, k_w, k_b, v_w, v_b, o_w, o_b, ln1_g, ln1_b, f1_w, f1_b, f2_w, f2_b, ln2_g, ln2_b, conv_w, conv_b):
        import jax, jax.numpy as jnp
        import numpy as np
        H = 8
        TOP_FRAC = 0.2
        EPS = 1e-05

        def _layernorm(x, g, b):
            mu = jnp.mean(x, axis=-1, keepdims=True)
            var = jnp.mean((x - mu) ** 2, axis=-1, keepdims=True)
            return (x - mu) * jax.lax.rsqrt(var + EPS) * g + b
        B, L, D = x.shape
        hd = D // H
        scale = hd ** (-0.5)
        k_top = max(1, int(L * TOP_FRAC))

        def split_heads(t):
            return t.reshape(B, L, H, hd).transpose(0, 2, 1, 3)
        q = split_heads(x @ q_w + q_b)
        k = split_heads(x @ k_w + k_b)
        v = split_heads(x @ v_w + v_b)
        q_norm = jnp.sum(q * q, axis=-1)
        _, top_idx = jax.lax.top_k(q_norm, k_top)
        bi = jnp.arange(B)[:, None, None]
        hi = jnp.arange(H)[None, :, None]
        mask = jnp.zeros((B, H, L), bool).at[bi, hi, top_idx].set(True)
        q = q * mask[..., None]
        scores = jnp.einsum('bhld,bhmd->bhlm', q, k) * scale
        probs = jax.nn.softmax(scores, axis=-1)
        attn = jnp.einsum('bhlm,bhmd->bhld', probs, v)
        attn = attn.transpose(0, 2, 1, 3).reshape(B, L, D)
        attn_out = attn @ o_w + o_b
        h1 = _layernorm(x + attn_out, ln1_g, ln1_b)
        ff = jax.nn.relu(h1 @ f1_w + f1_b) @ f2_w + f2_b
        h2 = _layernorm(h1 + ff, ln2_g, ln2_b)
        fused = h2 + attn_out
        y = fused.transpose(0, 2, 1)
        y = jax.lax.conv_general_dilated(y, conv_w, window_strides=(1,), padding=[(1, 1)], dimension_numbers=('NCH', 'OIH', 'NCH')) + conv_b[None, :, None]
        y = jax.nn.relu(y)
        y = y.reshape(B, D, L // 2, 2).max(axis=-1)
        return y.transpose(0, 2, 1)

    def _L0_attn_ref(lstm_out, attention_weights):
        import jax, jax.numpy as jnp
        import numpy as np
        B, S, D = (8, 512, 128)
        proj = jnp.einsum('bsd,de->bse', lstm_out, attention_weights)
        scores = jnp.tanh(jnp.einsum('bsd,btd->bst', proj, lstm_out))
        attn = jax.nn.softmax(scores, axis=-1)
        return jnp.einsum('bst,btd->bsd', attn, lstm_out)

    def _L0_ffn_ref(x, Wr, br, W1, b1, W2, b2):
        import jax, jax.numpy as jnp
        import numpy as np
        B, S, D = (8, 1024, 128)
        H = 512
        O = 128
        E = 8
        TOP_K = 1
        b, s, d = x.shape
        xf = x.reshape(-1, d)
        router_logits = xf @ Wr + br
        topk_logits, topk_idx = jax.lax.top_k(router_logits, TOP_K)
        topk_gates = jax.nn.softmax(topk_logits, axis=1)
        out = jnp.zeros((xf.shape[0], O), dtype=x.dtype)
        for k in range(TOP_K):
            idx_k = topk_idx[:, k]
            gate_k = topk_gates[:, k:k + 1]
            for e in range(E):
                h = jax.nn.relu(xf @ W1[e] + b1[e])
                oe = h @ W2[e] + b2[e]
                mask = (idx_k == e)[:, None]
                out = out + jnp.where(mask, gate_k * oe, 0.0)
        return out.reshape(b, s, O)
    h = _L0_tok_ref(x, L0_tok_q_w, L0_tok_q_b, L0_tok_k_w, L0_tok_k_b, L0_tok_v_w, L0_tok_v_b, L0_tok_o_w, L0_tok_o_b, L0_tok_ln1_g, L0_tok_ln1_b, L0_tok_f1_w, L0_tok_f1_b, L0_tok_f2_w, L0_tok_f2_b, L0_tok_ln2_g, L0_tok_ln2_b, L0_tok_conv_w, L0_tok_conv_b)
    h = h + _L0_attn_ref(_layernorm(h, axis=-1), L0_attn_attention_weights)
    h = h + _L0_ffn_ref(_layernorm(h, axis=-1), L0_ffn_Wr, L0_ffn_br, L0_ffn_W1, L0_ffn_b1, L0_ffn_W2, L0_ffn_b2)
    return h

_drawn_inputs = setup_inputs


def setup_inputs(seed=0):
    import zlib

    import numpy as np

    out = dict(_drawn_inputs(seed))
    spreads = {'L0_tok_q_b': (0.0, 0.8),
     'L0_tok_k_b': (0.0, 0.8),
     'L0_tok_v_b': (0.0, 0.1),
     'L0_tok_o_b': (0.0, 0.1),
     'L0_tok_ln1_g': (1.0, 0.2),
     'L0_tok_ln1_b': (0.0, 0.1),
     'L0_tok_f1_b': (0.0, 0.1),
     'L0_tok_f2_b': (0.0, 0.1),
     'L0_tok_ln2_g': (1.0, 0.2),
     'L0_tok_ln2_b': (0.0, 0.1),
     'L0_tok_conv_b': (0.0, 0.1),
     'L0_ffn_br': (0.0, 0.1),
     'L0_ffn_b1': (0.0, 0.1),
     'L0_ffn_b2': (0.0, 0.1)}
    factors = {'L0_tok_q_w': 8.0, 'L0_tok_k_w': 8.0, 'L0_tok_v_w': 6.892}
    for name, (base, spread) in spreads.items():
        noise = np.random.default_rng([zlib.crc32(name.encode()), seed]).standard_normal(out[name].shape)
        drawn = base * np.exp(spread * noise) if base else spread * noise
        out[name] = jnp.asarray(drawn.astype(out[name].dtype))
    for name, factor in factors.items():
        out[name] = (out[name] * factor).astype(out[name].dtype)
    return out
```

```python
from contextlib import ExitStack

import concourse.bass as bass
from concourse import mybir
import numpy as np

F32 = mybir.dt.float32
BF16 = mybir.dt.bfloat16
I32 = mybir.dt.int32
ALU = mybir.AluOpType
ACT = mybir.ActivationFunctionType
AX = mybir.AxisListType

NB, L, D = 16, 750, 128
H = 8
HD = D // H
SCALE = float(HD) ** -0.5
K_TOP = max(1, int(L * 0.2))
EPS = 1e-5
FF = 512
TT = 125
NT = L // TT
HALF = L // 2
NG = NB * H
JT = 76
NJ = 2 * JT
PARTS = 6
KR = PARTS * HD
S = L // 2
ST = S // TT
NTILE = NB * ST
E = 8
EH = 512
BLK = 128
NBLK = (NB * S) // BLK + E
assert NT * TT == L and ST * TT == S and K_TOP + 2 == NJ and NG == 128

COLS = ["o_b", "ln1_g", "ln1_b", "f2_b", "ln2_g", "ln2_b", "conv_b", "f1_b0", "f1_b1", "f1_b2", "f1_b3"]


def norms_and_ranks(nc, t, io):
    with ExitStack() as ctx:
        def sb(name, shape, dt=F32):
            return ctx.enter_context(nc.sbuf_tensor(name, shape, dt))

        def sem(name):
            return ctx.enter_context(nc.semaphore(name))

        wq = sb("wq", [D, D])
        qb = sb("qb_rows", [TT, D])
        x_in = [sb(f"x_in1{p}", [TT, NT, D]) for p in range(2)]
        xT = [sb(f"xT1{p}", [D, L]) for p in range(2)]
        q_sb = [sb(f"q_sb{p}", [TT, NT * D]) for p in range(2)]
        sq = [sb(f"sq{p}", [TT, NT * D]) for p in range(2)]
        qn_tok = sb("qn_tok", [TT, NT, NG])
        qn = sb("qn", [NG, L])
        top8 = sb("top8", [NG, 8])
        ones = sb("ones_row", [NG, L])
        count = sb("count", [NG, L])
        rank = sb("rank", [NG, L])
        rank_bf = sb("rank_bf", [NG, L], BF16)
        xT_ps = [ctx.enter_context(nc.psum_tensor(f"xT_ps{p}", [D, 2, 512], F32)) for p in range(2)]
        q_ps = [ctx.enter_context(nc.psum_tensor(f"q_ps{p}", [D, 2, 512], F32)) for p in range(2)]

        w_loaded = sem("w_loaded")
        x_loaded = [sem(f"x_loaded1{p}") for p in range(2)]
        xT_done = [sem(f"xT_done1{p}") for p in range(2)]
        xT_ready = [sem(f"xT_ready1{p}") for p in range(2)]
        q_done = [sem(f"q_done{p}") for p in range(2)]
        q_ready = [sem(f"q_ready{p}") for p in range(2)]
        q_stored = [sem(f"q_stored{p}") for p in range(2)]
        sq_ready = [sem(f"sq_ready{p}") for p in range(2)]
        norm_ready = [sem(f"norm_ready{p}") for p in range(2)]
        norms_turned = sem("norms_turned")
        top = sem("top_step")
        ranks_ready = sem("ranks_ready")
        ranks_turned = sem("ranks_turned")
        ranks_out = sem("ranks_out")
        x_v = io["x"].rearrange("b (n p) d -> b p n d", p=TT)

        with nc.Block() as block:
            @block.sync
            def _(sp):
                sp.dma_start(t["ident"][:, :], io["c_ident"]).then_inc(w_loaded, 16)
                sp.dma_start(wq[:, :], io["L0_tok_q_w"]).then_inc(w_loaded, 16)
                sp.dma_start(qb[:, :], io["L0_tok_q_b"].rearrange("(a n) -> a n", a=1).to_broadcast([TT, D])).then_inc(w_loaded, 16)
                with sp.Fori(0, NB // 2) as i:
                    for p in range(2):
                        sp.wait_ge(xT_done[p], i)
                        sp.dma_start(x_in[p][:, :, :], x_v[bass.ds(2 * i + p, 1), :, :, :].rearrange("b p n d -> (b p) n d"))\
                          .then_inc(x_loaded[p], 16)
                sp.wait_ge(ranks_ready, 1)
                sp.dma_start(io["rank_rows"], rank_bf[:, :]).then_inc(ranks_out, 16)
                sp.wait_ge(ranks_out, 16)

            @block.tensor
            def _(pe):
                pe.wait_ge(w_loaded, 48)
                with pe.Fori(0, NB // 2) as i:
                    for p in range(2):
                        pe.wait_ge(x_loaded[p], 16 * i + 16)
                        pe.wait_ge(xT_ready[p], i)
                        for n in range(NT):
                            mm = pe.transpose(xT_ps[p][:, n // 3, (n % 3) * TT:(n % 3 + 1) * TT],
                                              x_in[p][:, n, :], t["ident"][0:TT, 0:TT])
                        mm.then_inc(xT_done[p], 1)
                    for p in range(2):
                        pe.wait_ge(xT_ready[p], i + 1)
                        pe.wait_ge(q_ready[p], i)
                        for n in range(NT):
                            mm = pe.matmul(q_ps[p][0:TT, n // 3, (n % 3) * D:(n % 3 + 1) * D],
                                           xT[p][:, n * TT:(n + 1) * TT], wq[:, :], start=True, stop=True)
                        mm.then_inc(q_done[p], 1)
                for p in range(2):
                    pe.wait_ge(norm_ready[p], NB // 2)
                for n in range(NT):
                    mm = pe.transpose(xT_ps[0][:, n // 3, (n % 3) * TT:(n % 3 + 1) * TT], qn_tok[:, n, :],
                                      t["ident"][0:TT, 0:TT])
                mm.then_inc(norms_turned, 1)
                pe.wait_ge(ranks_ready, 1)
                for n in range(NT):
                    mm = pe.transpose(q_ps[0][0:TT, n // 3, (n % 3) * NG:(n % 3 + 1) * NG], rank[:, n * TT:(n + 1) * TT],
                                      t["ident"][:, :])
                mm.then_inc(ranks_turned, 1)

            @block.scalar
            def _(act):
                with act.Fori(0, NB // 2) as i:
                    for p in range(2):
                        act.wait_ge(xT_done[p], i + 1)
                        act.wait_ge(q_done[p], i)
                        act.activation(xT[p][:, :].rearrange("p (a c) -> p a c", a=2), xT_ps[p][:, :, 0:HALF],
                                       ACT.Copy).then_inc(xT_ready[p], 1)
                    for p in range(2):
                        act.wait_ge(q_ready[p], i + 1)
                        act.wait_ge(norm_ready[p], i)
                        act.activation(sq[p][:, :], q_sb[p][:, :], ACT.Square).then_inc(sq_ready[p], 1)
                        act.dma_start(io["q_rows"][bass.ds(2 * i + p, 1), :, :].rearrange("b p n -> (b p) n"), q_sb[p][:, :])\
                           .then_inc(q_stored[p], 16)
                for p in range(2):
                    act.wait_ge(q_stored[p], 16 * (NB // 2))

            @block.vector
            def _(dve):
                step = [0]

                def chain(ins):
                    step[0] += 1
                    ins.then_inc(top, 1)
                    dve.wait_ge(top, step[0])

                chain(dve.memset(ones[:, :], 1.0))
                dve.wait_ge(w_loaded, 48)
                with dve.Fori(0, NB // 2) as i:
                    for p in range(2):
                        dve.wait_ge(q_done[p], i + 1)
                        dve.wait_ge(q_stored[p], 16 * i)
                        dve.wait_ge(sq_ready[p], i)
                        dve.tensor_tensor(
                            q_sb[p][:, :].rearrange("p (a n d) -> p a n d", a=2, n=3),
                            q_ps[p][0:TT, :, 0:3 * D].rearrange("p a (n d) -> p a n d", n=3),
                            qb[:, :].unsqueeze(1).unsqueeze(1).to_broadcast([TT, 2, 3, D]), ALU.add).then_inc(q_ready[p], 1)
                    for p in range(2):
                        dve.wait_ge(sq_ready[p], i + 1)
                        dve.tensor_reduce(qn_tok[:, :, bass.ds((2 * i + p) * H, H)],
                                          sq[p][:, :].rearrange("p (n h d) -> p n h d", n=NT, h=H), AX.X, ALU.add)\
                           .then_inc(norm_ready[p], 1)
                dve.wait_ge(norms_turned, 1)
                chain(dve.tensor_copy(qn[:, :].rearrange("p (a c) -> p a c", a=2), xT_ps[0][:, :, 0:HALF]))
                left = K_TOP
                while left > 0:
                    chain(dve.max(top8[:, :], qn[:, :]))
                    if left < 8:
                        chain(dve.memset(top8[:, left:8], -1.0))
                    chain(dve.match_replace(qn[:, :], top8[:, :], qn[:, :], -1.0))
                    left -= 8
                chain(dve.tensor_scalar(qn[:, :], qn[:, :], -1.0, None, ALU.is_equal))
                chain(dve.tensor_tensor_scan(count[:, :], ones[:, :], qn[:, :], 0.0, ALU.mult, ALU.add))
                chain(dve.tensor_tensor(count[:, :], count[:, :], qn[:, :], ALU.mult))
                chain(dve.tensor_scalar(rank[:, :], count[:, :], -1.0, None, ALU.add))
                dve.tensor_copy(rank_bf[:, :], rank[:, :]).then_inc(ranks_ready, 1)
                dve.wait_ge(ranks_turned, 1)
                dve.tensor_copy(t["rank_tok"][:, :, :].rearrange("p (a n) g -> p a n g", a=2),
                                q_ps[0][0:TT, :, 0:3 * NG].rearrange("p a (n g) -> p a n g", n=3))


def sequences(nc, t, io):
    A_TILES = ["xT", "k", "v"] + [f"kt{i}" for i in range(4)] + ["g0", "g1"] \
        + [f"max{i}" for i in range(2 * H)] + [f"s{h}" for h in range(H)] + ["at"]
    D_TILES = ["sc0", "sc1", "o", "c1", "m1", "f0", "f1", "f2", "f3", "ff", "c2", "m2", "cv", "ht"]
    A_SLOTS = 2
    A_PER = len(A_TILES) // A_SLOTS
    D_PER = len(D_TILES)
    assert A_PER * A_SLOTS == len(A_TILES)

    with ExitStack() as ctx:
        def sb(name, shape, dt=F32):
            return ctx.enter_context(nc.sbuf_tensor(name, shape, dt))

        def sem(name):
            return ctx.enter_context(nc.semaphore(name))

        wkv = sb("wkv", [D, 2 * D])
        kvb = sb("kvb_rows", [TT, 2 * D])
        wo = sb("wo_pad", [128, 2, D])
        f1 = sb("f1", [D, FF])
        f2 = sb("f2", [128, FF // 128, D])
        cw = sb("conv_taps", [D, 3, D])
        cols = sb("feature_cols", [D, len(COLS)])
        center = sb("center", [D, D])
        mean = sb("mean", [D, D])
        ident_bf = sb("ident_bf", [128, 128], BF16)
        iota = sb("iota_f", [TT, NJ])
        iota_bf = sb("iota_bf", [TT, NJ], BF16)
        slot_id = sb("slot_id", [JT, 2])
        eps = sb("eps", [D, 1])
        x_in = sb("x_in", [TT, NT, D])
        q_in = sb("q_in", [TT, NT * H, HD])
        xT = [sb(f"xT{p}", [D, L]) for p in range(2)]
        kf = sb("kf", [TT, NT * H, HD])
        q_rest = sb("q_rest", [TT, NT * H, HD])
        k_rest = sb("k_rest", [TT, NT * H, HD])
        qst = sb("qst", [TT, NT * H, PARTS, HD], BF16)
        kst = sb("kst", [TT, NT * H, PARTS, HD], BF16)
        v_pad = sb("v_pad", [TT, NT, H, 32])
        rank_cur = sb("rank_cur", [TT, NT, H])
        rank_bc = sb("rank_bc", [JT, H * L], BF16)
        G = sb("G", [TT, NT, H, NJ], BF16)
        GT = sb("GT", [JT, 2, H * L], BF16)
        kT = sb("kT", [KR + 3, H, L], BF16)
        qT = sb("qT", [KR + 3, H * NJ], BF16)
        mx = sb("mx", [JT, 2 * H])
        mx_rest = sb("mx_rest", [JT, 2 * H])
        mx_rest2 = sb("mx_rest2", [JT, 2 * H])
        mxp = sb("mxp", [JT, 3, 2 * H], BF16)
        mxT = sb("mxT", [6 * H, JT], BF16)
        Pt = sb("Pt", [TT, H, NT * NJ])
        au = sb("au", [128, 2, NJ])
        rden = sb("rden", [JT, 4, 4])
        att = sb("att", [JT, 512])
        att_rest = sb("att_rest", [JT, 512])
        attp = sb("attp", [JT, 3, 512], BF16)
        attT = sb("attT", [128, 2, L])
        ao = sb("ao", [D, L])
        aob = sb("aob", [D, L])
        r = sb("r", [D, L])
        cS = sb("cS", [D, L])
        sq = sb("sqD", [D, L])
        h1 = sb("h1", [D, L])
        rl = sb("rl", [128, FF // 128, L])
        fu = sb("fu", [D, L + 2])
        hp = sb("hp", [D, S])
        hT = sb("hT", [D, S])
        h_sb = sb("h_sb", [TT, ST * D])

        a_ps = [ctx.enter_context(nc.psum_tensor(f"a_ps{s}", [128, 2, 512], F32)) for s in range(A_SLOTS)]
        d_ps = ctx.enter_context(nc.psum_tensor("d_ps", [128, 2, 512], F32))
        pv_ps = ctx.enter_context(nc.psum_tensor("pv_ps", [128, 512], F32))
        mt_ps = ctx.enter_context(nc.psum_tensor("mt_ps", [128, 1024], BF16))

        const_loaded = sem("const_loaded")
        const_made = sem("const_made")
        const_set = sem("const_set")
        wo_cleared = sem("wo_cleared")
        a_done = [sem(f"a_done{s}") for s in range(A_SLOTS)]
        a_free = [sem(f"a_free{s}") for s in range(A_SLOTS)]
        d_done = sem("d_done")
        d_free = sem("d_free")
        x_loaded = sem("x_loaded")
        q_loaded = sem("q_loaded")
        rank_loaded = sem("rank_loaded")
        k_step = sem("k_step")
        q_step = sem("q_step")
        kst_ready = sem("kst_ready")
        qst_ready = sem("qst_ready")
        cur_ready = sem("cur_ready")
        g_ready = sem("g_ready")
        gt_ready = sem("gt_ready")
        mx_step = sem("mx_step")
        mxp_ready = sem("mxp_ready")
        mx_turned = sem("mx_turned")
        mxT_ready = sem("mxT_ready")
        mx_rows = sem("mx_rows")
        pv_done = [sem(f"pv_done{q}") for q in range(2)]
        au_ready = sem("au_ready")
        att_step = sem("att_step")
        attp_ready = sem("attp_ready")
        r_ready = sem("r_ready")
        aob_ready = sem("aob_ready")
        sq_ready = sem("sq_readyD")
        ln_step = sem("ln_step")
        rstd_ready = sem("rstd_ready")
        n_ready = sem("n_ready")
        h1_ready = sem("h1_ready")
        fu_ready = sem("fu_ready")
        hp_ready = sem("hp_ready")
        hT_ready = sem("hT_ready")
        h_ready = sem("h_ready")
        h_stored = sem("h_stored")
        gates = {eng: sem(f"gate_{n}") for n, eng in (("sp", nc.sync), ("pool", nc.gpsimd), ("pe", nc.tensor))}

        def a_slot(name):
            return A_TILES.index(name) % A_SLOTS

        def a_count(name, b):
            return A_PER * (b + 1) + A_TILES.index(name) // A_SLOTS + 1

        def a_tile(name):
            return a_ps[a_slot(name)]

        def d_count(name, b):
            return D_PER * (b + 1) + D_TILES.index(name) + 1

        def await_a(eng, what, name, b):
            eng.wait_ge(what[a_slot(name)], a_count(name, b))

        def col(name):
            return cols[:, COLS.index(name):COLS.index(name) + 1]

        def gate(eng):
            eng.sem_inc(gates[eng], 1)

        def two(ap):
            return ap.rearrange("p (a c) -> p a c", a=2)

        def two_of_three(ap, n):
            return ap[0:TT, :, 0:3 * n].rearrange("p a (t c) -> p a t c", t=3)

        KTS = TT + 1

        def turned_k(i):
            return a_tile(f"kt{i}")[0:KR, :, 0:NT * KTS // 2].bitcast(BF16).rearrange("p g (n c) -> p g n c", n=NT)[:, :, :, 0:TT]

        x_v = io["x"].rearrange("b (n p) d -> b p n d", p=TT)

        def run(eng, part_a, part_d):
            def both(b, pb):
                for part, step in ORDER:
                    if part == "A" and b is not None and step in part_a:
                        part_a[step](b, pb)
                    if part == "D" and step in part_d:
                        part_d[step](b - 1, 1 - pb)
            for part, step in ORDER:
                if part == "A" and step in part_a:
                    part_a[step](0, 0)
            with eng.Fori(0, NB // 2 - 1) as i:
                both(2 * i + 1, 1)
                both(2 * i + 2, 0)
            both(NB - 1, 1)
            for part, step in ORDER:
                if part == "D" and step in part_d:
                    part_d[step](NB - 1, 1)

        ORDER = order()

        with nc.Block() as block:
            @block.sync
            def _(sp):
                loads = [(wkv[:, 0:D], io["L0_tok_k_w"]), (wkv[:, D:2 * D], io["L0_tok_v_w"]),
                         (kvb[:, 0:D], io["L0_tok_k_b"].rearrange("(a n) -> a n", a=1).to_broadcast([TT, D])),
                         (kvb[:, D:2 * D], io["L0_tok_v_b"].rearrange("(a n) -> a n", a=1).to_broadcast([TT, D])),
                         (f1[:, :], io["L0_tok_f1_w"]), (f2[:, :, :], io["L0_tok_f2_w"].rearrange("(c p) d -> p c d", p=128)),
                         (cw[:, :, :], io["conv_w"]), (cols[:, :], io["cols"]), (center[:, :], io["c_center"]),
                         (iota[:, :], io["c_iota"].to_broadcast([TT, NJ])), (slot_id[:, :], io["c_slot_id"])]
                for dst, src in loads:
                    sp.dma_start(dst, src).then_inc(const_loaded, 16)
                sp.wait_ge(wo_cleared, 1)
                for h in range(H):
                    sp.dma_start(wo[32 * (h % 4):32 * (h % 4) + HD, h // 4, :], io["L0_tok_o_w"][HD * h:HD * (h + 1), :])\
                      .then_inc(const_loaded, 16)
                CONSTS = len(loads) + H
                assert CONSTS == N_CONST

                def load(b, pb):
                    await_a(sp, a_done, "xT", b - 1)
                    gate(sp)
                    sp.dma_start(x_in[:, :, :], x_v[bass.ds(b, 1), :, :, :].rearrange("b p n d -> (b p) n d")).then_inc(x_loaded, 16)
                    sp.wait_ge(qst_ready, b)
                    gate(sp)
                    sp.dma_start(q_in[:, :, :].rearrange("p g d -> p (g d)"),
                                 io["q_rows"][bass.ds(b, 1), :, :].rearrange("b p n -> (b p) n")).then_inc(q_loaded, 16)
                    sp.wait_ge(gt_ready, b)
                    gate(sp)
                    sp.dma_start(rank_bc[:, :], io["rank_rows"].rearrange("(b h) l -> b (h l)", h=H)[bass.ds(b, 1), :]
                                 .to_broadcast([JT, H * L])).then_inc(rank_loaded, 16)

                def max_rows(b, pb):
                    sp.wait_ge(mxT_ready, b + 1)
                    gate(sp)
                    for k in range(3):
                        sp.dma_start(qT[KR + k:KR + k + 1, :], mxT[2 * H * k:2 * H * (k + 1), :]).then_inc(mx_rows, 16)

                def store_h(b, pb):
                    sp.wait_ge(h_ready, b + 1)
                    gate(sp)
                    sp.dma_start(io["h_rows"][bass.ds(b, 1), :, :].rearrange("b p n -> (b p) n"), h_sb[:, :]).then_inc(h_stored, 16)

                run(sp, {"load": load, "mx": max_rows}, {"ht": store_h})
                sp.wait_ge(h_stored, 16 * NB)

            @block.gpsimd
            def _(pool):
                pool.wait_ge(const_loaded, 16 * N_CONST)
                pool.tensor_copy(iota_bf[:, :], iota[:, :]).then_inc(const_made, 1)
                pool.tensor_copy(ident_bf[:, :], t["ident"][:, :]).then_inc(const_made, 1)

                def split(src, rest, st, places, step, ready, b):
                    first, second, third = places
                    base = 3 * b
                    gate(pool)
                    pool.tensor_copy(st[:, :, first[0], :], src[:, :, :]).then_inc(step, 1)
                    pool.wait_ge(step, base + 1)
                    pool.tensor_tensor(rest[:, :, :], src[:, :, :], st[:, :, first[0], :], ALU.subtract).then_inc(step, 1)
                    pool.wait_ge(step, base + 2)
                    gate(pool)
                    pool.tensor_copy(st[:, :, second[0], :], rest[:, :, :]).then_inc(step, 1)
                    for to in first[1:]:
                        pool.tensor_copy(st[:, :, to, :], st[:, :, first[0], :])
                    pool.wait_ge(step, base + 3)
                    pool.tensor_tensor(st[:, :, third[0], :], rest[:, :, :], st[:, :, second[0], :], ALU.subtract)
                    for n, to in enumerate(second[1:]):
                        pool.tensor_copy(st[:, :, to, :], st[:, :, second[0], :])
                    pool.drain().then_inc(ready, 1)

                def q_parts(b, pb):
                    pool.wait_ge(q_loaded, 16 * b + 16)
                    await_a(pool, a_done, "g1", b - 1)
                    split(q_in, q_rest, qst, ([0, 1, 2], [3, 4], [5]), q_step, qst_ready, b)

                def k_parts(b, pb):
                    await_a(pool, a_free, "k", b)
                    await_a(pool, a_done, "kt3", b - 1)
                    split(kf, k_rest, kst, ([0, 3, 5], [1, 4], [2]), k_step, kst_ready, b)

                def residual_bias(b, pb):
                    pool.wait_ge(d_free, d_count("o", b))
                    pool.wait_ge(fu_ready, b)
                    gate(pool)
                    pool.tensor_scalar(aob[:, :], ao[:, :], col("ln2_b"), None, ALU.add).then_inc(aob_ready, 1)

                run(pool, {"load": q_parts, "k": k_parts}, {"o": residual_bias})

            @block.tensor
            def _(pe):
                for s in a_done:
                    pe.sem_inc(s, A_PER)
                pe.sem_inc(d_done, D_PER)
                pe.wait_ge(const_loaded, 16 * N_CONST)
                pe.wait_ge(const_made, 2)
                pe.wait_ge(const_set, 6)

                def taken(b, names, fill=None):
                    for slot in range(A_SLOTS):
                        counts = [A_TILES.index(n) for n in names if a_slot(n) == slot]
                        if fill is not None and a_slot(fill) == slot:
                            counts.append(A_TILES.index(fill) - A_SLOTS)
                        if counts:
                            pe.wait_ge(a_free[slot], A_PER * (b + 1) + max(counts) // A_SLOTS + 1)

                def fill_a(name, b, reads=()):
                    taken(b, reads, name)
                    return a_tile(name)

                def filled_a(mm, name):
                    mm.then_inc(a_done[a_slot(name)], 1)

                def fill_d(name, b):
                    pe.wait_ge(d_free, d_count(name, b) - 1)
                    return d_ps

                def turn_x(b, pb):
                    pe.wait_ge(x_loaded, 16 * b + 16)
                    ps = fill_a("xT", b)
                    for n in range(NT):
                        mm = pe.transpose(ps[:, n // 3, (n % 3) * TT:(n % 3 + 1) * TT], x_in[:, n, :], t["ident"][0:TT, 0:TT])
                    filled_a(mm, "xT")

                def project(name, w):
                    def go(b, pb):
                        ps = fill_a(name, b, ["xT"])
                        for n in range(NT):
                            mm = pe.matmul(ps[0:TT, n // 3, (n % 3) * D:(n % 3 + 1) * D], xT[pb][:, n * TT:(n + 1) * TT], w,
                                           start=True, stop=True)
                        filled_a(mm, name)
                    return go

                def turn_k(i):
                    def go(b, pb):
                        pe.wait_ge(kst_ready, b + 1)
                        ps = fill_a(f"kt{i}", b)
                        for g in range(2):
                            for n in range(NT):
                                mm = pe.transpose(ps[0:KR, g, :].bitcast(BF16)[:, n * KTS:n * KTS + TT],
                                                  kst[:, n * H + 2 * i + g, :, :].rearrange("p a d -> p (a d)"),
                                                  ident_bf[0:TT, 0:TT])
                        filled_a(mm, f"kt{i}")
                    return go

                def gather(i):
                    def go(b, pb):
                        pe.wait_ge(qst_ready, b + 1)
                        pe.wait_ge(g_ready, b + 1)
                        ps = fill_a(f"g{i}", b)
                        for g in range(4):
                            h = 4 * i + g
                            for n in range(NT):
                                mm = pe.matmul(ps[0:KR, g // 2, (g % 2) * NJ:(g % 2 + 1) * NJ],
                                               qst[:, n * H + h, :, :].rearrange("p a d -> p (a d)"), G[:, n, h, :],
                                               start=(n == 0), stop=(n == NT - 1))
                        filled_a(mm, f"g{i}")
                    return go

                def scores_for_max(i):
                    h, jt = i // 2, i % 2

                    def go(b, pb):
                        ps = fill_a(f"max{i}", b, [f"kt{h // 2}", f"g{h // 4}"])
                        for c in range(2):
                            mm = pe.matmul(ps[0:JT, c, 0:HALF], qT[0:KR, i * JT:(i + 1) * JT],
                                           kT[0:KR, h, c * HALF:(c + 1) * HALF], start=True, stop=True)
                        filled_a(mm, f"max{i}")
                    return go

                def turn_max(b, pb):
                    pe.wait_ge(mxp_ready, b + 1)
                    pe.wait_ge(mxT_ready, b)
                    gate(pe)
                    pe.transpose(mt_ps[0:6 * H, 0:JT], mxp[:, :, :].rearrange("p a s -> p (a s)"), ident_bf[0:JT, 0:JT])\
                      .then_inc(mx_turned, 1)

                def scores(h):
                    def go(b, pb):
                        pe.wait_ge(mx_rows, 48 * b + 48)
                        ps = fill_a(f"s{h}", b)
                        for n in range(NT):
                            mm = pe.matmul(ps[0:TT, n // 3, (n % 3) * NJ:(n % 3 + 1) * NJ], kT[:, h, n * TT:(n + 1) * TT],
                                           qT[:, h * NJ:(h + 1) * NJ], start=True, stop=True)
                        filled_a(mm, f"s{h}")
                    return go

                def values(q):
                    def go(b, pb):
                        taken(b, ["v"] + [f"s{4 * q + g}" for g in range(4)])
                        pe.wait_ge(au_ready, b)
                        for n in range(NT):
                            for g in range(4):
                                mm = pe.matmul(pv_ps[32 * g:32 * g + 32, q * NJ:(q + 1) * NJ], v_pad[:, n, 4 * q + g, :],
                                               Pt[:, 4 * q + g, n * NJ:(n + 1) * NJ], start=(n == 0), stop=(n == NT - 1))
                        mm.then_inc(pv_done[q], 1)
                    return go

                def turn_att(b, pb):
                    pe.wait_ge(au_ready, b + 1)
                    ps = fill_a("at", b)
                    for q in range(2):
                        for jt in range(2):
                            mm = pe.transpose(ps[0:JT, 0, (2 * q + jt) * 128:(2 * q + jt + 1) * 128],
                                              au[:, q, jt * JT:(jt + 1) * JT], t["ident"][:, :])
                    filled_a(mm, "at")

                def scatter(q):
                    def go(b, pb):
                        pe.wait_ge(attp_ready, b + 1)
                        pe.wait_ge(gt_ready, b + 1)
                        ps = fill_d(f"sc{q}", b)
                        for c in range(2):
                            for k in range(3):
                                for jt in range(2):
                                    for g in range(4):
                                        h = 4 * q + g
                                        at = (2 * q + jt) * 128 + 32 * g
                                        mm = pe.matmul(ps[32 * g:32 * g + 32, c, 0:HALF], attp[:, k, at:at + 32],
                                                       GT[:, jt, h * L + c * HALF:h * L + (c + 1) * HALF],
                                                       start=(k == 0 and jt == 0), stop=(k == 2 and jt == 1))
                        mm.then_inc(d_done, 1)
                    return go

                def dense(name, terms, waits):
                    def go(b, pb):
                        for w in waits:
                            w(b)
                        ps = fill_d(name, b)
                        for c in range(2):
                            for k, (w, data) in enumerate(terms):
                                mm = pe.matmul(ps[:, c, 0:HALF], w, data[:, c * HALF:(c + 1) * HALF],
                                               start=(k == 0), stop=(k == len(terms) - 1))
                        mm.then_inc(d_done, 1)
                    return go

                def convolve(b, pb):
                    pe.wait_ge(fu_ready, b + 1)
                    ps = fill_d("cv", b)
                    for c, (at, n) in enumerate(((0, HALF + 1), (HALF + 1, HALF - 1))):
                        for tap in range(3):
                            mm = pe.matmul(ps[:, c, 0:n], cw[:, tap, :], fu[:, at + tap:at + tap + n],
                                           start=(tap == 0), stop=(tap == 2))
                    mm.then_inc(d_done, 1)

                def turn_h(b, pb):
                    pe.wait_ge(hT_ready, b + 1)
                    ps = fill_d("ht", b)
                    for n in range(ST):
                        mm = pe.transpose(ps[0:TT, 0, n * D:(n + 1) * D], hT[:, n * TT:(n + 1) * TT], t["ident"][:, :])
                    mm.then_inc(d_done, 1)

                part_a = {"xT": turn_x, "k": project("k", wkv[:, 0:D]), "v": project("v", wkv[:, D:2 * D]),
                          "mx": turn_max, "at": turn_att}
                for i in range(4):
                    part_a[f"kt{i}"] = turn_k(i)
                for i in range(2):
                    part_a[f"g{i}"] = gather(i)
                    part_a[f"pv{i}"] = values(i)
                for i in range(2 * H):
                    part_a[f"max{i}"] = scores_for_max(i)
                for h in range(H):
                    part_a[f"s{h}"] = scores(h)
                part_d = {"sc0": scatter(0), "sc1": scatter(1), "cv": convolve, "ht": turn_h}
                part_d["o"] = dense("o", [(wo[:, 0, :], attT[:, 0, :]), (wo[:, 1, :], attT[:, 1, :])],
                                    [lambda b: pe.wait_ge(d_free, d_count("sc1", b))])
                part_d["c1"] = dense("c1", [(center[:, :], r[:, :])], [lambda b: pe.wait_ge(r_ready, 2 * b + 1)])
                part_d["m1"] = dense("m1", [(mean[:, :], sq[:, :])], [lambda b: pe.wait_ge(sq_ready, 2 * b + 1)])
                for i in range(4):
                    part_d[f"f{i}"] = dense(f"f{i}", [(f1[:, i * 128:(i + 1) * 128], h1[:, :])],
                                            [lambda b: pe.wait_ge(h1_ready, b + 1)])
                part_d["ff"] = dense("ff", [(f2[:, i, :], rl[:, i, :]) for i in range(4)],
                                     [lambda b: pe.wait_ge(d_free, d_count("f3", b))])
                part_d["c2"] = dense("c2", [(center[:, :], r[:, :])], [lambda b: pe.wait_ge(r_ready, 2 * b + 2)])
                part_d["m2"] = dense("m2", [(mean[:, :], sq[:, :])], [lambda b: pe.wait_ge(sq_ready, 2 * b + 2)])
                run(pe, part_a, part_d)

            @block.scalar
            def _(act):
                for s in a_free:
                    act.sem_inc(s, A_PER)
                act.sem_inc(d_free, D_PER)
                act.wait_ge(const_loaded, 16 * N_CONST)
                act.wait_ge(const_made, 2)
                act.wait_ge(const_set, 6)

                def take_xT(b, pb):
                    await_a(act, a_done, "xT", b)
                    act.wait_ge(r_ready, 2 * b - 2 if not isinstance(b, int) else max(2 * b - 2, 0))
                    act.activation(two(xT[pb][:, :]), a_tile("xT")[:, :, 0:HALF], ACT.Copy).then_inc(a_free[a_slot("xT")], 1)

                def take_kT(i):
                    def go(b, pb):
                        await_a(act, a_done, f"kt{i}", b)
                        act.activation(kT[0:KR, 2 * i:2 * i + 2, :].rearrange("p g (n c) -> p g n c", n=NT), turned_k(i), ACT.Copy)\
                           .then_inc(a_free[a_slot(f"kt{i}")], 1)
                    return go

                def take_qT(i):
                    def go(b, pb):
                        await_a(act, a_done, f"g{i}", b)
                        act.activation(qT[0:KR, i * 4 * NJ:(i + 1) * 4 * NJ].rearrange("p (a c) -> p a c", a=2),
                                       a_tile(f"g{i}")[0:KR, :, 0:2 * NJ], ACT.Copy).then_inc(a_free[a_slot(f"g{i}")], 1)
                    return go

                def exps(h):
                    def go(b, pb):
                        await_a(act, a_done, f"s{h}", b)
                        act.activation(Pt[:, h, :].rearrange("p (a c) -> p a c", a=2), a_tile(f"s{h}")[0:TT, :, 0:3 * NJ],
                                       ACT.Exp, scale=SCALE).then_inc(a_free[a_slot(f"s{h}")], 1)
                    return go

                def take_pv(b, pb):
                    act.wait_ge(pv_done[0], b + 1)
                    act.wait_ge(pv_done[1], b + 1)
                    act.activation(au[:, :, :].rearrange("p a c -> p (a c)"), pv_ps[:, 0:2 * NJ], ACT.Copy).then_inc(au_ready, 1)

                def take_sc(q):
                    def go(b, pb):
                        act.wait_ge(d_done, d_count(f"sc{q}", b))
                        act.activation(two(attT[:, q, :]), d_ps[:, :, 0:HALF], ACT.Copy).then_inc(d_free, 1)
                    return go

                def take_o(b, pb):
                    act.wait_ge(d_done, d_count("o", b))
                    act.wait_ge(aob_ready, b)
                    act.wait_ge(r_ready, 2 * b)
                    act.activation(two(ao[:, :]), d_ps[:, :, 0:HALF], ACT.Identity, bias=col("o_b")).then_inc(d_free, 1)

                def take_c(i):
                    def go(b, pb):
                        act.wait_ge(d_done, d_count(f"c{i}", b))
                        act.wait_ge(n_ready, 2 * b + i - 1)
                        act.activation(two(cS[:, :]), d_ps[:, :, 0:HALF], ACT.Copy)
                        act.activation(two(sq[:, :]), d_ps[:, :, 0:HALF], ACT.Square).then_inc(sq_ready, 1)
                        act.wait_ge(sq_ready, 2 * b + i)
                        act.sem_inc(d_free, 1)
                    return go

                def take_m(i):
                    def go(b, pb):
                        act.wait_ge(d_done, d_count(f"m{i}", b))
                        act.activation(two(sq[:, :]), d_ps[:, :, 0:HALF], ACT.Ln, bias=eps[:, :]).then_inc(d_free, 1)
                        act.wait_ge(d_free, d_count(f"m{i}", b))
                        act.activation(sq[:, :], sq[:, :], ACT.Exp, scale=-0.5).then_inc(rstd_ready, 1)
                    return go

                def take_f(i):
                    def go(b, pb):
                        act.wait_ge(d_done, d_count(f"f{i}", b))
                        act.activation(two(rl[:, i, :]), d_ps[:, :, 0:HALF], ACT.Relu, bias=col(f"f1_b{i}")).then_inc(d_free, 1)
                    return go

                def relu_h(b, pb):
                    act.wait_ge(hp_ready, 2 * b + 2)
                    act.activation(hT[:, :], hp[:, :], ACT.Relu, bias=col("conv_b")).then_inc(hT_ready, 1)

                def take_h(b, pb):
                    act.wait_ge(d_done, d_count("ht", b))
                    act.wait_ge(h_stored, 16 * b)
                    act.activation(h_sb[:, :], d_ps[0:TT, 0, 0:ST * D], ACT.Copy).then_inc(h_ready, 1)
                    act.wait_ge(h_ready, b + 1)
                    act.sem_inc(d_free, 1)

                part_a = {"xT": take_xT, "kt0": take_kT(0), "kt2": take_kT(2), "g0": take_qT(0), "g1": take_qT(1),
                          "au": take_pv}
                for h in range(H):
                    part_a[f"s{h}"] = exps(h)
                run(act, part_a, {"sc0": take_sc(0), "sc1": take_sc(1), "o": take_o, "c1": take_c(1), "c2": take_c(2),
                                  "m1": take_m(1), "m2": take_m(2), "f0": take_f(0), "f2": take_f(2), "relu": relu_h,
                                  "ht": take_h})

            @block.vector
            def _(dve):
                dve.memset(wo[:, :, :], 0.0).then_inc(wo_cleared, 1)
                dve.memset(mean[:, :], 1.0 / D).then_inc(const_set, 1)
                dve.memset(eps[:, :], EPS).then_inc(const_set, 1)
                dve.memset(v_pad[:, :, :, :], 0.0).then_inc(const_set, 1)
                dve.memset(kT[KR:KR + 3, :, :], -1.0).then_inc(const_set, 1)
                dve.memset(fu[:, :], 0.0).then_inc(const_set, 1)
                dve.wait_ge(const_set, 3)
                dve.memset(v_pad[:, :, :, HD:HD + 1], 1.0).then_inc(const_set, 1)
                dve.wait_ge(const_loaded, 16 * N_CONST)
                dve.wait_ge(const_made, 2)
                dve.wait_ge(const_set, 6)

                def one_hots(b, pb):
                    dve.tensor_copy(rank_cur[:, :, :], t["rank_tok"][:, :, bass.ds(b * H, H)]).then_inc(cur_ready, 1)
                    dve.wait_ge(cur_ready, b + 1)
                    await_a(dve, a_done, "g1", b - 1)
                    for n in range(NT):
                        for h in range(H):
                            ins = dve.tensor_scalar(G[:, n, h, :], iota_bf[:, :], rank_cur[:, n, h:h + 1], None, ALU.is_equal)
                    ins.then_inc(g_ready, 1)

                def slot_rows(b, pb):
                    dve.wait_ge(rank_loaded, 16 * b + 16)
                    dve.wait_ge(d_done, d_count("sc1", b - 1))
                    for jt in range(2):
                        ins = dve.tensor_scalar(GT[:, jt, :], rank_bc[:, :], slot_id[:, jt:jt + 1], None, ALU.is_equal)
                    ins.then_inc(gt_ready, 1)

                def take_k(b, pb):
                    await_a(dve, a_done, "k", b)
                    dve.wait_ge(kst_ready, b)
                    dve.tensor_tensor(kf[:, :, :].rearrange("p (a n h) d -> p a n (h d)", a=2, n=3), two_of_three(a_tile("k"), D),
                                      kvb[:, 0:D].unsqueeze(1).unsqueeze(1).to_broadcast([TT, 2, 3, D]), ALU.add)\
                       .then_inc(a_free[a_slot("k")], 1)

                def take_v(b, pb):
                    await_a(dve, a_done, "v", b)
                    for a in range(2):
                        ins = dve.tensor_tensor(v_pad[:, 3 * a:3 * a + 3, :, 0:HD],
                                                a_tile("v")[0:TT, a, 0:3 * D].rearrange("p (n h d) -> p n h d", n=3, h=H),
                                                kvb[:, D:2 * D].rearrange("p (h d) -> p h d", h=H).unsqueeze(1)
                                                .to_broadcast([TT, 3, H, HD]), ALU.add)
                    ins.then_inc(a_free[a_slot("v")], 1)

                def take_kT(i):
                    def go(b, pb):
                        await_a(dve, a_done, f"kt{i}", b)
                        dve.tensor_copy(kT[0:KR, 2 * i:2 * i + 2, :].rearrange("p g (n c) -> p g n c", n=NT), turned_k(i))\
                           .then_inc(a_free[a_slot(f"kt{i}")], 1)
                    return go

                def take_max(i):
                    def go(b, pb):
                        await_a(dve, a_done, f"max{i}", b)
                        dve.tensor_reduce(mx[:, i:i + 1], a_tile(f"max{i}")[0:JT, :, 0:HALF], AX.XY, ALU.max)\
                           .then_inc(a_free[a_slot(f"max{i}")], 1)
                    return go

                def max_parts(b, pb):
                    await_a(dve, a_free, f"max{2 * H - 2}", b)
                    await_a(dve, a_free, f"max{2 * H - 1}", b)
                    dve.wait_ge(mx_turned, b)
                    dve.tensor_copy(mxp[:, 0, :], mx[:, :]).then_inc(mx_step, 1)
                    dve.wait_ge(mx_step, 3 * b + 1)
                    dve.tensor_tensor(mx_rest[:, :], mx[:, :], mxp[:, 0, :], ALU.subtract).then_inc(mx_step, 1)
                    dve.wait_ge(mx_step, 3 * b + 2)
                    dve.tensor_copy(mxp[:, 1, :], mx_rest[:, :]).then_inc(mx_step, 1)
                    dve.wait_ge(mx_step, 3 * b + 3)
                    dve.tensor_tensor(mxp[:, 2, :], mx_rest[:, :], mxp[:, 1, :], ALU.subtract).then_inc(mxp_ready, 1)

                def take_max_rows(b, pb):
                    dve.wait_ge(mx_turned, b + 1)
                    dve.wait_ge(mx_rows, 48 * b)
                    dve.tensor_copy(mxT[:, :], mt_ps[0:6 * H, 0:JT]).then_inc(mxT_ready, 1)

                def take_att(b, pb):
                    await_a(dve, a_done, "at", b)
                    at = a_tile("at")[0:JT, 0, :].rearrange("p (s g d) -> p s g d", s=4, g=4)
                    dve.reciprocal(rden[:, :, :], at[:, :, :, HD]).then_inc(att_step, 1)
                    dve.wait_ge(att_step, 4 * b + 1)
                    dve.tensor_tensor(att[:, :].rearrange("p (s g d) -> p s g d", s=4, g=4), at,
                                      rden[:, :, :].unsqueeze(3).to_broadcast([JT, 4, 4, 32]), ALU.mult)\
                       .then_inc(a_free[a_slot("at")], 1)
                    await_a(dve, a_free, "at", b)
                    dve.tensor_copy(attp[:, 0, :], att[:, :]).then_inc(att_step, 1)
                    dve.wait_ge(att_step, 4 * b + 2)
                    dve.tensor_tensor(att_rest[:, :], att[:, :], attp[:, 0, :], ALU.subtract).then_inc(att_step, 1)
                    dve.wait_ge(att_step, 4 * b + 3)
                    dve.tensor_copy(attp[:, 1, :], att_rest[:, :]).then_inc(att_step, 1)
                    dve.wait_ge(att_step, 4 * b + 4)
                    dve.tensor_tensor(attp[:, 2, :], att_rest[:, :], attp[:, 1, :], ALU.subtract).then_inc(attp_ready, 1)

                def residual1(b, pb):
                    dve.wait_ge(d_free, d_count("o", b))
                    dve.tensor_tensor(r[:, :], ao[:, :], xT[pb][:, :], ALU.add).then_inc(r_ready, 1)

                def norm1(b, pb):
                    dve.wait_ge(rstd_ready, 2 * b + 1)
                    dve.tensor_tensor(cS[:, :], cS[:, :], sq[:, :], ALU.mult).then_inc(ln_step, 1)
                    dve.wait_ge(ln_step, 2 * b + 1)
                    dve.tensor_scalar(h1[:, :], cS[:, :], col("ln1_g"), col("ln1_b"), ALU.mult, ALU.add).then_inc(h1_ready, 1)
                    dve.wait_ge(h1_ready, b + 1)
                    dve.sem_inc(n_ready, 1)

                def take_f(i):
                    def go(b, pb):
                        dve.wait_ge(d_done, d_count(f"f{i}", b))
                        dve.tensor_scalar(two(rl[:, i, :]), d_ps[:, :, 0:HALF], col(f"f1_b{i}"), 0.0, ALU.add, ALU.max)\
                           .then_inc(d_free, 1)
                    return go

                def residual2(b, pb):
                    dve.wait_ge(d_done, d_count("ff", b))
                    dve.scalar_tensor_tensor(two(r[:, :]), d_ps[:, :, 0:HALF], col("f2_b"), two(h1[:, :]), ALU.add, ALU.add)\
                       .then_inc(d_free, 1)
                    dve.wait_ge(d_free, d_count("ff", b))
                    dve.sem_inc(r_ready, 1)

                def norm2(b, pb):
                    dve.wait_ge(rstd_ready, 2 * b + 2)
                    dve.tensor_tensor(cS[:, :], cS[:, :], sq[:, :], ALU.mult).then_inc(ln_step, 1)
                    dve.wait_ge(ln_step, 2 * b + 2)
                    dve.wait_ge(aob_ready, b + 1)
                    dve.scalar_tensor_tensor(fu[:, 1:L + 1], cS[:, :], col("ln2_g"), aob[:, :], ALU.mult, ALU.add)\
                       .then_inc(fu_ready, 1)
                    dve.wait_ge(fu_ready, b + 1)
                    dve.sem_inc(n_ready, 1)

                def pool_pairs(b, pb):
                    dve.wait_ge(d_done, d_count("cv", b))
                    dve.wait_ge(hT_ready, b)
                    n = (HALF + 1) // 2
                    dve.tensor_reduce(hp[:, 0:n], d_ps[:, 0, 0:2 * n].rearrange("p (s w) -> p s w", w=2), AX.X, ALU.max)\
                       .then_inc(hp_ready, 1)
                    dve.tensor_reduce(hp[:, n:S], d_ps[:, 1, 0:2 * (S - n)].rearrange("p (s w) -> p s w", w=2), AX.X, ALU.max)\
                       .then_inc(hp_ready, 1)
                    dve.wait_ge(hp_ready, 2 * b + 2)
                    dve.sem_inc(d_free, 1)

                part_a = {"g": one_hots, "gt": slot_rows, "k": take_k, "v": take_v, "kt1": take_kT(1), "kt3": take_kT(3),
                          "mp": max_parts, "mx": take_max_rows, "at": take_att}
                for i in range(2 * H):
                    part_a[f"max{i}"] = take_max(i)
                run(dve, part_a, {"o": residual1, "m1": norm1, "f1": take_f(1), "f3": take_f(3), "ff": residual2,
                                  "m2": norm2, "cv": pool_pairs})


N_CONST = 11 + H


def order():
    a = ["load", "xT", "g", "k", "v", "gt"] + [f"kt{i}" for i in range(4)] + ["g0", "g1"] \
        + [f"max{i}" for i in range(2 * H)] + ["mp", "mx"] + [f"s{h}" for h in range(4)] + ["pv0"] \
        + [f"s{h}" for h in range(4, H)] + ["pv1", "au", "at"]
    d = ["sc0", "sc1", "o", "c1", "m1", "f0", "f1", "f2", "f3", "ff", "c2", "m2", "cv", "relu", "ht"]
    before = {"sc0": "load", "sc1": "load", "o": "k", "c1": "kt1", "m1": "kt3", "f0": "g0", "f1": "g1", "f2": "max2",
              "f3": "max4", "ff": "max6", "c2": "max10", "m2": "max14", "cv": "s0", "relu": "s2", "ht": "s4"}
    out = []
    for step in a:
        out += [("D", s) for s in d if before[s] == step]
        out.append(("A", step))
    return out


def tanh_attention(nc, t, io):
    with ExitStack() as ctx:
        def sb(name, shape, dt=F32):
            return ctx.enter_context(nc.sbuf_tensor(name, shape, dt))

        def sem(name):
            return ctx.enter_context(nc.semaphore(name))

        aw = sb("attention_w", [D, D])
        wr = sb("router_w", [D, E])
        brc = sb("router_b_rows", [TT, E])
        minus_half = sb("minus_half", [TT, ST])
        h_in = [sb(f"h_in{p}", [TT, ST, D]) for p in range(2)]
        z = [sb(f"z{p}", [TT, ST, D + 1]) for p in range(2)]
        stats = [sb(f"ln_stats{k}", [TT, ST, 6]) for k in range(2)]
        mv = [sb(f"ln_mv{k}", [TT, ST, 2]) for k in range(2)]
        ve = [sb(f"ln_ve{k}", [TT, ST]) for k in range(2)]
        rs = [sb(f"ln_rs{k}", [TT, ST]) for k in range(2)]
        zT = sb("zT", [D, S])
        pT = sb("pT", [D, S])
        th = sb("tanh_s", [TT, ST, S])
        ex = [sb(f"exp_s{p}", [TT, ST, S]) for p in range(2)]
        rden = sb("rden4", [TT, ST])
        uT = sb("uT4", [D, S])
        zT_ps = ctx.enter_context(nc.psum_tensor("zT_ps", [128, 512], F32))
        pT_ps = ctx.enter_context(nc.psum_tensor("pT_ps", [128, 512], F32))
        s_ps = ctx.enter_context(nc.psum_tensor("s_ps", [128, ST, 512], F32))
        o_ps = ctx.enter_context(nc.psum_tensor("o_ps4", [128, 512], F32))
        uT_ps = ctx.enter_context(nc.psum_tensor("uT_ps", [128, 512], F32))
        l_ps = ctx.enter_context(nc.psum_tensor("l_ps", [128, 512], F32))

        names = ["w4", "set4", "zT_done", "zT_ready", "pT_done", "pT_ready", "s_done", "th_ready", "ex_ready", "o_done",
                 "rden_ready", "hh_ready", "uT_done", "uT_ready", "l_done", "l_ready"]
        w4, set4, zT_done, zT_ready, pT_done, pT_ready, s_done, th_ready, ex_ready, o_done, rden_ready, hh_ready, uT_done, \
            uT_ready, l_done, l_ready = [sem(n) for n in names]
        gate4 = sem("gate4")
        h_loaded = [sem(f"h_loaded4{p}") for p in range(2)]
        st_ready = [sem(f"st_ready{k}") for k in range(2)]
        mv_ready = [sem(f"mv_ready{k}") for k in range(2)]
        ve_ready = [sem(f"ve_ready{k}") for k in range(2)]
        rs_ready = [sem(f"rs_ready{k}") for k in range(2)]
        n_ready = [sem(f"n_ready4{k}") for k in range(2)]
        u_all, hh_all, logits = t["u_all"], t["hh_all"], t["logits"]

        def run(eng, part_a, part_b):
            part_a(0, 0, 0)
            with eng.Fori(0, NB // 2 - 1) as i:
                part_a(2 * i + 1, 1, i)
                part_b(2 * i, 0, i)
                part_a(2 * i + 2, 0, i + 1)
                part_b(2 * i + 1, 1, i)
            part_a(NB - 1, 1, NB // 2 - 1)
            part_b(NB - 2, 0, NB // 2 - 1)
            part_b(NB - 1, 1, NB // 2 - 1)

        with nc.Block() as block:
            @block.sync
            def _(sp):
                sp.dma_start(aw[:, :], io["L0_attn_attention_weights"]).then_inc(w4, 16)
                sp.dma_start(wr[:, :], io["L0_ffn_Wr"]).then_inc(w4, 16)
                sp.dma_start(brc[:, :], io["L0_ffn_br"].rearrange("(a n) -> a n", a=1).to_broadcast([TT, E])).then_inc(w4, 16)

                def load(b, p, i):
                    sp.wait_ge(hh_ready, ST * b - ST if not isinstance(b, int) else max(ST * b - ST, 0))
                    sp.dma_start(h_in[p][:, :, :].rearrange("p n d -> p (n d)"),
                                 io["h_rows"][bass.ds(b, 1), :, :].rearrange("b p n -> (b p) n")).then_inc(h_loaded[p], 16)

                run(sp, load, lambda b, p, i: None)

            @block.gpsimd
            def _(pool):
                pool.memset(minus_half[:, :], -0.5).then_inc(set4, 1)
                pool.wait_ge(set4, 1)

                def power(k):
                    def go(b, p, i):
                        pool.wait_ge(ve_ready[k], b + 1)
                        pool.wait_ge(n_ready[k], b)
                        pool.tensor_tensor(rs[k][:, :], ve[k][:, :], minus_half[:, :], ALU.pow).then_inc(rs_ready[k], 1)
                    return go

                run(pool, power(0), power(1))

            @block.tensor
            def _(pe):
                pe.wait_ge(w4, 48)

                def part_a(b, p, i):
                    pe.wait_ge(n_ready[0], b + 1)
                    for n in range(ST):
                        mm = pe.transpose(zT_ps[:, n * TT:(n + 1) * TT], z[p][:, n, 0:D], t["ident"][0:TT, 0:TT])
                    mm.then_inc(zT_done, 1)
                    pe.wait_ge(zT_ready, b + 1)
                    pe.matmul(pT_ps[:, 0:S], aw[:, :], zT[:, :], start=True, stop=True).then_inc(pT_done, 1)
                    pe.wait_ge(pT_ready, b + 1)
                    pe.wait_ge(th_ready, b)
                    for n in range(ST):
                        mm = pe.matmul(s_ps[0:TT, n, 0:S], zT[:, n * TT:(n + 1) * TT], pT[:, :], start=True, stop=True)
                    mm.then_inc(s_done, 1)

                def part_b(b, p, i):
                    pe.wait_ge(ex_ready, b + 1)
                    pe.wait_ge(hh_ready, ST * b)
                    for m in range(ST):
                        for n in range(ST):
                            mm = pe.matmul(o_ps[0:TT, m * (D + 1):(m + 1) * (D + 1)], ex[p][:, n, m * TT:(m + 1) * TT],
                                           z[p][:, n, :], start=(n == 0), stop=(n == ST - 1))
                    mm.then_inc(o_done, 1)
                    pe.wait_ge(n_ready[1], b + 1)
                    for n in range(ST):
                        mm = pe.transpose(uT_ps[:, n * TT:(n + 1) * TT], t["u_cur"][p][:, n, :], t["ident"][0:TT, 0:TT])
                    mm.then_inc(uT_done, 1)
                    pe.wait_ge(uT_ready, b + 1)
                    pe.wait_ge(l_ready, b)
                    for n in range(ST):
                        mm = pe.matmul(l_ps[0:TT, n * E:(n + 1) * E], uT[:, n * TT:(n + 1) * TT], wr[:, :], start=True, stop=True)
                    mm.then_inc(l_done, 1)

                run(pe, part_a, part_b)

            @block.scalar
            def _(act):
                def part_a(b, p, i):
                    act.wait_ge(zT_done, b + 1)
                    act.wait_ge(s_done, b)
                    act.activation(zT[:, :], zT_ps[:, 0:S], ACT.Copy).then_inc(zT_ready, 1)
                    act.wait_ge(s_done, b + 1)
                    act.activation(th[:, :, :], s_ps[0:TT, :, 0:S], ACT.Tanh).then_inc(th_ready, 1)
                    act.wait_ge(th_ready, b + 1)
                    act.activation(ex[p][:, :, :], th[:, :, :], ACT.Exp).then_inc(ex_ready, 1)

                def part_b(b, p, i):
                    act.wait_ge(uT_done, b + 1)
                    act.activation(uT[:, :], uT_ps[:, 0:S], ACT.Copy).then_inc(uT_ready, 1)

                run(act, part_a, part_b)

            @block.vector
            def _(dve):
                for p in range(2):
                    dve.memset(z[p][:, :, D:D + 1], 1.0).then_inc(t["z_set"], 1)
                dve.wait_ge(t["z_set"], 2)
                dve.wait_ge(w4, 48)

                def norm(k, src, dst, b):
                    for n in range(ST):
                        dve.bn_stats(stats[k][:, n, :], src(n)).then_inc(st_ready[k], 1)
                    dve.wait_ge(st_ready[k], ST * b + ST)
                    dve.sem_inc(gate4, 1)
                    for n in range(ST):
                        dve.bn_aggr(mv[k][:, n, :], stats[k][:, n, :]).then_inc(mv_ready[k], 1)
                    dve.wait_ge(mv_ready[k], ST * b + ST)
                    dve.tensor_scalar(ve[k][:, :], mv[k][:, :, 1], EPS, None, ALU.add).then_inc(ve_ready[k], 1)
                    dve.wait_ge(rs_ready[k], b + 1)
                    for n in range(ST):
                        ins = dve.tensor_scalar(dst(n), src(n), mv[k][:, n, 0:1], rs[k][:, n:n + 1], ALU.subtract, ALU.mult)
                    ins.then_inc(n_ready[k], 1)

                def part_a(b, p, i):
                    dve.wait_ge(h_loaded[p], 16 * i + 16)
                    norm(0, lambda n: h_in[p][:, n, :], lambda n: z[p][:, n, 0:D], b)
                    dve.wait_ge(pT_done, b + 1)
                    dve.tensor_copy(pT[:, :], pT_ps[:, 0:S]).then_inc(pT_ready, 1)

                def part_b(b, p, i):
                    dve.wait_ge(o_done, b + 1)
                    o = o_ps[0:TT, 0:ST * (D + 1)].rearrange("p (n d) -> p n d", n=ST)
                    dve.reciprocal(rden[:, :], o[:, :, D]).then_inc(rden_ready, 1)
                    dve.wait_ge(rden_ready, b + 1)
                    cur = t["hh_cur"][p]
                    for n in range(ST):
                        dve.scalar_tensor_tensor(cur[:, n, :], o[:, n, 0:D], rden[:, n:n + 1], h_in[p][:, n, :], ALU.mult, ALU.add)\
                           .then_inc(hh_ready, 1)
                    dve.wait_ge(hh_ready, ST * b + ST)
                    u = t["u_cur"][p]
                    norm(1, lambda n: cur[:, n, :], lambda n: u[:, n, :], b)
                    dve.tensor_copy(hh_all[:, bass.ds(b * ST * D, ST * D)], cur[:, :, :].rearrange("p n d -> p (n d)"))
                    dve.wait_ge(n_ready[1], b + 1)
                    dve.tensor_copy(u_all[:, bass.ds(b * ST * D, ST * D)], u[:, :, :].rearrange("p n d -> p (n d)"))
                    dve.wait_ge(l_done, b + 1)
                    dve.tensor_tensor(logits[:, bass.ds(b * ST, ST), :], l_ps[0:TT, 0:ST * E].rearrange("p (n e) -> p n e", n=ST),
                                      brc[:, :].unsqueeze(1).to_broadcast([TT, ST, E]), ALU.add).then_inc(l_ready, 1)

                run(dve, part_a, part_b)


def route(nc, t, io):
    with ExitStack() as ctx:
        def sb(name, shape, dt=F32):
            return ctx.enter_context(nc.sbuf_tensor(name, shape, dt))

        def sem(name):
            return ctx.enter_context(nc.semaphore(name))

        top = sb("top_logit", [TT, NTILE])
        hot = sb("hot", [TT, NTILE, E])
        pick = sb("pick", [TT, NTILE, E])
        best = sb("best", [TT, NTILE])
        e_id = sb("e_id", [TT, E])
        upper = sb("upper", [TT, TT])
        ones = sb("ones5", [TT, TT])
        ones_t = sb("ones_t", [TT, NTILE])
        total = sb("total", [TT, NTILE, E])
        cum = sb("cum", [TT, E, NTILE])
        blk_row = sb("blk_row", [TT, NBLK])
        full = sb("full", [TT, E, NBLK])
        nblk = sb("nblk", [TT, E])
        bend = sb("bend", [TT, E])
        bstart = sb("bstart", [TT, E])
        past = sb("past", [TT, NBLK, E])
        owner = sb("owner", [TT, NBLK])
        slot = sb("slot_f", [TT, NTILE])
        gate = t["gate"]
        p_ps = ctx.enter_context(nc.psum_tensor("p_ps", [128, 512], F32))
        t_ps = ctx.enter_context(nc.psum_tensor("t_ps", [128, 512], F32))
        const5 = sem("const5")
        hot_ready = sem("hot_ready")
        counted = sem("counted")
        diff_ready = sem("diff_ready")
        gate_exp = sem("gate_exp")
        step5 = sem("step5")
        slots_ready = sem("slots_ready")
        scattered = sem("scattered")

        with nc.Block() as block:
            @block.sync
            def _(sp):
                sp.dma_start(e_id[:, :], io["c_e_id"].to_broadcast([TT, E])).then_inc(const5, 16)
                sp.dma_start(upper[:, :], io["c_upper"]).then_inc(const5, 16)
                sp.dma_start(blk_row[:, :], io["c_blk"].to_broadcast([TT, NBLK])).then_inc(const5, 16)

            @block.scalar
            def _(act):
                act.wait_ge(diff_ready, 1)
                act.activation(gate[:, :], best[:, :], ACT.Exp).then_inc(gate_exp, 1)

            @block.tensor
            def _(pe):
                pe.wait_ge(const5, 48)
                pe.wait_ge(hot_ready, 1)
                m = hot[:, :, :].rearrange("p t e -> p (t e)")
                pe.matmul(p_ps[0:TT, 0:NTILE * E], upper[:, :], m, start=True, stop=True)
                pe.matmul(t_ps[0:TT, 0:NTILE * E], ones[:, :], m, start=True, stop=True).then_inc(counted, 1)

            @block.vector
            def _(dve):
                n_step = [0]

                def chain(ins):
                    n_step[0] += 1
                    ins.then_inc(step5, 1)
                    dve.wait_ge(step5, n_step[0])

                def tiles(ap):
                    return ap.unsqueeze(2).to_broadcast([TT, NTILE, E])

                def experts(ap, n=NTILE):
                    return ap.unsqueeze(1).to_broadcast([TT, n, E])

                chain(dve.memset(ones[:, :], 1.0))
                chain(dve.memset(ones_t[:, :], 1.0))
                dve.wait_ge(const5, 48)
                chain(dve.tensor_reduce(top[:, :], t["logits"][:, :, :], AX.X, ALU.max))
                dve.tensor_tensor(best[:, :], top[:, :], top[:, :], ALU.subtract).then_inc(diff_ready, 1)
                dve.wait_ge(gate_exp, 1)
                chain(dve.reciprocal(best[:, :], gate[:, :]))
                chain(dve.tensor_tensor(gate[:, :], gate[:, :], best[:, :], ALU.mult))
                chain(dve.tensor_tensor(pick[:, :, :], t["logits"][:, :, :], tiles(top[:, :]), ALU.is_equal))
                chain(dve.tensor_tensor(pick[:, :, :], pick[:, :, :], experts(e_id[:, :]), ALU.mult))
                chain(dve.tensor_reduce(best[:, :], pick[:, :, :], AX.X, ALU.max))
                dve.tensor_tensor(hot[:, :, :], experts(e_id[:, :]), tiles(best[:, :]), ALU.is_equal).then_inc(hot_ready, 1)
                dve.wait_ge(counted, 1)
                chain(dve.tensor_copy(total[:, :, :].rearrange("p t e -> p (t e)"), t_ps[0:TT, 0:NTILE * E]))
                for e in range(E):
                    chain(dve.tensor_tensor_scan(cum[:, e, :], ones_t[:, :], total[:, :, e], 0.0, ALU.mult, ALU.add))
                chain(dve.tensor_scalar(full[:, 0, :], blk_row[:, :], float(BLK), None, ALU.mult))
                chain(dve.tensor_copy(owner[:, :], full[:, 0, :]))
                chain(dve.tensor_tensor(full[:, :, :], cum[:, :, NTILE - 1:NTILE].to_broadcast([TT, E, NBLK]),
                                        owner[:, :].unsqueeze(1).to_broadcast([TT, E, NBLK]), ALU.is_gt))
                chain(dve.tensor_reduce(nblk[:, :], full[:, :, :], AX.X, ALU.add))
                chain(dve.tensor_tensor_scan(bend[:, :], ones_t[:, 0:E], nblk[:, :], 0.0, ALU.mult, ALU.add))
                chain(dve.tensor_tensor(bstart[:, :], bend[:, :], nblk[:, :], ALU.subtract))
                chain(dve.tensor_scalar(bstart[:, :], bstart[:, :], float(BLK), None, ALU.mult))
                chain(dve.tensor_tensor(past[:, :, :], blk_row[:, :].unsqueeze(2).to_broadcast([TT, NBLK, E]),
                                        experts(bend[:, :], NBLK), ALU.is_ge))
                chain(dve.tensor_reduce(owner[:, :], past[:, :, :], AX.X, ALU.add))
                chain(dve.tensor_scalar(t["block_expert"][:, :], owner[:, :], float(E - 1), None, ALU.min))
                chain(dve.tensor_tensor(pick[:, :, :], cum[:, :, :].rearrange("p e t -> p t e"), total[:, :, :], ALU.subtract))
                chain(dve.tensor_tensor(pick[:, :, :], pick[:, :, :], experts(bstart[:, :]), ALU.add))
                chain(dve.tensor_tensor(pick[:, :, :], pick[:, :, :], p_ps[0:TT, 0:NTILE * E].rearrange("p (t e) -> p t e", e=E),
                                        ALU.add))
                chain(dve.tensor_tensor(pick[:, :, :], pick[:, :, :], hot[:, :, :], ALU.mult))
                chain(dve.tensor_reduce(slot[:, :], pick[:, :, :], AX.X, ALU.add))
                dve.tensor_copy(t["slot"][:, :], slot[:, :]).then_inc(slots_ready, 1)

            @block.gpsimd
            def _(pool):
                pool.wait_ge(slots_ready, 1)
                for n in range(NTILE):
                    pool.indirect_dma_start(out=io["u_rows"], out_offset=bass.IndirectOffsetOnAxis(ap=t["slot"][:, n:n + 1], axis=0),
                                            in_=t["u_all"][:, n * D:(n + 1) * D], in_offset=None).then_inc(scattered, 16)
                pool.wait_ge(scattered, 16 * NTILE)


def experts(nc, t, io):
    with ExitStack() as ctx:
        def sb(name, shape, dt=F32):
            return ctx.enter_context(nc.sbuf_tensor(name, shape, dt))

        def sem(name):
            return ctx.enter_context(nc.semaphore(name))

        def two(f):
            return [f(p) for p in range(2)]

        NC = EH // 128
        w1 = sb("w1", [D, E, EH])
        w2 = sb("w2", [128, E * NC, D])
        b1 = sb("b1_rows", [128, E * EH])
        b2 = sb("b2_rows", [128, E * D])
        ub = two(lambda p: sb(f"u_block{p}", [BLK, D]))
        uT = two(lambda p: sb(f"uT_block{p}", [D, BLK]))
        hb = two(lambda p: sb(f"h_block{p}", [BLK, EH]))
        hT = two(lambda p: sb(f"hT_block{p}", [128, NC, BLK]))
        ob = two(lambda p: sb(f"o_block{p}", [BLK, D]))
        gt = two(lambda p: sb(f"gathered{p}", [TT, ST, D]))
        fin = two(lambda p: sb(f"final{p}", [TT, ST, D]))
        uT_ps = two(lambda p: ctx.enter_context(nc.psum_tensor(f"uTb_ps{p}", [128, 512], F32)))
        h_ps = two(lambda p: ctx.enter_context(nc.psum_tensor(f"h_ps{p}", [128, 512], F32)))
        hT_ps = two(lambda p: ctx.enter_context(nc.psum_tensor(f"hT_ps{p}", [128, 512], F32)))
        o_ps = two(lambda p: ctx.enter_context(nc.psum_tensor(f"ob_ps{p}", [128, 512], F32)))
        w_loaded = sem("w_loaded6")
        u_loaded, u_turned, uT_ready, h_done, h_ready, h_turned, hT_ready, o_done, o_ready, o_stored, g_loaded, f_ready, f_stored = [
            two(lambda p: sem(f"{n}6{p}")) for n in ("u_loaded", "u_turned", "uT_ready", "h_done", "h_ready", "h_turned", "hT_ready",
                                                    "o_done", "o_ready", "o_stored", "g_loaded", "f_ready", "f_stored")]
        assert NBLK % 2 == 0
        HB = NBLK // 2

        with nc.Block() as block:
            @block.sync
            def _(sp):
                def load(j, p, i):
                    sp.wait_ge(u_turned[p], i)
                    sp.dma_start(ub[p][:, :], io["u_rows"][bass.ds(j * BLK, BLK), :]).then_inc(u_loaded[p], 16)

                def store(p, i, j):
                    sp.wait_ge(o_ready[p], i + 1)
                    sp.dma_start(io["o_rows"][bass.ds(j * BLK, BLK), :], ob[p][:, :]).then_inc(o_stored[p], 16)

                for p in range(2):
                    load(p, p, 0)
                with sp.Fori(0, HB - 1) as i:
                    for p in range(2):
                        load(2 * i + 2 + p, p, i + 1)
                        store(p, i, 2 * i + p)
                for p in range(2):
                    store(p, HB - 1, NBLK - 2 + p)
                for p in range(2):
                    sp.wait_ge(o_stored[p], 16 * HB)

            @block.gpsimd
            def _(pool):
                for dst, src in ((w1[:, :, :], io["L0_ffn_W1"].rearrange("e d h -> d e h")),
                                 (w2[:, :, :], io["L0_ffn_W2"].rearrange("e (c p) d -> p (e c) d", p=128)),
                                 (b1[:, :], io["L0_ffn_b1"].rearrange("(a e) h -> a (e h)", a=1).to_broadcast([128, E * EH])),
                                 (b2[:, :], io["L0_ffn_b2"].rearrange("(a e) d -> a (e d)", a=1).to_broadcast([128, E * D]))):
                    pool.dma_start(dst, src).then_inc(w_loaded, 16)

            @block.tensor
            def _(pe):
                pe.wait_ge(w_loaded, 64)

                def turn_u(p, i):
                    pe.wait_ge(u_loaded[p], 16 * i + 16)
                    pe.wait_ge(uT_ready[p], i)
                    pe.transpose(uT_ps[p][:, 0:BLK], ub[p][:, :], t["ident"][:, :]).then_inc(u_turned[p], 1)

                def up(p, i, e):
                    pe.wait_ge(uT_ready[p], i + 1)
                    pe.wait_ge(h_ready[p], i)
                    pe.matmul(h_ps[p][:, :], uT[p][:, :], w1[:, bass.ds(e, 1), :].rearrange("p a h -> p (a h)"), start=True, stop=True)\
                      .then_inc(h_done[p], 1)

                def turn_h(p, i):
                    pe.wait_ge(h_ready[p], i + 1)
                    pe.wait_ge(hT_ready[p], i)
                    for c in range(NC):
                        mm = pe.transpose(hT_ps[p][:, c * BLK:(c + 1) * BLK], hb[p][:, c * 128:(c + 1) * 128], t["ident"][:, :])
                    mm.then_inc(h_turned[p], 1)

                def down(p, i, e):
                    pe.wait_ge(hT_ready[p], i + 1)
                    pe.wait_ge(o_ready[p], i)
                    for c in range(NC):
                        mm = pe.matmul(o_ps[p][:, 0:D], hT[p][:, c, :], w2[:, bass.ds(e * NC + c, 1), :].rearrange("p a d -> p (a d)"),
                                       start=(c == 0), stop=(c == NC - 1))
                    mm.then_inc(o_done[p], 1)

                def expert(j):
                    return pe.value_load(t["block_expert"][0:1, bass.ds(j, 1)], min_val=0, max_val=E - 1)

                turn_u(0, 0)
                turn_u(1, 0)
                up(0, 0, expert(0))
                turn_h(0, 0)
                with pe.Fori(0, HB - 1) as i:
                    turn_u(0, i + 1)
                    up(1, i, expert(2 * i + 1))
                    down(0, i, expert(2 * i))
                    turn_h(1, i)
                    turn_u(1, i + 1)
                    up(0, i + 1, expert(2 * i + 2))
                    down(1, i, expert(2 * i + 1))
                    turn_h(0, i + 1)
                up(1, HB - 1, expert(NBLK - 1))
                down(0, HB - 1, expert(NBLK - 2))
                turn_h(1, HB - 1)
                down(1, HB - 1, expert(NBLK - 1))

            @block.scalar
            def _(act):
                def take_u(p, i):
                    act.wait_ge(u_turned[p], i + 1)
                    act.wait_ge(h_done[p], i)
                    act.activation(uT[p][:, :], uT_ps[p][:, 0:BLK], ACT.Copy).then_inc(uT_ready[p], 1)

                def take_h(p, i):
                    act.wait_ge(h_turned[p], i + 1)
                    act.wait_ge(o_done[p], i)
                    act.activation(hT[p][:, :, :].rearrange("p c t -> p (c t)"), hT_ps[p][:, :], ACT.Relu).then_inc(hT_ready[p], 1)

                take_u(0, 0)
                take_u(1, 0)
                take_h(0, 0)
                with act.Fori(0, HB - 1) as i:
                    take_u(0, i + 1)
                    take_h(1, i)
                    take_u(1, i + 1)
                    take_h(0, i + 1)
                take_h(1, HB - 1)

            @block.vector
            def _(dve):
                dve.wait_ge(w_loaded, 64)

                def add1(p, i, e):
                    dve.wait_ge(h_done[p], i + 1)
                    dve.wait_ge(h_turned[p], i)
                    dve.tensor_tensor(hb[p][:, :], h_ps[p][:, :], b1[:, bass.ds(e * EH, EH)], ALU.add).then_inc(h_ready[p], 1)

                def add2(p, i, e):
                    dve.wait_ge(o_done[p], i + 1)
                    dve.wait_ge(o_stored[p], 16 * i)
                    dve.tensor_tensor(ob[p][:, :], o_ps[p][:, 0:D], b2[:, bass.ds(e * D, D)], ALU.add).then_inc(o_ready[p], 1)

                def expert(j):
                    return dve.value_load(t["block_expert"][0:1, bass.ds(j, 1)], min_val=0, max_val=E - 1)

                add1(0, 0, expert(0))
                with dve.Fori(0, HB - 1) as i:
                    add1(1, i, expert(2 * i + 1))
                    add2(0, i, expert(2 * i))
                    add1(0, i + 1, expert(2 * i + 2))
                    add2(1, i, expert(2 * i + 1))
                add1(1, HB - 1, expert(NBLK - 1))
                add2(0, HB - 1, expert(NBLK - 2))
                add2(1, HB - 1, expert(NBLK - 1))

        with nc.Block() as block:
            @block.gpsimd
            def _(pool):
                for b in range(NB):
                    p, i = b % 2, b // 2
                    if i:
                        pool.wait_ge(f_ready[p], i)
                    for n in range(ST):
                        k = b * ST + n
                        pool.indirect_dma_start(out=gt[p][:, n, :], out_offset=None, in_=io["o_rows"],
                                                in_offset=bass.IndirectOffsetOnAxis(ap=t["slot"][:, k:k + 1], axis=0))\
                            .then_inc(g_loaded[p], 16)

            @block.vector
            def _(dve):
                for b in range(NB):
                    p, i = b % 2, b // 2
                    dve.wait_ge(g_loaded[p], 16 * ST * (i + 1))
                    if i:
                        dve.wait_ge(f_stored[p], 16 * i)
                    for n in range(ST):
                        k = b * ST + n
                        ins = dve.scalar_tensor_tensor(fin[p][:, n, :], gt[p][:, n, :], t["gate"][:, k:k + 1],
                                                       t["hh_all"][:, k * D:(k + 1) * D], ALU.mult, ALU.add)
                    ins.then_inc(f_ready[p], 1)

            @block.sync
            def _(sp):
                out_v = io["out"].rearrange("b (n p) d -> b p n d", p=TT)
                for b in range(NB):
                    p, i = b % 2, b // 2
                    sp.wait_ge(f_ready[p], i + 1)
                    sp.dma_start(out_v[b, :, :, :], fin[p][:, :, :]).then_inc(f_stored[p], 16)
                for p in range(2):
                    sp.wait_ge(f_stored[p], 16 * (NB // 2))


def audio_tower(nc, io):
    with ExitStack() as ctx:
        def sb(name, shape, dt=F32):
            return ctx.enter_context(nc.sbuf_tensor(name, shape, dt))

        t = {"ident": sb("ident", [128, 128])}
        with nc.sbuf_tensor("rank_tok", [TT, NT, NG], F32) as rank_tok:
            t["rank_tok"] = rank_tok
            clear_blocks(nc, io)
            norms_and_ranks(nc, t, io)
            sequences(nc, t, io)
        t["z_set"] = ctx.enter_context(nc.semaphore("z_set"))
        t["hh_all"] = sb("hh_all", [TT, NTILE * D])
        t["u_all"] = sb("u_all", [TT, NTILE * D])
        t["logits"] = sb("logits", [TT, NTILE, E])
        t["gate"] = sb("gate", [TT, NTILE])
        t["slot"] = sb("slot", [TT, NTILE], I32)
        t["block_expert"] = sb("block_expert", [TT, NBLK], I32)
        t["hh_cur"] = [sb(f"hh_cur{p}", [TT, ST, D]) for p in range(2)]
        t["u_cur"] = [sb(f"u_cur{p}", [TT, ST, D]) for p in range(2)]
        tanh_attention(nc, t, io)
        route(nc, t, io)
        experts(nc, t, io)


def clear_blocks(nc, io):
    with nc.sbuf_tensor("zeros", [128, NBLK * BLK // 128 * D], F32) as zeros, nc.semaphore("zeros_made") as made, \
            nc.semaphore("rows_cleared") as cleared, nc.Block() as block:
        @block.vector
        def _(dve):
            dve.memset(zeros[:, :], 0.0).then_inc(made, 1)

        @block.sync
        def _(sp):
            sp.wait_ge(made, 1)
            sp.dma_start(io["u_rows"].rearrange("(p r) d -> p (r d)", p=128), zeros[:, :]).then_inc(cleared, 16)
            sp.wait_ge(cleared, 16)


def constants():
    slot_id = np.arange(NJ, dtype=np.float32)
    slot_id[K_TOP] = -1.0
    slot_id[K_TOP + 1] = -2.0
    return {
        "c_ident": np.eye(128, dtype=np.float32),
        "c_center": (np.eye(D) - 1.0 / D).astype(np.float32),
        "c_iota": np.arange(NJ, dtype=np.float32)[None],
        "c_slot_id": np.ascontiguousarray(slot_id.reshape(2, JT).T),
        "c_e_id": (E - np.arange(E, dtype=np.float32))[None],
        "c_upper": np.triu(np.ones((TT, TT), np.float32), 1),
        "c_blk": np.arange(NBLK, dtype=np.float32)[None],
    }


def kernel(**inputs):
    import concourse.bacc as _bacc
    from concourse.bass_utils import run_bass_kernel_spmd as _run

    nc = _bacc.Bacc("TRN2", target_bir_lowering=False, num_devices=1)
    laid = {k: np.ascontiguousarray(v) for k, v in inputs.items()}
    laid["conv_w"] = np.ascontiguousarray(laid.pop("L0_tok_conv_w").transpose(1, 2, 0))
    f1_b = laid.pop("L0_tok_f1_b").reshape(FF // 128, 128)
    laid["cols"] = np.ascontiguousarray(np.stack([laid.pop("L0_tok_" + n) for n in COLS[:7]] + list(f1_b), 1))
    laid.update(constants())
    arrays, io = {}, {}
    for name, a in laid.items():
        arrays[f"in_{name}"] = a
        io[name] = nc.dram_tensor(f"in_{name}", a.shape, mybir.dt.from_np(a.dtype), kind="ExternalInput").ap()
    io["out"] = nc.dram_tensor("out_0", (NB, S, D), F32, kind="ExternalOutput").ap()
    for name, shape, dt in (("q_rows", (NB, TT, NT * D), F32), ("rank_rows", (NG, L), BF16), ("h_rows", (NB, TT, ST * D), F32),
                            ("u_rows", (NBLK * BLK, D), F32), ("o_rows", (NBLK * BLK, D), F32)):
        io[name] = nc.dram_tensor(name, shape, dt, kind="Internal").ap()
    audio_tower(nc, io)
    r = _run(nc, [arrays], core_ids=[0])
    return r.results[0]["out_0"]
```

```python
from contextlib import ExitStack

import concourse.bass as bass
from concourse import mybir
import numpy as np

F32 = mybir.dt.float32
BF16 = mybir.dt.bfloat16
I32 = mybir.dt.int32
ALU = mybir.AluOpType
ACT = mybir.ActivationFunctionType
AX = mybir.AxisListType

NB, L, D = 16, 750, 128
H = 8
HD = D // H
SCALE = float(HD) ** -0.5
K_TOP = max(1, int(L * 0.2))
EPS = 1e-5
FF = 512
TT = 125
NT = L // TT
HALF = L // 2
NG = NB * H
JT = 76
NJ = 2 * JT
PARTS = 6
KR = PARTS * HD
S = L // 2
ST = S // TT
NTILE = NB * ST
E = 8
EH = 512
BLK = 128
ROUNDER = 1.5 * 2.0 ** 23
CUTS = 4
NBLK = (NB * S) // BLK + E
assert NT * TT == L and ST * TT == S and K_TOP + 2 == NJ and NG == 128

COLS = ["o_b", "ln1_g", "ln1_b", "f2_b", "ln2_g", "ln2_b", "conv_b", "f1_b0", "f1_b1", "f1_b2", "f1_b3"]


def norms_and_ranks(nc, t, io):
    with ExitStack() as ctx:
        def sb(name, shape, dt=F32):
            return ctx.enter_context(nc.sbuf_tensor(name, shape, dt))

        def sem(name):
            return ctx.enter_context(nc.semaphore(name))

        wq = sb("wq", [D, D])
        qb = sb("qb_rows", [TT, D])
        x_in = [sb(f"x_in1{p}", [TT, NT, D]) for p in range(2)]
        xT = [sb(f"xT1{p}", [D, L]) for p in range(2)]
        q_sb = [sb(f"q_sb{p}", [TT, NT * D]) for p in range(2)]
        sq = [sb(f"sq{p}", [TT, NT * D]) for p in range(2)]
        qn_tok = sb("qn_tok", [TT, NT, NG])
        qn = sb("qn", [NG, L])
        top8 = sb("top8", [NG, 8])
        ones = sb("ones_row", [NG, L])
        count = sb("count", [NG, L])
        rank = sb("rank", [NG, L])
        rank_bf = sb("rank_bf", [NG, L], BF16)
        xT_ps = [ctx.enter_context(nc.psum_tensor(f"xT_ps{p}", [D, 2, 512], F32)) for p in range(2)]
        q_ps = [ctx.enter_context(nc.psum_tensor(f"q_ps{p}", [D, 2, 512], F32)) for p in range(2)]

        w_loaded = sem("w_loaded")
        x_loaded = [sem(f"x_loaded1{p}") for p in range(2)]
        xT_done = [sem(f"xT_done1{p}") for p in range(2)]
        xT_ready = [sem(f"xT_ready1{p}") for p in range(2)]
        q_done = [sem(f"q_done{p}") for p in range(2)]
        q_ready = [sem(f"q_ready{p}") for p in range(2)]
        q_stored = [sem(f"q_stored{p}") for p in range(2)]
        sq_ready = [sem(f"sq_ready{p}") for p in range(2)]
        norm_ready = [sem(f"norm_ready{p}") for p in range(2)]
        norms_turned = sem("norms_turned")
        top = sem("top_step")
        ranks_ready = sem("ranks_ready")
        ranks_turned = sem("ranks_turned")
        ranks_out = sem("ranks_out")
        x_v = io["x"].rearrange("b (n p) d -> b p n d", p=TT)

        with nc.Block() as block:
            @block.sync
            def _(sp):
                sp.dma_start(t["ident"][:, :], io["c_ident"]).then_inc(w_loaded, 16)
                sp.dma_start(wq[:, :], io["L0_tok_q_w"]).then_inc(w_loaded, 16)
                sp.dma_start(qb[:, :], io["L0_tok_q_b"].rearrange("(a n) -> a n", a=1).to_broadcast([TT, D])).then_inc(w_loaded, 16)
                with sp.Fori(0, NB // 2) as i:
                    for p in range(2):
                        sp.wait_ge(xT_done[p], i)
                        sp.dma_start(x_in[p][:, :, :], x_v[bass.ds(2 * i + p, 1), :, :, :].rearrange("b p n d -> (b p) n d"))\
                          .then_inc(x_loaded[p], 16)
                sp.wait_ge(ranks_ready, 1)
                sp.dma_start(io["rank_rows"], rank_bf[:, :]).then_inc(ranks_out, 16)
                sp.wait_ge(ranks_out, 16)

            @block.tensor
            def _(pe):
                pe.wait_ge(w_loaded, 48)
                with pe.Fori(0, NB // 2) as i:
                    for p in range(2):
                        pe.wait_ge(x_loaded[p], 16 * i + 16)
                        pe.wait_ge(xT_ready[p], i)
                        for n in range(NT):
                            mm = pe.transpose(xT_ps[p][:, n // 3, (n % 3) * TT:(n % 3 + 1) * TT],
                                              x_in[p][:, n, :], t["ident"][0:TT, 0:TT])
                        mm.then_inc(xT_done[p], 1)
                    for p in range(2):
                        pe.wait_ge(xT_ready[p], i + 1)
                        pe.wait_ge(q_ready[p], i)
                        for n in range(NT):
                            mm = pe.matmul(q_ps[p][0:TT, n // 3, (n % 3) * D:(n % 3 + 1) * D],
                                           xT[p][:, n * TT:(n + 1) * TT], wq[:, :], start=True, stop=True)
                        mm.then_inc(q_done[p], 1)
                for p in range(2):
                    pe.wait_ge(norm_ready[p], NB // 2)
                for n in range(NT):
                    mm = pe.transpose(xT_ps[0][:, n // 3, (n % 3) * TT:(n % 3 + 1) * TT], qn_tok[:, n, :],
                                      t["ident"][0:TT, 0:TT])
                mm.then_inc(norms_turned, 1)
                pe.wait_ge(ranks_ready, 1)
                for n in range(NT):
                    mm = pe.transpose(q_ps[0][0:TT, n // 3, (n % 3) * NG:(n % 3 + 1) * NG], rank[:, n * TT:(n + 1) * TT],
                                      t["ident"][:, :])
                mm.then_inc(ranks_turned, 1)

            @block.scalar
            def _(act):
                with act.Fori(0, NB // 2) as i:
                    for p in range(2):
                        act.wait_ge(xT_done[p], i + 1)
                        act.wait_ge(q_done[p], i)
                        act.activation(xT[p][:, :].rearrange("p (a c) -> p a c", a=2), xT_ps[p][:, :, 0:HALF],
                                       ACT.Copy).then_inc(xT_ready[p], 1)
                    for p in range(2):
                        act.wait_ge(q_ready[p], i + 1)
                        act.wait_ge(norm_ready[p], i)
                        act.activation(sq[p][:, :], q_sb[p][:, :], ACT.Square).then_inc(sq_ready[p], 1)
                        act.dma_start(io["q_rows"][bass.ds(2 * i + p, 1), :, :].rearrange("b p n -> (b p) n"), q_sb[p][:, :])\
                           .then_inc(q_stored[p], 16)
                for p in range(2):
                    act.wait_ge(q_stored[p], 16 * (NB // 2))

            @block.vector
            def _(dve):
                step = [0]

                def chain(ins):
                    step[0] += 1
                    ins.then_inc(top, 1)
                    dve.wait_ge(top, step[0])

                chain(dve.memset(ones[:, :], 1.0))
                dve.wait_ge(w_loaded, 48)
                with dve.Fori(0, NB // 2) as i:
                    for p in range(2):
                        dve.wait_ge(q_done[p], i + 1)
                        dve.wait_ge(q_stored[p], 16 * i)
                        dve.wait_ge(sq_ready[p], i)
                        dve.tensor_tensor(
                            q_sb[p][:, :].rearrange("p (a n d) -> p a n d", a=2, n=3),
                            q_ps[p][0:TT, :, 0:3 * D].rearrange("p a (n d) -> p a n d", n=3),
                            qb[:, :].unsqueeze(1).unsqueeze(1).to_broadcast([TT, 2, 3, D]), ALU.add).then_inc(q_ready[p], 1)
                    for p in range(2):
                        dve.wait_ge(sq_ready[p], i + 1)
                        dve.tensor_reduce(qn_tok[:, :, bass.ds((2 * i + p) * H, H)],
                                          sq[p][:, :].rearrange("p (n h d) -> p n h d", n=NT, h=H), AX.X, ALU.add)\
                           .then_inc(norm_ready[p], 1)
                dve.wait_ge(norms_turned, 1)
                chain(dve.tensor_copy(qn[:, :].rearrange("p (a c) -> p a c", a=2), xT_ps[0][:, :, 0:HALF]))
                left = K_TOP
                while left > 0:
                    chain(dve.max(top8[:, :], qn[:, :]))
                    if left < 8:
                        chain(dve.memset(top8[:, left:8], -1.0))
                    chain(dve.match_replace(qn[:, :], top8[:, :], qn[:, :], -1.0))
                    left -= 8
                chain(dve.tensor_scalar(qn[:, :], qn[:, :], -1.0, None, ALU.is_equal))
                chain(dve.tensor_tensor_scan(count[:, :], ones[:, :], qn[:, :], 0.0, ALU.mult, ALU.add))
                chain(dve.tensor_tensor(count[:, :], count[:, :], qn[:, :], ALU.mult))
                chain(dve.tensor_scalar(rank[:, :], count[:, :], -1.0, None, ALU.add))
                dve.tensor_copy(rank_bf[:, :], rank[:, :]).then_inc(ranks_ready, 1)
                dve.wait_ge(ranks_turned, 1)
                dve.tensor_copy(t["rank_tok"][:, :, :].rearrange("p (a n) g -> p a n g", a=2),
                                q_ps[0][0:TT, :, 0:3 * NG].rearrange("p a (n g) -> p a n g", n=3))


def sequences(nc, t, io):
    P_TILES = ["xT", "k", "v"]
    A_ONLY = [f"kt{i}" for i in range(4)] + ["g0", "g1"] + [f"max{i}" for i in range(2 * H)] + ["mt"] + [f"s{h}" for h in range(H)]
    A_TILES = [step for part, step in order() if step in P_TILES + A_ONLY]
    D_TILES = ["sc", "o", "c1", "m1", "f0", "f1", "f2", "f3", "ff", "c2", "m2", "cv", "ht"]
    A_SLOTS = 2
    FIRST = A_TILES.index("xT")
    EMPTY = [("P", name) for name in A_TILES[FIRST:] if name not in P_TILES] + [("AD", "xT"), ("AD", "k")]
    assert A_TILES[-1] == "v" and all(name[0] == "s" or parts == "AD" for parts, name in EMPTY)
    A_PER = len(A_TILES) // A_SLOTS
    D_PER = len(D_TILES)
    assert A_PER * A_SLOTS == len(A_TILES)

    with ExitStack() as ctx:
        def sb(name, shape, dt=F32):
            return ctx.enter_context(nc.sbuf_tensor(name, shape, dt))

        def sem(name):
            return ctx.enter_context(nc.semaphore(name))

        wkv = sb("wkv", [D, 2 * D])
        kvb = sb("kvb_rows", [TT, 2 * D])
        wo = sb("wo", [D, D])
        f1 = sb("f1", [D, FF])
        f2 = sb("f2", [128, FF // 128, D])
        cw = sb("conv_taps", [D, 3, D])
        cols = sb("feature_cols", [D, len(COLS)])
        center = sb("center", [D, D])
        mean = sb("mean", [D, D])
        ident_bf = sb("ident_bf", [128, 128], BF16)
        iota = sb("iota_f", [TT, NJ])
        iota_bf = sb("iota_bf", [TT, NJ], BF16)
        slot_id = sb("slot_id", [JT, 2])
        eps = sb("eps", [D, 1])
        x_in = sb("x_in", [TT, NT, D])
        q_in = sb("q_in", [TT, NT * H, HD])
        xT = [sb(f"xT{p}", [D, L]) for p in range(2)]
        kf = sb("kf", [TT, NT * H, HD])
        q_rest = sb("q_rest", [TT, NT * H, HD])
        k_rest = sb("k_rest", [TT, NT * H, HD])
        qst = sb("qst", [TT, NT * H, PARTS, HD], BF16)
        kst = sb("kst", [TT, NT * H, PARTS, HD], BF16)
        v_pad = sb("v_pad", [TT, NT, H, 32])
        rank_cur = sb("rank_cur", [TT, NT, H])
        rank_bc = sb("rank_bc", [JT, H * L], BF16)
        G = sb("G", [TT, NT, H, NJ], BF16)
        GT = sb("GT", [JT, 2, H * L], BF16)
        kT = sb("kT", [KR + 3, H, L], BF16)
        qT = sb("qT", [KR + 3, H * NJ], BF16)
        mx = sb("mx", [JT, 2 * H])
        mx_rest = sb("mx_rest", [JT, 2 * H])
        mx_rest2 = sb("mx_rest2", [JT, 2 * H])
        mxp = sb("mxp", [JT, 3, 2 * H], BF16)
        mxT = sb("mxT", [6 * H, JT], BF16)
        Pt = sb("Pt", [TT, H, NT * NJ])
        au = sb("au", [128, 2, NJ])
        rden = sb("rden", [JT, 4, 4])
        att = sb("att", [JT, 512])
        att_rest = sb("att_rest", [JT, 512])
        attp = sb("attp", [JT, 3, 512], BF16)
        attT = sb("attT", [D, L])
        ao = sb("ao", [D, L])
        aob = sb("aob", [D, L])
        r = sb("r", [D, L])
        cS = sb("cS", [D, L])
        sq = sb("sqD", [D, L])
        h1 = sb("h1", [D, L])
        rl = sb("rl", [128, FF // 128, L])
        fu = sb("fu", [D, L + 2])
        hp = sb("hp", [D, S])
        hT = sb("hT", [D, S])
        h_sb = sb("h_sb", [TT, ST * D])

        a_ps = [ctx.enter_context(nc.psum_tensor(f"a_ps{s}", [128, 2, 512], F32)) for s in range(A_SLOTS)]
        d_ps = ctx.enter_context(nc.psum_tensor("d_ps", [128, 2, 512], F32))
        pv_ps = ctx.enter_context(nc.psum_tensor("pv_ps", [128, 512], F32))
        at_ps = ctx.enter_context(nc.psum_tensor("at_ps", [128, 512], F32))

        const_loaded = sem("const_loaded")
        const_made = sem("const_made")
        const_set = sem("const_set")
        a_done = [sem(f"a_done{s}") for s in range(A_SLOTS)]
        a_free = [sem(f"a_free{s}") for s in range(A_SLOTS)]
        d_done = sem("d_done")
        d_free = sem("d_free")
        x_loaded = sem("x_loaded")
        q_loaded = sem("q_loaded")
        rank_loaded = sem("rank_loaded")
        rounded = {"q": sem("q_rounded"), "k": sem("k_rounded")}
        reduced = {"q": sem("q_reduced"), "k": sem("k_reduced")}
        copied = {"q": sem("q_copied"), "k": sem("k_copied")}
        cur_ready = sem("cur_ready")
        g_ready = sem("g_ready")
        gt_ready = sem("gt_ready")
        mx_step = sem("mx_step")
        mxp_ready = sem("mxp_ready")
        mxT_ready = sem("mxT_ready")
        mx_rows = sem("mx_rows")
        pv_done = [sem(f"pv_done{q}") for q in range(2)]
        au_ready = sem("au_ready")
        att_step = sem("att_step")
        attp_ready = sem("attp_ready")
        r_ready = sem("r_ready")
        aob_ready = sem("aob_ready")
        sq_ready = sem("sq_readyD")
        ln_step = sem("ln_step")
        rstd_ready = sem("rstd_ready")
        at_done = sem("at_done")
        h1_ready = sem("h1_ready")
        fu_ready = sem("fu_ready")
        hp_ready = sem("hp_ready")
        hT_ready = sem("hT_ready")
        h_ready = sem("h_ready")
        h_stored = sem("h_stored")
        gates = {eng: sem(f"gate_{n}") for n, eng in (("sp", nc.sync), ("pool", nc.gpsimd), ("pe", nc.tensor))}

        def a_slot(name):
            return A_TILES.index(name) % A_SLOTS

        def a_count(name, b):
            return A_PER * (b if name in P_TILES else b + 1) + A_TILES.index(name) // A_SLOTS + 1

        def credit(slot):
            return len([n for n in A_TILES[:FIRST] if a_slot(n) == slot])

        def a_tile(name):
            return a_ps[a_slot(name)]

        def d_count(name, b):
            return D_PER * (b + 1) + D_TILES.index(name) + 1

        def await_a(eng, what, name, b):
            await_count(eng, what[a_slot(name)], a_count(name, b))

        def col(name):
            return cols[:, COLS.index(name):COLS.index(name) + 1]

        def await_count(eng, semaphore, count):
            if not isinstance(count, int) or count > 0:
                eng.wait_ge(semaphore, count)

        def gate(eng):
            eng.sem_inc(gates[eng], 1)

        def two(ap):
            return ap.rearrange("p (a c) -> p a c", a=2)

        def two_of_three(ap, n):
            return ap[0:TT, :, 0:3 * n].rearrange("p a (t c) -> p a t c", t=3)

        KTS = TT + 1

        def turned_k(i):
            return a_tile(f"kt{i}")[0:KR, :, 0:NT * KTS // 2].bitcast(BF16).rearrange("p g (n c) -> p g n c", n=NT)[:, :, :, 0:TT]

        x_v = io["x"].rearrange("b (n p) d -> b p n d", p=TT)

        def run(eng, part_p, part_a, part_d, hand_on=None):
            def round_of(b, pb, parts="PAD"):
                for part, step in ORDER:
                    if hand_on and (parts, step) in EMPTY:
                        hand_on(step, b + 1 if part == "P" else b)
                    if part == "P" and part in parts and step in part_p:
                        part_p[step](b + 1, 1 - pb)
                    if part == "A" and part in parts and step in part_a:
                        part_a[step](b, pb)
                    if part == "D" and part in parts and step in part_d:
                        part_d[step](b - 1, 1 - pb)
            round_of(-1, 1, "P")
            round_of(0, 0, "PA")
            with eng.Fori(0, NB // 2 - 1) as i:
                round_of(2 * i + 1, 1)
                round_of(2 * i + 2, 0)
            round_of(NB - 1, 1, "AD")
            round_of(NB, 0, "D")

        ORDER = order()

        with nc.Block() as block:
            @block.sync
            def _(sp):
                loads = [(wkv[:, 0:D], io["L0_tok_k_w"]), (wkv[:, D:2 * D], io["L0_tok_v_w"]),
                         (kvb[:, 0:D], io["L0_tok_k_b"].rearrange("(a n) -> a n", a=1).to_broadcast([TT, D])),
                         (kvb[:, D:2 * D], io["L0_tok_v_b"].rearrange("(a n) -> a n", a=1).to_broadcast([TT, D])),
                         (wo[:, :], io["L0_tok_o_w"]), (f1[:, :], io["L0_tok_f1_w"]), (f2[:, :, :], io["L0_tok_f2_w"].rearrange("(c p) d -> p c d", p=128)),
                         (cw[:, :, :], io["conv_w"]), (cols[:, :], io["cols"]), (center[:, :], io["c_center"]),
                         (iota[:, :], io["c_iota"].to_broadcast([TT, NJ])), (slot_id[:, :], io["c_slot_id"])]
                for dst, src in loads:
                    sp.dma_start(dst, src).then_inc(const_loaded, 16)
                sp.sem_inc(h_stored, 16)
                CONSTS = len(loads)
                assert CONSTS == N_CONST

                def load(b, pb):
                    await_a(sp, a_done, "xT", b - 1)
                    gate(sp)
                    sp.dma_start(x_in[:, :, :], x_v[bass.ds(b, 1), :, :, :].rearrange("b p n d -> (b p) n d")).then_inc(x_loaded, 16)
                    await_count(sp, reduced["q"], 2 * b - 1)
                    gate(sp)
                    sp.dma_start(q_in[:, :, :].rearrange("p g d -> p (g d)"),
                                 io["q_rows"][bass.ds(b, 1), :, :].rearrange("b p n -> (b p) n")).then_inc(q_loaded, 16)

                def load_ranks(b, pb):
                    await_count(sp, gt_ready, b)
                    gate(sp)
                    sp.dma_start(rank_bc[:, :], io["rank_rows"].rearrange("(b h) l -> b (h l)", h=H)[bass.ds(b, 1), :]
                                 .to_broadcast([JT, H * L])).then_inc(rank_loaded, 16)

                def max_rows(b, pb):
                    sp.wait_ge(mxT_ready, b + 1)
                    gate(sp)
                    for k in range(3):
                        sp.dma_start(qT[KR + k:KR + k + 1, :], mxT[2 * H * k:2 * H * (k + 1), :]).then_inc(mx_rows, 16)

                def store_h(b, pb):
                    sp.wait_ge(h_ready, b + 1)
                    gate(sp)
                    sp.dma_start(io["h_rows"][bass.ds(b, 1), :, :].rearrange("b p n -> (b p) n"), h_sb[:, :]).then_inc(h_stored, 16)

                run(sp, {"load": load, "ranks": load_ranks}, {"mt": max_rows}, {"ht": store_h})
                sp.wait_ge(h_stored, 16 * NB + 16)

            @block.gpsimd
            def _(pool):
                pool.wait_ge(const_loaded, 16 * N_CONST)
                pool.tensor_copy(iota_bf[:, :], iota[:, :]).then_inc(const_made, 1)
                pool.tensor_copy(ident_bf[:, :], t["ident"][:, :]).then_inc(const_made, 1)

                def take_off(x, n, out, whole, part):
                    def go(b, pb):
                        pool.wait_ge(rounded[x], 2 * b + n)
                        pool.tensor_tensor(out, whole, part, ALU.subtract).then_inc(reduced[x], 1)
                    return go

                def residual_bias(b, pb):
                    pool.wait_ge(d_free, d_count("o", b))
                    gate(pool)
                    pool.tensor_scalar(aob[:, :], ao[:, :], col("ln2_b"), None, ALU.add).then_inc(aob_ready, 1)

                run(pool, {"q_rest": take_off("q", 1, q_rest[:, :, :], q_in[:, :, :], qst[:, :, 0, :]),
                           "q_third": take_off("q", 2, qst[:, :, 5, :], q_rest[:, :, :], qst[:, :, 3, :]),
                           "k_rest": take_off("k", 1, k_rest[:, :, :], kf[:, :, :], kst[:, :, 0, :]),
                           "k_third": take_off("k", 2, kst[:, :, 2, :], k_rest[:, :, :], kst[:, :, 1, :])},
                    {}, {"o": residual_bias})

            @block.tensor
            def _(pe):
                for slot in range(A_SLOTS):
                    pe.sem_inc(a_done[slot], credit(slot))
                pe.sem_inc(d_done, D_PER)
                pe.wait_ge(const_loaded, 16 * N_CONST)
                pe.wait_ge(const_made, 2)
                pe.wait_ge(const_set, 11)

                def taken(b, names, fill=None):
                    for slot in range(A_SLOTS):
                        counts = [a_count(n, 0) for n in names if a_slot(n) == slot]
                        if fill is not None and a_slot(fill) == slot:
                            counts.append(a_count(fill, 0) - 1)
                        if counts:
                            pe.wait_ge(a_free[slot], A_PER * b + max(counts))

                def fill_a(name, b, reads=()):
                    taken(b, reads, name)
                    return a_tile(name)

                def filled_a(mm, name):
                    mm.then_inc(a_done[a_slot(name)], 1)

                def fill_d(name, b):
                    pe.wait_ge(d_free, d_count(name, b) - 1)
                    return d_ps

                def turn_x(b, pb):
                    pe.wait_ge(x_loaded, 16 * b + 16)
                    ps = fill_a("xT", b)
                    for n in range(NT):
                        mm = pe.transpose(ps[:, n // 3, (n % 3) * TT:(n % 3 + 1) * TT], x_in[:, n, :], t["ident"][0:TT, 0:TT])
                    filled_a(mm, "xT")

                def project(name, w):
                    def go(b, pb):
                        ps = fill_a(name, b, ["xT"])
                        for n in range(NT):
                            mm = pe.matmul(ps[0:TT, n // 3, (n % 3) * D:(n % 3 + 1) * D], xT[pb][:, n * TT:(n + 1) * TT], w,
                                           start=True, stop=True)
                        filled_a(mm, name)
                    return go

                def turn_k(i):
                    def go(b, pb):
                        pe.wait_ge(copied["k"], b + 1)
                        pe.wait_ge(reduced["k"], 2 * b + 2)
                        ps = fill_a(f"kt{i}", b)
                        for g in range(2):
                            for n in range(NT):
                                mm = pe.transpose(ps[0:KR, g, :].bitcast(BF16)[:, n * KTS:n * KTS + TT],
                                                  kst[:, n * H + 2 * i + g, :, :].rearrange("p a d -> p (a d)"),
                                                  ident_bf[0:TT, 0:TT])
                        filled_a(mm, f"kt{i}")
                    return go

                def gather(i):
                    def go(b, pb):
                        pe.wait_ge(copied["q"], b + 1)
                        pe.wait_ge(reduced["q"], 2 * b + 2)
                        pe.wait_ge(g_ready, b + 1)
                        ps = fill_a(f"g{i}", b)
                        for g in range(4):
                            h = 4 * i + g
                            for n in range(NT):
                                mm = pe.matmul(ps[0:KR, g // 2, (g % 2) * NJ:(g % 2 + 1) * NJ],
                                               qst[:, n * H + h, :, :].rearrange("p a d -> p (a d)"), G[:, n, h, :],
                                               start=(n == 0), stop=(n == NT - 1))
                        filled_a(mm, f"g{i}")
                    return go

                def scores_for_max(i):
                    h, jt = i // 2, i % 2

                    def go(b, pb):
                        ps = fill_a(f"max{i}", b, [f"kt{h // 2}", f"g{h // 4}"])
                        for c in range(2):
                            mm = pe.matmul(ps[0:JT, c, 0:HALF], qT[0:KR, i * JT:(i + 1) * JT],
                                           kT[0:KR, h, c * HALF:(c + 1) * HALF], start=True, stop=True)
                        filled_a(mm, f"max{i}")
                    return go

                def turn_max(b, pb):
                    pe.wait_ge(mxp_ready, b + 1)
                    ps = fill_a("mt", b)
                    gate(pe)
                    filled_a(pe.transpose(ps[0:6 * H, 0, 0:JT // 2].bitcast(BF16), mxp[:, :, :].rearrange("p a s -> p (a s)"),
                                          ident_bf[0:JT, 0:JT]), "mt")

                def scores(h):
                    def go(b, pb):
                        pe.wait_ge(mx_rows, 48 * b + 48)
                        ps = fill_a(f"s{h}", b)
                        for n in range(NT):
                            mm = pe.matmul(ps[0:TT, n // 3, (n % 3) * NJ:(n % 3 + 1) * NJ], kT[:, h, n * TT:(n + 1) * TT],
                                           qT[:, h * NJ:(h + 1) * NJ], start=True, stop=True)
                        filled_a(mm, f"s{h}")
                    return go

                def values(q):
                    def go(b, pb):
                        taken(b, ["v"] + [f"s{4 * q + g}" for g in range(4)])
                        await_count(pe, au_ready, b)
                        for n in range(NT):
                            for g in range(4):
                                mm = pe.matmul(pv_ps[32 * g:32 * g + 32, q * NJ:(q + 1) * NJ], v_pad[:, n, 4 * q + g, :],
                                               Pt[:, 4 * q + g, n * NJ:(n + 1) * NJ], start=(n == 0), stop=(n == NT - 1))
                        mm.then_inc(pv_done[q], 1)
                    return go

                def turn_att(b, pb):
                    pe.wait_ge(au_ready, b + 1)
                    for q in range(2):
                        for jt in range(2):
                            mm = pe.transpose(at_ps[0:JT, (2 * q + jt) * 128:(2 * q + jt + 1) * 128],
                                              au[:, q, jt * JT:(jt + 1) * JT], t["ident"][:, :])
                    mm.then_inc(at_done, 1)

                def scatter(b, pb):
                    pe.wait_ge(attp_ready, b + 1)
                    pe.wait_ge(gt_ready, b + 1)
                    ps = fill_d("sc", b)
                    for c in range(2):
                        for odd in range(2):
                            for k in range(3):
                                for jt in range(2):
                                    for g in range(4):
                                        h = 2 * g + odd
                                        at = (2 * (h // 4) + jt) * 128 + 32 * (h % 4)
                                        mm = pe.matmul(ps[32 * g:32 * g + 32, c, 0:HALF], attp[:, k, at:at + 32],
                                                       GT[:, jt, h * L + c * HALF:h * L + (c + 1) * HALF],
                                                       start=(odd == 0 and k == 0 and jt == 0), stop=(odd == 1 and k == 2 and jt == 1))
                    mm.then_inc(d_done, 1)

                def dense(name, terms, waits):
                    def go(b, pb):
                        for w in waits:
                            w(b)
                        ps = fill_d(name, b)
                        for c in range(2):
                            for k, (w, data) in enumerate(terms):
                                mm = pe.matmul(ps[:, c, 0:HALF], w, data[:, c * HALF:(c + 1) * HALF],
                                               start=(k == 0), stop=(k == len(terms) - 1))
                        mm.then_inc(d_done, 1)
                    return go

                def convolve(b, pb):
                    pe.wait_ge(fu_ready, b + 1)
                    ps = fill_d("cv", b)
                    for c, (at, n) in enumerate(((0, HALF + 1), (HALF + 1, HALF - 1))):
                        for tap in range(3):
                            mm = pe.matmul(ps[:, c, 0:n], cw[:, tap, :], fu[:, at + tap:at + tap + n],
                                           start=(tap == 0), stop=(tap == 2))
                    mm.then_inc(d_done, 1)

                def turn_h(b, pb):
                    pe.wait_ge(hT_ready, b + 1)
                    ps = fill_d("ht", b)
                    for n in range(ST):
                        mm = pe.transpose(ps[0:TT, 0, n * D:(n + 1) * D], hT[:, n * TT:(n + 1) * TT], t["ident"][:, :])
                    mm.then_inc(d_done, 1)

                part_p = {"xT": turn_x, "k": project("k", wkv[:, 0:D]), "v": project("v", wkv[:, D:2 * D])}
                part_a = {"mt": turn_max}
                for i in range(4):
                    part_a[f"kt{i}"] = turn_k(i)
                for i in range(2):
                    part_a[f"g{i}"] = gather(i)
                    part_a[f"pv{i}"] = values(i)
                for i in range(2 * H):
                    part_a[f"max{i}"] = scores_for_max(i)
                for h in range(H):
                    part_a[f"s{h}"] = scores(h)
                part_d = {"at": turn_att, "sc": scatter, "cv": convolve, "ht": turn_h}
                part_d["o"] = dense("o", [(wo[:, :], attT[:, :])], [])
                part_d["c1"] = dense("c1", [(center[:, :], r[:, :])], [lambda b: pe.wait_ge(r_ready, 2 * b + 1)])
                part_d["m1"] = dense("m1", [(mean[:, :], sq[:, :])], [lambda b: pe.wait_ge(sq_ready, 2 * b + 1)])
                for i in range(4):
                    part_d[f"f{i}"] = dense(f"f{i}", [(f1[:, i * 128:(i + 1) * 128], h1[:, :])],
                                            [lambda b: pe.wait_ge(h1_ready, b + 1)])
                part_d["ff"] = dense("ff", [(f2[:, i, :], rl[:, i, :]) for i in range(4)],
                                     [])
                part_d["c2"] = dense("c2", [(center[:, :], r[:, :])], [lambda b: pe.wait_ge(r_ready, 2 * b + 2)])
                part_d["m2"] = dense("m2", [(mean[:, :], sq[:, :])], [lambda b: pe.wait_ge(sq_ready, 2 * b + 2)])
                def hand_on(name, b):
                    fill_a(name, b)
                    pe.sem_inc(a_done[a_slot(name)], 1)

                run(pe, part_p, part_a, part_d, hand_on)

            @block.scalar
            def _(act):
                act.preload_act_table_set("natural_log_exp_and_others")
                for slot in range(A_SLOTS):
                    act.sem_inc(a_free[slot], credit(slot))
                act.sem_inc(d_free, D_PER)
                act.wait_ge(const_loaded, 16 * N_CONST)
                act.wait_ge(const_made, 2)
                act.wait_ge(const_set, 11)

                def take_xT(b, pb):
                    await_a(act, a_done, "xT", b)
                    await_count(act, r_ready, 2 * b - 3)
                    act.activation(two(xT[pb][:, :]), a_tile("xT")[:, :, 0:HALF], ACT.Copy).then_inc(a_free[a_slot("xT")], 1)

                def take_kT(i):
                    def go(b, pb):
                        await_a(act, a_done, f"kt{i}", b)
                        act.activation(kT[0:KR, 2 * i:2 * i + 2, :].rearrange("p g (n c) -> p g n c", n=NT), turned_k(i), ACT.Copy)\
                           .then_inc(a_free[a_slot(f"kt{i}")], 1)
                    return go

                def take_qT(i):
                    def go(b, pb):
                        await_a(act, a_done, f"g{i}", b)
                        act.activation(qT[0:KR, i * 4 * NJ:(i + 1) * 4 * NJ].rearrange("p (a c) -> p a c", a=2),
                                       a_tile(f"g{i}")[0:KR, :, 0:2 * NJ], ACT.Copy).then_inc(a_free[a_slot(f"g{i}")], 1)
                    return go

                def exps(h):
                    def go(b, pb):
                        await_a(act, a_done, f"s{h}", b)
                        act.activation(Pt[:, h, :].rearrange("p (a c) -> p a c", a=2), a_tile(f"s{h}")[0:TT, :, 0:3 * NJ],
                                       ACT.Exp, scale=SCALE).then_inc(a_free[a_slot(f"s{h}")], 1)
                    return go

                def round_part(x, n, out, whole, last_read):
                    def go(b, pb):
                        if n == 1:
                            x_there(b)[x]()
                            await_a(act, a_done, last_read, b - 1)
                        else:
                            act.wait_ge(reduced[x], 2 * b + 1)
                        act.activation(out, whole, ACT.Copy).then_inc(rounded[x], 1)
                    return go

                def x_there(b):
                    return {"q": lambda: act.wait_ge(q_loaded, 16 * b + 16), "k": lambda: await_a(act, a_free, "k", b)}

                def take_pv(b, pb):
                    act.wait_ge(pv_done[0], b + 1)
                    act.wait_ge(pv_done[1], b + 1)
                    act.activation(au[:, :, :].rearrange("p a c -> p (a c)"), pv_ps[:, 0:2 * NJ], ACT.Copy).then_inc(au_ready, 1)

                def take_sc(b, pb):
                    act.wait_ge(d_done, d_count("sc", b))
                    act.activation(two(attT[:, :]), d_ps[:, :, 0:HALF], ACT.Copy).then_inc(d_free, 1)

                def take_o(b, pb):
                    act.wait_ge(d_done, d_count("o", b))
                    act.activation(two(ao[:, :]), d_ps[:, :, 0:HALF], ACT.Identity, bias=col("o_b")).then_inc(d_free, 1)

                def take_c(i):
                    def go(b, pb):
                        act.wait_ge(d_done, d_count(f"c{i}", b))
                        act.activation(two(cS[:, :]), d_ps[:, :, 0:HALF], ACT.Copy)
                        act.activation(two(sq[:, :]), d_ps[:, :, 0:HALF], ACT.Square).then_inc(sq_ready, 1)
                        act.wait_ge(sq_ready, 2 * b + i)
                        act.sem_inc(d_free, 1)
                    return go

                def take_m(i):
                    def go(b, pb):
                        act.wait_ge(d_done, d_count(f"m{i}", b))
                        act.activation(two(sq[:, :]), d_ps[:, :, 0:HALF], ACT.Ln, bias=eps[:, :]).then_inc(d_free, 1)
                        act.wait_ge(d_free, d_count(f"m{i}", b))
                        act.activation(sq[:, :], sq[:, :], ACT.Exp, scale=-0.5).then_inc(rstd_ready, 1)
                    return go

                def take_f(i):
                    def go(b, pb):
                        act.wait_ge(d_done, d_count(f"f{i}", b))
                        act.activation(two(rl[:, i, :]), d_ps[:, :, 0:HALF], ACT.Relu, bias=col(f"f1_b{i}")).then_inc(d_free, 1)
                    return go

                def relu_h(b, pb):
                    act.wait_ge(hp_ready, 2 * b + 2)
                    act.activation(hT[:, :], hp[:, :], ACT.Relu, bias=col("conv_b")).then_inc(hT_ready, 1)

                def take_h(b, pb):
                    act.wait_ge(d_done, d_count("ht", b))
                    act.wait_ge(h_stored, 16 * b + 16)
                    act.activation(h_sb[:, :], d_ps[0:TT, 0, 0:ST * D], ACT.Copy).then_inc(h_ready, 1)
                    act.wait_ge(h_ready, b + 1)
                    act.sem_inc(d_free, 1)

                part_p = {"xT": take_xT,
                          "q_first": round_part("q", 1, qst[:, :, 0, :], q_in[:, :, :], "g1"),
                          "q_second": round_part("q", 2, qst[:, :, 3, :], q_rest[:, :, :], "g1"),
                          "k_first": round_part("k", 1, kst[:, :, 0, :], kf[:, :, :], "kt3"),
                          "k_second": round_part("k", 2, kst[:, :, 1, :], k_rest[:, :, :], "kt3")}
                part_a = {"g0": take_qT(0), "g1": take_qT(1), "au": take_pv}
                for i in ACT_KT:
                    part_a[f"kt{i}"] = take_kT(i)
                for h in range(H):
                    part_a[f"s{h}"] = exps(h)
                part_d = {"sc": take_sc, "o": take_o, "c1": take_c(1), "c2": take_c(2), "m1": take_m(1), "m2": take_m(2),
                          "relu": relu_h, "ht": take_h}
                for i in ACT_F:
                    part_d[f"f{i}"] = take_f(i)
                def hand_on(name, b):
                    if name != "k":
                        await_a(act, a_done, name, b)
                        act.sem_inc(a_free[a_slot(name)], 1)

                run(act, part_p, part_a, part_d, hand_on)

            @block.vector
            def _(dve):
                dve.memset(mean[:, :], 1.0 / D).then_inc(const_set, 1)
                dve.memset(eps[:, :], EPS).then_inc(const_set, 1)
                dve.memset(v_pad[:, :, :, :], 0.0).then_inc(const_set, 1)
                dve.memset(kT[KR:KR + 3, :, :], -1.0).then_inc(const_set, 1)
                dve.memset(fu[:, :], 0.0).then_inc(const_set, 1)
                dve.wait_ge(const_set, 3)
                for odd in range(2):
                    dve.memset(v_pad[:, :, odd:H:2, HD * (1 - odd):HD * (1 - odd) + 1], 1.0).then_inc(const_set, 1)
                for k in range(3):
                    dve.memset(attp[:, k, :], 0.0).then_inc(const_set, 1)
                dve.memset(att[:, :], 0.0).then_inc(const_set, 1)
                dve.wait_ge(const_loaded, 16 * N_CONST)
                dve.wait_ge(const_made, 2)
                dve.wait_ge(const_set, 11)

                def one_hots(part):
                    def go(b, pb):
                        if part == 0:
                            dve.tensor_copy(rank_cur[:, :, :], t["rank_tok"][:, :, bass.ds(b * H, H)]).then_inc(cur_ready, 1)
                            dve.wait_ge(cur_ready, b + 1)
                            await_a(dve, a_done, "g1", b - 1)
                        for n in range(part * NT // G_CUTS, (part + 1) * NT // G_CUTS):
                            for h in range(H):
                                ins = dve.tensor_scalar(G[:, n, h, :], iota_bf[:, :], rank_cur[:, n, h:h + 1], None, ALU.is_equal)
                        if part == G_CUTS - 1:
                            ins.then_inc(g_ready, 1)
                    return go

                def slot_rows(b, pb):
                    dve.wait_ge(rank_loaded, 16 * b + 16)
                    dve.wait_ge(d_done, d_count("sc", b - 1))
                    for jt in range(2):
                        ins = dve.tensor_scalar(GT[:, jt, :], rank_bc[:, :], slot_id[:, jt:jt + 1], None, ALU.is_equal)
                    ins.then_inc(gt_ready, 1)

                def take_k(b, pb):
                    await_a(dve, a_done, "k", b)
                    await_count(dve, reduced["k"], 2 * b - 1)
                    dve.tensor_tensor(kf[:, :, :].rearrange("p (a n h) d -> p a n (h d)", a=2, n=3), two_of_three(a_tile("k"), D),
                                      kvb[:, 0:D].unsqueeze(1).unsqueeze(1).to_broadcast([TT, 2, 3, D]), ALU.add)\
                       .then_inc(a_free[a_slot("k")], 1)

                def take_v(b, pb):
                    await_a(dve, a_done, "v", b)
                    await_count(dve, pv_done[1], b)
                    for a in range(2):
                        for odd in range(2):
                            ins = dve.tensor_tensor(
                                v_pad[:, 3 * a:3 * a + 3, odd:H:2, HD * odd:HD * odd + HD],
                                a_tile("v")[0:TT, a, 0:3 * D].rearrange("p (n h d) -> p n h d", n=3, h=H)[:, :, odd:H:2, :],
                                kvb[:, D:2 * D].rearrange("p (h d) -> p h d", h=H)[:, odd:H:2, :].unsqueeze(1)
                                .to_broadcast([TT, 3, H // 2, HD]), ALU.add)
                    ins.then_inc(a_free[a_slot("v")], 1)

                def take_kT(i):
                    def go(b, pb):
                        await_a(dve, a_done, f"kt{i}", b)
                        dve.tensor_copy(kT[0:KR, 2 * i:2 * i + 2, :].rearrange("p g (n c) -> p g n c", n=NT), turned_k(i))\
                           .then_inc(a_free[a_slot(f"kt{i}")], 1)
                    return go

                def take_max(i):
                    def go(b, pb):
                        await_a(dve, a_done, f"max{i}", b)
                        dve.tensor_reduce(mx[:, i:i + 1], a_tile(f"max{i}")[0:JT, :, 0:HALF], AX.XY, ALU.max)\
                           .then_inc(a_free[a_slot(f"max{i}")], 1)
                    return go

                def max_parts(b, pb):
                    await_a(dve, a_free, f"max{2 * H - 2}", b)
                    await_a(dve, a_free, f"max{2 * H - 1}", b)
                    dve.tensor_copy(mxp[:, 0, :], mx[:, :]).then_inc(mx_step, 1)
                    dve.wait_ge(mx_step, 3 * b + 1)
                    dve.tensor_tensor(mx_rest[:, :], mx[:, :], mxp[:, 0, :], ALU.subtract).then_inc(mx_step, 1)
                    dve.wait_ge(mx_step, 3 * b + 2)
                    dve.tensor_copy(mxp[:, 1, :], mx_rest[:, :]).then_inc(mx_step, 1)
                    dve.wait_ge(mx_step, 3 * b + 3)
                    dve.tensor_tensor(mxp[:, 2, :], mx_rest[:, :], mxp[:, 1, :], ALU.subtract).then_inc(mxp_ready, 1)

                def take_max_rows(b, pb):
                    await_a(dve, a_done, "mt", b)
                    dve.tensor_copy(mxT[:, :], a_tile("mt")[0:6 * H, 0, 0:JT // 2].bitcast(BF16)).then_inc(mxT_ready, 1)
                    dve.wait_ge(mxT_ready, b + 1)
                    dve.sem_inc(a_free[a_slot("mt")], 1)

                def take_att(b, pb):
                    dve.wait_ge(at_done, b + 1)
                    at = at_ps[0:JT, :].rearrange("p (s g d) -> p s g d", s=4, g=4)
                    to = att[:, :].rearrange("p (s g d) -> p s g d", s=4, g=4)
                    for odd in range(2):
                        dve.reciprocal(rden[:, :, odd:4:2], at[:, :, odd:4:2, HD * (1 - odd)]).then_inc(att_step, 1)
                    dve.wait_ge(att_step, 7 * b + 2)
                    for odd in range(2):
                        half = slice(HD * odd, HD * odd + HD)
                        dve.tensor_tensor(to[:, :, odd:4:2, half], at[:, :, odd:4:2, half],
                                          rden[:, :, odd:4:2].unsqueeze(3).to_broadcast([JT, 4, 2, HD]), ALU.mult)\
                           .then_inc(att_step, 1)
                    dve.wait_ge(att_step, 7 * b + 4)
                    dve.tensor_copy(attp[:, 0, :], att[:, :]).then_inc(att_step, 1)
                    dve.wait_ge(att_step, 7 * b + 5)
                    dve.tensor_tensor(att_rest[:, :], att[:, :], attp[:, 0, :], ALU.subtract).then_inc(att_step, 1)
                    dve.wait_ge(att_step, 7 * b + 6)
                    dve.tensor_copy(attp[:, 1, :], att_rest[:, :]).then_inc(att_step, 1)
                    dve.wait_ge(att_step, 7 * b + 7)
                    dve.tensor_tensor(attp[:, 2, :], att_rest[:, :], attp[:, 1, :], ALU.subtract).then_inc(attp_ready, 1)

                def copy_parts(x, st, first, second):
                    def go(b, pb):
                        dve.wait_ge(rounded[x], 2 * b + 2)
                        for src, places in (first, second):
                            for to in places:
                                ins = dve.tensor_copy(st[:, :, to, :], st[:, :, src, :])
                        ins.then_inc(copied[x], 1)
                    return go

                def residual1(b, pb):
                    dve.wait_ge(d_free, d_count("o", b))
                    dve.tensor_tensor(r[:, :], ao[:, :], xT[pb][:, :], ALU.add).then_inc(r_ready, 1)

                def norm1(b, pb):
                    dve.wait_ge(rstd_ready, 2 * b + 1)
                    dve.tensor_tensor(cS[:, :], cS[:, :], sq[:, :], ALU.mult).then_inc(ln_step, 1)
                    dve.wait_ge(ln_step, 2 * b + 1)
                    dve.tensor_scalar(h1[:, :], cS[:, :], col("ln1_g"), col("ln1_b"), ALU.mult, ALU.add).then_inc(h1_ready, 1)

                def take_f(i):
                    def go(b, pb):
                        dve.wait_ge(d_done, d_count(f"f{i}", b))
                        dve.tensor_scalar(two(rl[:, i, :]), d_ps[:, :, 0:HALF], col(f"f1_b{i}"), 0.0, ALU.add, ALU.max)\
                           .then_inc(d_free, 1)
                    return go

                def residual2(b, pb):
                    dve.wait_ge(d_done, d_count("ff", b))
                    dve.scalar_tensor_tensor(two(r[:, :]), d_ps[:, :, 0:HALF], col("f2_b"), two(h1[:, :]), ALU.add, ALU.add)\
                       .then_inc(d_free, 1)
                    dve.wait_ge(d_free, d_count("ff", b))
                    dve.sem_inc(r_ready, 1)

                def norm2(b, pb):
                    dve.wait_ge(rstd_ready, 2 * b + 2)
                    dve.tensor_tensor(cS[:, :], cS[:, :], sq[:, :], ALU.mult).then_inc(ln_step, 1)
                    dve.wait_ge(ln_step, 2 * b + 2)
                    dve.wait_ge(aob_ready, b + 1)
                    dve.scalar_tensor_tensor(fu[:, 1:L + 1], cS[:, :], col("ln2_g"), aob[:, :], ALU.mult, ALU.add)\
                       .then_inc(fu_ready, 1)

                def pool_pairs(b, pb):
                    dve.wait_ge(d_done, d_count("cv", b))
                    n = (HALF + 1) // 2
                    dve.tensor_reduce(hp[:, 0:n], d_ps[:, 0, 0:2 * n].rearrange("p (s w) -> p s w", w=2), AX.X, ALU.max)\
                       .then_inc(hp_ready, 1)
                    dve.tensor_reduce(hp[:, n:S], d_ps[:, 1, 0:2 * (S - n)].rearrange("p (s w) -> p s w", w=2), AX.X, ALU.max)\
                       .then_inc(hp_ready, 1)
                    dve.wait_ge(hp_ready, 2 * b + 2)
                    dve.sem_inc(d_free, 1)

                part_p = {"k": take_k, "v_pad": take_v, "q_copy": copy_parts("q", qst, (0, [1, 2]), (3, [4])),
                          "k_copy": copy_parts("k", kst, (0, [3, 5]), (1, [4]))}
                for i in range(G_CUTS):
                    part_p[f"hot{i}"] = one_hots(i)
                part_a = {"gt": slot_rows, "mp": max_parts, "mt": take_max_rows}
                for i in range(4):
                    if i not in ACT_KT:
                        part_a[f"kt{i}"] = take_kT(i)
                for i in range(2 * H):
                    part_a[f"max{i}"] = take_max(i)
                part_d = {"at": take_att, "r1": residual1, "n1": norm1, "r2": residual2, "n2": norm2, "cv": pool_pairs}
                for i in range(4):
                    if i not in ACT_F:
                        part_d[f"f{i}"] = take_f(i)
                def hand_on(name, b):
                    if name == "k":
                        await_a(dve, a_done, name, b)
                        dve.sem_inc(a_free[a_slot(name)], 1)

                run(dve, part_p, part_a, part_d, hand_on)


N_CONST = 12


ACT_KT = ()
ACT_F = (0, 1, 2, 3)
G_CUTS = 6


def order():
    text = """A.kt0 D.at A.kt1 D.sc P.load A.kt2 A.kt3 D.o A.g0 A.g1 D.r1 D.c1 A.max0 A.max1 D.m1 A.max2 A.max3
        D.n1 D.f0 A.max4 A.max5 D.f1 A.max6 A.max7 P.q_first P.q_rest D.f2 A.max8 A.max9 P.q_second P.q_third
        P.hot0 D.f3 A.max10 A.max11 A.max12 A.max13 A.max14 A.max15
        A.mp P.hot1 P.hot2 D.ff D.r2 A.mt D.c2 P.xT D.m2 P.k P.k_first P.k_rest P.q_copy D.n2 P.k_second P.k_third A.s0 A.s1 D.cv P.k_copy P.hot3 P.hot4
        A.s2 A.s3 A.s4 A.s5 A.pv0 P.hot5 A.gt P.ranks
        D.relu D.ht A.s6 A.s7 P.v A.pv1 P.v_pad A.au"""
    return [tuple(s.split(".")) for s in text.split()]


def tanh_attention(nc, t, io):
    BUFS = 4
    with ExitStack() as ctx:
        def sb(name, shape, dt=F32):
            return ctx.enter_context(nc.sbuf_tensor(name, shape, dt))

        def sem(name):
            return ctx.enter_context(nc.semaphore(name))

        aw = sb("attention_w", [D, D])
        wr = sb("router_w", [D, E])
        brc = sb("router_b_rows", [TT, E])
        minus_half = sb("minus_half", [TT, ST])
        h_in = [sb(f"h_in{p}", [TT, ST, D]) for p in range(BUFS)]
        z = [sb(f"z{p}", [TT, ST, D + 1]) for p in range(BUFS)]
        rows = [sb(f"rows{p}", [TT, ST, 2 * D]) for p in range(BUFS)]
        zero_row = sb("zero_row", [1, 2 * D])
        stats = [sb(f"ln_stats{k}", [TT, ST, 6]) for k in range(2)]
        mv = [sb(f"ln_mv{k}", [TT, ST, 2]) for k in range(2)]
        ve = [sb(f"ln_ve{k}", [TT, ST]) for k in range(2)]
        rs = [sb(f"ln_rs{k}", [TT, ST]) for k in range(2)]
        zT = sb("zT", [D, S])
        pT = sb("pT", [D, S])
        th = sb("tanh_s", [TT, ST, S])
        ex = [sb(f"exp_s{p}", [TT, ST, S]) for p in range(2)]
        rden = sb("rden4", [TT, ST])
        uT = sb("uT4", [D, S])
        zT_ps = ctx.enter_context(nc.psum_tensor("zT_ps", [128, 512], F32))
        pT_ps = ctx.enter_context(nc.psum_tensor("pT_ps", [128, 512], F32))
        s_ps = ctx.enter_context(nc.psum_tensor("s_ps", [128, ST, 512], F32))
        o_ps = ctx.enter_context(nc.psum_tensor("o_ps4", [128, 512], F32))
        uT_ps = ctx.enter_context(nc.psum_tensor("uT_ps", [128, 512], F32))
        l_ps = ctx.enter_context(nc.psum_tensor("l_ps", [128, 512], F32))

        names = ["w4", "set4", "zT_done", "zT_ready", "pT_done", "pT_ready", "s_done", "th_ready", "ex_ready", "o_done",
                 "rden_ready", "hh_ready", "uT_done", "uT_ready", "l_done", "l_ready"]
        w4, set4, zT_done, zT_ready, pT_done, pT_ready, s_done, th_ready, ex_ready, o_done, rden_ready, hh_ready, uT_done, \
            uT_ready, l_done, l_ready = [sem(n) for n in names]
        gate4 = sem("gate4")
        h_loaded = [sem(f"h_loaded4{p}") for p in range(BUFS)]
        st_ready = [sem(f"st_ready{k}") for k in range(2)]
        mv_ready = [sem(f"mv_ready{k}") for k in range(2)]
        ve_ready = [sem(f"ve_ready{k}") for k in range(2)]
        rs_ready = [sem(f"rs_ready{k}") for k in range(2)]
        n_ready = [sem(f"n_ready4{k}") for k in range(2)]
        rows_stored = [sem(f"rows_stored{p}") for p in range(BUFS)]
        zero_made = sem("zero_made")
        logits = t["logits"]
        rows_v = io["token_rows"][1:1 + NB * S, :].rearrange("(b n p) d -> b p n d", n=ST, p=TT)

        def run(eng, steps):
            def round_of(r, i=0):
                for lead, step in steps:
                    b = r + lead
                    if not isinstance(i, int) or 0 <= b < NB:
                        step(BUFS * i + b, b % BUFS, i + b // BUFS)
            for r in range(-3, 1):
                round_of(r)
            with eng.Fori(0, (NB - BUFS) // BUFS) as i:
                for r in range(1, 1 + BUFS):
                    round_of(r, i)
            for r in range(NB - BUFS + 1, NB + 1):
                round_of(r)

        def before(eng, semaphore, count):
            if not isinstance(count, int) or count > 0:
                eng.wait_ge(semaphore, count)

        with nc.Block() as block:
            @block.sync
            def _(sp):
                sp.dma_start(aw[:, :], io["L0_attn_attention_weights"]).then_inc(w4, 16)
                sp.dma_start(wr[:, :], io["L0_ffn_Wr"]).then_inc(w4, 16)
                sp.dma_start(brc[:, :], io["L0_ffn_br"].rearrange("(a n) -> a n", a=1).to_broadcast([TT, E])).then_inc(w4, 16)

                def load(b, p, j):
                    before(sp, hh_ready, ST * (b - BUFS + 1))
                    sp.dma_start(h_in[p][:, :, :].rearrange("p n d -> p (n d)"),
                                 io["h_rows"][bass.ds(b, 1), :, :].rearrange("b p n -> (b p) n")).then_inc(h_loaded[p], 16)

                def store(b, p, j):
                    sp.wait_ge(n_ready[1], b + 1)
                    sp.dma_start(rows_v[bass.ds(b, 1), :, :, :].rearrange("b p n d -> (b p) n d"), rows[p][:, :, :]).then_inc(rows_stored[p], 16)

                sp.wait_ge(zero_made, 1)
                sp.dma_start(io["token_rows"][0:1, :], zero_row[:, :]).then_inc(zero_made, 16)
                for p in range(BUFS):
                    sp.sem_inc(rows_stored[p], 16)
                run(sp, [(3, load), (0, store)])
                sp.wait_ge(zero_made, 17)
                for p in range(BUFS):
                    sp.wait_ge(rows_stored[p], 16 * (NB // BUFS) + 16)

            @block.gpsimd
            def _(pool):
                for dst, src in ((t["w1"][:, :, :], io["L0_ffn_W1"].rearrange("e d h -> d e h")),
                                 (t["w2"][:, :, :], io["L0_ffn_W2"].rearrange("e (c p) d -> p (e c) d", p=128)),
                                 (t["b1"][:, :], io["L0_ffn_b1"].rearrange("(a e) h -> a (e h)", a=1).to_broadcast([128, E * EH])),
                                 (t["b2"][:, :], io["L0_ffn_b2"].rearrange("(a e) d -> a (e d)", a=1).to_broadcast([128, E * D]))):
                    pool.dma_start(dst, src).then_inc(t["experts_loaded"], 16)
                pool.memset(zero_row[:, :], 0.0).then_inc(zero_made, 1)
                pool.memset(minus_half[:, :], -0.5).then_inc(set4, 1)
                pool.wait_ge(set4, 1)

                def power(k):
                    def go(b, p, j):
                        pool.wait_ge(ve_ready[k], b + 1)
                        pool.tensor_tensor(rs[k][:, :], ve[k][:, :], minus_half[:, :], ALU.pow).then_inc(rs_ready[k], 1)
                    return go

                run(pool, [(2, power(0)), (0, power(1))])

            @block.tensor
            def _(pe):
                pe.wait_ge(w4, 48)

                def turn_z(b, p, j):
                    pe.wait_ge(n_ready[0], b + 1)
                    for n in range(ST):
                        mm = pe.transpose(zT_ps[:, n * TT:(n + 1) * TT], z[p][:, n, 0:D], t["ident"][0:TT, 0:TT])
                    mm.then_inc(zT_done, 1)

                def project(b, p, j):
                    pe.wait_ge(zT_ready, b + 1)
                    pe.matmul(pT_ps[:, 0:S], aw[:, :], zT[:, :], start=True, stop=True).then_inc(pT_done, 1)

                def scores(b, p, j):
                    pe.wait_ge(pT_ready, b + 1)
                    before(pe, th_ready, b)
                    for n in range(ST):
                        mm = pe.matmul(s_ps[0:TT, n, 0:S], zT[:, n * TT:(n + 1) * TT], pT[:, :], start=True, stop=True)
                    mm.then_inc(s_done, 1)

                def attend(b, p, j):
                    pe.wait_ge(ex_ready, b + 1)
                    before(pe, hh_ready, ST * b)
                    for m in range(ST):
                        for n in range(ST):
                            mm = pe.matmul(o_ps[0:TT, m * (D + 1):(m + 1) * (D + 1)], ex[p % 2][:, n, m * TT:(m + 1) * TT],
                                           z[p][:, n, :], start=(n == 0), stop=(n == ST - 1))
                    mm.then_inc(o_done, 1)

                def turn_u(b, p, j):
                    pe.wait_ge(n_ready[1], b + 1)
                    for n in range(ST):
                        mm = pe.transpose(uT_ps[:, n * TT:(n + 1) * TT], rows[p][:, n, 0:D], t["ident"][0:TT, 0:TT])
                    mm.then_inc(uT_done, 1)

                def router(b, p, j):
                    pe.wait_ge(uT_ready, b + 1)
                    pe.wait_ge(l_ready, b + 1)
                    for n in range(ST):
                        mm = pe.matmul(l_ps[0:TT, n * E:(n + 1) * E], uT[:, n * TT:(n + 1) * TT], wr[:, :], start=True, stop=True)
                    mm.then_inc(l_done, 1)

                run(pe, [(1, turn_z), (1, project), (0, attend), (-1, turn_u), (1, scores), (-1, router)])

            @block.scalar
            def _(act):
                def take_z(b, p, j):
                    act.wait_ge(zT_done, b + 1)
                    act.activation(zT[:, :], zT_ps[:, 0:S], ACT.Copy).then_inc(zT_ready, 1)

                def exps(b, p, j):
                    act.wait_ge(s_done, b + 1)
                    act.activation(th[:, :, :], s_ps[0:TT, :, 0:S], ACT.Tanh).then_inc(th_ready, 1)
                    act.wait_ge(th_ready, b + 1)
                    act.activation(ex[p % 2][:, :, :], th[:, :, :], ACT.Exp).then_inc(ex_ready, 1)

                def take_u(b, p, j):
                    act.wait_ge(uT_done, b + 1)
                    act.activation(uT[:, :], uT_ps[:, 0:S], ACT.Copy).then_inc(uT_ready, 1)

                run(act, [(1, take_z), (-1, take_u), (1, exps)])

            @block.vector
            def _(dve):
                for p in range(BUFS):
                    dve.memset(z[p][:, :, D:D + 1], 1.0).then_inc(t["z_set"], 1)
                dve.sem_inc(l_ready, 1)
                dve.wait_ge(t["z_set"], BUFS)
                dve.wait_ge(w4, 48)

                def variance(k, src, b):
                    for n in range(ST):
                        dve.bn_stats(stats[k][:, n, :], src(n)).then_inc(st_ready[k], 1)
                    dve.wait_ge(st_ready[k], ST * b + ST)
                    dve.sem_inc(gate4, 1)
                    for n in range(ST):
                        dve.bn_aggr(mv[k][:, n, :], stats[k][:, n, :]).then_inc(mv_ready[k], 1)
                    dve.wait_ge(mv_ready[k], ST * b + ST)
                    dve.tensor_scalar(ve[k][:, :], mv[k][:, :, 1], EPS, None, ALU.add).then_inc(ve_ready[k], 1)

                def normalize(k, src, dst, b):
                    dve.wait_ge(rs_ready[k], b + 1)
                    for n in range(ST):
                        ins = dve.tensor_scalar(dst(n), src(n), mv[k][:, n, 0:1], rs[k][:, n:n + 1], ALU.subtract, ALU.mult)
                    ins.then_inc(n_ready[k], 1)

                def h_variance(b, p, j):
                    dve.wait_ge(h_loaded[p], 16 * j + 16)
                    variance(0, lambda n: h_in[p][:, n, :], b)

                def z_rows(b, p, j):
                    normalize(0, lambda n: h_in[p][:, n, :], lambda n: z[p][:, n, 0:D], b)

                def take_p(b, p, j):
                    dve.wait_ge(pT_done, b + 1)
                    dve.tensor_copy(pT[:, :], pT_ps[:, 0:S]).then_inc(pT_ready, 1)

                def residual(b, p, j):
                    dve.wait_ge(o_done, b + 1)
                    o = o_ps[0:TT, 0:ST * (D + 1)].rearrange("p (n d) -> p n d", n=ST)
                    dve.reciprocal(rden[:, :], o[:, :, D]).then_inc(rden_ready, 1)
                    dve.wait_ge(rden_ready, b + 1)
                    dve.wait_ge(rows_stored[p], 16 * j + 16)
                    for n in range(ST):
                        dve.scalar_tensor_tensor(rows[p][:, n, D:2 * D], o[:, n, 0:D], rden[:, n:n + 1], h_in[p][:, n, :], ALU.mult, ALU.add)\
                            .then_inc(hh_ready, 1)
                    dve.wait_ge(hh_ready, ST * b + ST)
                    variance(1, lambda n: rows[p][:, n, D:2 * D], b)

                def u_rows(b, p, j):
                    normalize(1, lambda n: rows[p][:, n, D:2 * D], lambda n: rows[p][:, n, 0:D], b)

                def take_logits(b, p, j):
                    dve.wait_ge(l_done, b + 1)
                    dve.tensor_tensor(logits[:, bass.ds(b * ST, ST), :], l_ps[0:TT, 0:ST * E].rearrange("p (n e) -> p n e", n=ST),
                                      brc[:, :].unsqueeze(1).to_broadcast([TT, ST, E]), ALU.add).then_inc(l_ready, 1)

                run(dve, [(2, h_variance), (1, take_p), (2, z_rows), (0, residual), (-1, take_logits), (0, u_rows)])


def route(nc, t, io):
    with ExitStack() as ctx:
        def sb(name, shape, dt=F32):
            return ctx.enter_context(nc.sbuf_tensor(name, shape, dt))

        def sem(name):
            return ctx.enter_context(nc.semaphore(name))

        top = sb("top_logit", [TT, NTILE])
        hot = sb("hot", [TT, NTILE, E])
        pick = sb("pick", [TT, NTILE, E])
        best = sb("best", [TT, NTILE])
        e_id = sb("e_id", [TT, E])
        upper = sb("upper", [TT, TT])
        ones = sb("ones5", [TT, TT])
        ones_t = sb("ones_t", [TT, NTILE])
        total = sb("total", [TT, NTILE, E])
        cum = sb("cum", [TT, E, NTILE])
        blk_row = sb("blk_row", [TT, NBLK])
        full = sb("full", [TT, E, NBLK])
        nblk = sb("nblk", [TT, E])
        bend = sb("bend", [TT, E])
        bstart = sb("bstart", [TT, E])
        past = sb("past", [TT, NBLK, E])
        owner = sb("owner", [TT, NBLK])
        slot = sb("slot_f", [TT, NTILE])
        first = sb("first_slot", [TT, NTILE])
        slot_row = sb("slot_row", [TT, BLK])
        row_id = sb("row_id", [TT, NTILE])
        is_slot = sb("is_slot", [TT, NTILE, BLK])
        in_block = sb("in_block", [TT, NTILE, 2, NBLK])
        rows_f = sb("rows_f", [BLK, NBLK])
        dest_f = sb("dest_f", [BLK, NBLK])
        gate = sb("gate_tok", [TT, NTILE])
        i_ps = ctx.enter_context(nc.psum_tensor("i_ps", [128, 512], F32))
        p_ps = ctx.enter_context(nc.psum_tensor("p_ps", [128, 512], F32))
        t_ps = ctx.enter_context(nc.psum_tensor("t_ps", [128, 512], F32))
        const5 = sem("const5")
        hot_ready = sem("hot_ready")
        counted = sem("counted")
        diff_ready = sem("diff_ready")
        gate_exp = sem("gate_exp")
        step5 = sem("step5")
        hot_slots = sem("hot_slots")
        inverted = sem("inverted")

        with nc.Block() as block:
            @block.sync
            def _(sp):
                sp.dma_start(e_id[:, :], io["c_e_id"].to_broadcast([TT, E])).then_inc(const5, 16)
                sp.dma_start(upper[:, :], io["c_upper"]).then_inc(const5, 16)
                sp.dma_start(blk_row[:, :], io["c_blk"].to_broadcast([TT, NBLK])).then_inc(const5, 16)
                sp.dma_start(slot_row[:, :], io["c_slot_row"].to_broadcast([TT, BLK])).then_inc(const5, 16)
                sp.dma_start(row_id[:, :], io["c_row_id"]).then_inc(const5, 16)

            @block.scalar
            def _(act):
                act.wait_ge(diff_ready, 1)
                act.activation(gate[:, :], best[:, :], ACT.Exp).then_inc(gate_exp, 1)

            @block.tensor
            def _(pe):
                pe.wait_ge(const5, 80)
                pe.wait_ge(hot_ready, 1)
                m = hot[:, :, :].rearrange("p t e -> p (t e)")
                pe.matmul(p_ps[0:TT, 0:NTILE * E], upper[:, :], m, start=True, stop=True)
                pe.matmul(t_ps[0:TT, 0:NTILE * E], ones[:, :], m, start=True, stop=True).then_inc(counted, 1)
                for n in range(NTILE):
                    if n % (NTILE // CUTS) == 0:
                        pe.wait_ge(hot_slots, n // (NTILE // CUTS) + 1)
                    mm = pe.matmul(i_ps[0:BLK, 0:2 * NBLK], is_slot[:, n, :], in_block[:, n, :, :].rearrange("p a j -> p (a j)"),
                                   start=(n == 0), stop=(n == NTILE - 1))
                mm.then_inc(inverted, 1)

            @block.vector
            def _(dve):
                n_step = [0]

                def chain(ins):
                    n_step[0] += 1
                    ins.then_inc(step5, 1)
                    dve.wait_ge(step5, n_step[0])

                def tiles(ap):
                    return ap.unsqueeze(2).to_broadcast([TT, NTILE, E])

                def experts(ap, n=NTILE):
                    return ap.unsqueeze(1).to_broadcast([TT, n, E])

                chain(dve.memset(ones[:, :], 1.0))
                chain(dve.memset(ones_t[:, :], 1.0))
                dve.wait_ge(const5, 80)
                chain(dve.tensor_reduce(top[:, :], t["logits"][:, :, :], AX.X, ALU.max))
                dve.tensor_tensor(best[:, :], top[:, :], top[:, :], ALU.subtract).then_inc(diff_ready, 1)
                dve.wait_ge(gate_exp, 1)
                chain(dve.reciprocal(best[:, :], gate[:, :]))
                chain(dve.tensor_tensor(gate[:, :], gate[:, :], best[:, :], ALU.mult))
                chain(dve.tensor_tensor(pick[:, :, :], t["logits"][:, :, :], tiles(top[:, :]), ALU.is_equal))
                chain(dve.tensor_tensor(pick[:, :, :], pick[:, :, :], experts(e_id[:, :]), ALU.mult))
                chain(dve.tensor_reduce(best[:, :], pick[:, :, :], AX.X, ALU.max))
                dve.tensor_tensor(hot[:, :, :], experts(e_id[:, :]), tiles(best[:, :]), ALU.is_equal).then_inc(hot_ready, 1)
                dve.wait_ge(counted, 1)
                chain(dve.tensor_copy(total[:, :, :].rearrange("p t e -> p (t e)"), t_ps[0:TT, 0:NTILE * E]))
                for e in range(E):
                    chain(dve.tensor_tensor_scan(cum[:, e, :], ones_t[:, :], total[:, :, e], 0.0, ALU.mult, ALU.add))
                chain(dve.tensor_scalar(full[:, 0, :], blk_row[:, :], float(BLK), None, ALU.mult))
                chain(dve.tensor_copy(owner[:, :], full[:, 0, :]))
                chain(dve.tensor_tensor(full[:, :, :], cum[:, :, NTILE - 1:NTILE].to_broadcast([TT, E, NBLK]),
                                        owner[:, :].unsqueeze(1).to_broadcast([TT, E, NBLK]), ALU.is_gt))
                chain(dve.tensor_reduce(nblk[:, :], full[:, :, :], AX.X, ALU.add))
                chain(dve.tensor_tensor_scan(bend[:, :], ones_t[:, 0:E], nblk[:, :], 0.0, ALU.mult, ALU.add))
                chain(dve.tensor_tensor(bstart[:, :], bend[:, :], nblk[:, :], ALU.subtract))
                chain(dve.tensor_scalar(bstart[:, :], bstart[:, :], float(BLK), None, ALU.mult))
                chain(dve.tensor_tensor(past[:, :, :], blk_row[:, :].unsqueeze(2).to_broadcast([TT, NBLK, E]),
                                        experts(bend[:, :], NBLK), ALU.is_ge))
                chain(dve.tensor_reduce(owner[:, :], past[:, :, :], AX.X, ALU.add))
                chain(dve.tensor_scalar(t["block_expert"][:, :], owner[:, :], float(E - 1), None, ALU.min))
                chain(dve.tensor_tensor(pick[:, :, :], cum[:, :, :].rearrange("p e t -> p t e"), total[:, :, :], ALU.subtract))
                chain(dve.tensor_tensor(pick[:, :, :], pick[:, :, :], experts(bstart[:, :]), ALU.add))
                chain(dve.tensor_tensor(pick[:, :, :], pick[:, :, :], p_ps[0:TT, 0:NTILE * E].rearrange("p (t e) -> p t e", e=E),
                                        ALU.add))
                chain(dve.tensor_tensor(pick[:, :, :], pick[:, :, :], hot[:, :, :], ALU.mult))
                chain(dve.tensor_reduce(slot[:, :], pick[:, :, :], AX.X, ALU.add))
                chain(dve.tensor_scalar(first[:, :], slot[:, :], 1.0 / BLK, -0.5 + 0.5 / BLK, ALU.mult, ALU.add))
                chain(dve.tensor_scalar(first[:, :], first[:, :], ROUNDER, None, ALU.add))
                chain(dve.tensor_scalar(first[:, :], first[:, :], -ROUNDER, float(BLK), ALU.add, ALU.mult))
                chain(dve.tensor_tensor(slot[:, :], slot[:, :], first[:, :], ALU.subtract))
                chain(dve.tensor_scalar(blk_row[:, :], blk_row[:, :], float(BLK), None, ALU.mult))
                for c in range(CUTS):
                    n = NTILE // CUTS
                    at = slice(c * n, (c + 1) * n)
                    dve.tensor_tensor(is_slot[:, at, :], slot_row[:, :].unsqueeze(1).to_broadcast([TT, n, BLK]),
                                      slot[:, at].unsqueeze(2).to_broadcast([TT, n, BLK]), ALU.is_equal)
                    chain(dve.tensor_tensor(in_block[:, at, 0, :], blk_row[:, :].unsqueeze(1).to_broadcast([TT, n, NBLK]),
                                            first[:, at].unsqueeze(2).to_broadcast([TT, n, NBLK]), ALU.is_equal))
                    dve.tensor_tensor(in_block[:, at, 1, :], in_block[:, at, 0, :],
                                      gate[:, at].unsqueeze(2).to_broadcast([TT, n, NBLK]), ALU.mult)
                    dve.tensor_tensor(in_block[:, at, 0, :], in_block[:, at, 0, :],
                                      row_id[:, at].unsqueeze(2).to_broadcast([TT, n, NBLK]), ALU.mult).then_inc(hot_slots, 1)
                dve.wait_ge(inverted, 1)
                chain(dve.tensor_copy(rows_f[:, :], i_ps[0:BLK, 0:NBLK]))
                dve.tensor_copy(t["gate"][:, :], i_ps[0:BLK, NBLK:2 * NBLK])
                dve.tensor_copy(t["row"][:, :], rows_f[:, :])
                chain(dve.tensor_scalar(dest_f[:, :], rows_f[:, :], 0.0, float(2 * NB * S), ALU.is_equal, ALU.mult))
                chain(dve.tensor_tensor(dest_f[:, :], dest_f[:, :], rows_f[:, :], ALU.add))
                dve.tensor_scalar(t["dest"][:, :], dest_f[:, :], -1.0, None, ALU.add)


def experts(nc, t, io):
    NC = EH // 128
    BODY = 6
    UB, OB = BODY, 3
    AHEAD = 4
    assert NBLK % BODY == 0
    with ExitStack() as ctx:
        def sb(name, shape, dt=F32):
            return ctx.enter_context(nc.sbuf_tensor(name, shape, dt))

        def sem(name):
            return ctx.enter_context(nc.semaphore(name))

        w1, w2, b1, b2 = t["w1"], t["w2"], t["b1"], t["b2"]
        rows = [sb(f"block_rows{p}", [BLK, 2 * D]) for p in range(UB)]
        uT = [sb(f"uT_block{p}", [D, BLK]) for p in range(2)]
        hb = [sb(f"h_block{p}", [BLK, EH]) for p in range(2)]
        hT = [sb(f"hT_block{p}", [128, NC, BLK]) for p in range(2)]
        ob = sb("o_block", [BLK, D])
        gated = sb("gated_block", [BLK, D])
        res = [sb(f"result{p}", [BLK, D]) for p in range(OB)]
        uT_ps = [ctx.enter_context(nc.psum_tensor(f"uTb_ps{p}", [128, 512], F32)) for p in range(2)]
        h_ps = [ctx.enter_context(nc.psum_tensor(f"h_ps{p}", [128, 512], F32)) for p in range(2)]
        hT_ps = [ctx.enter_context(nc.psum_tensor(f"hT_ps{p}", [128, 512], F32)) for p in range(2)]
        o_ps = [ctx.enter_context(nc.psum_tensor(f"ob_ps{p}", [128, 512], F32)) for p in range(2)]
        gathered = [sem(f"gathered{p}") for p in range(UB)]
        u_turned = sem("u_turned6")
        uT_ready = sem("uT_ready6")
        h_done = sem("h_done6")
        h_ready = sem("h_ready6")
        h_turned = sem("h_turned6")
        hT_ready = sem("hT_ready6")
        o_done = sem("o_done6")
        o_ready = sem("o_ready6")
        gated_ready = sem("gated_ready6")
        res_ready = sem("res_ready6")
        scattered = [sem(f"scattered{p}") for p in range(OB)]

        def run(eng, steps):
            def round_of(r, i=0):
                for lead, step in steps:
                    j = r + lead
                    if not isinstance(i, int) or 0 <= j < NBLK:
                        step(BODY * i + j, j % BODY, i + j // BODY)
            for r in range(-AHEAD, OB):
                round_of(r)
            with eng.Fori(0, NBLK // BODY - 1) as i:
                for r in range(OB, OB + BODY):
                    round_of(r, i)
            for r in range(OB + NBLK - BODY, NBLK + 1):
                round_of(r)

        def before(eng, semaphore, count):
            if not isinstance(count, int) or count > 0:
                eng.wait_ge(semaphore, count)

        def expert(eng, j):
            return eng.value_load(t["block_expert"][0:1, bass.ds(j, 1)], min_val=0, max_val=E - 1)

        out_rows = io["out"].rearrange("b s d -> (b s) d")

        with nc.Block() as block:
            @block.gpsimd
            def _(pool):
                for r in range(-AHEAD, NBLK):
                    j = r + AHEAD
                    if j < NBLK:
                        before(pool, res_ready, j - UB + 1)
                        pool.indirect_dma_start(out=rows[j % UB][:, :], out_offset=None, in_=io["token_rows"],
                                                in_offset=bass.IndirectOffsetOnAxis(ap=t["row"][:, j:j + 1], axis=0))\
                            .then_inc(gathered[j % UB], 16)
                    if r >= 0:
                        pool.wait_ge(res_ready, r + 1)
                        pool.indirect_dma_start(out=out_rows, out_offset=bass.IndirectOffsetOnAxis(ap=t["dest"][:, r:r + 1], axis=0),
                                                in_=res[r % OB][:, :], in_offset=None, bounds_check=NB * S - 1, oob_is_err=False)\
                            .then_inc(scattered[r % OB], 16)
                for p in range(OB):
                    pool.wait_ge(scattered[p], 16 * (NBLK // OB))

            @block.tensor
            def _(pe):
                pe.wait_ge(t["experts_loaded"], 64)

                def turn_u(j, k, m):
                    pe.wait_ge(gathered[k], 16 * m + 16)
                    pe.transpose(uT_ps[k % 2][:, 0:BLK], rows[k][:, 0:D], t["ident"][:, :]).then_inc(u_turned, 1)

                def up(j, k, m):
                    e = expert(pe, j)
                    pe.wait_ge(uT_ready, j + 1)
                    pe.matmul(h_ps[k % 2][:, :], uT[k % 2][:, :], w1[:, bass.ds(e, 1), :].rearrange("p a h -> p (a h)"),
                              start=True, stop=True).then_inc(h_done, 1)

                def turn_h(j, k, m):
                    pe.wait_ge(h_ready, j + 1)
                    for c in range(NC):
                        mm = pe.transpose(hT_ps[k % 2][:, c * BLK:(c + 1) * BLK], hb[k % 2][:, c * 128:(c + 1) * 128], t["ident"][:, :])
                    mm.then_inc(h_turned, 1)

                def down(j, k, m):
                    e = expert(pe, j)
                    pe.wait_ge(hT_ready, j + 1)
                    before(pe, o_ready, j - 1)
                    for c in range(NC):
                        mm = pe.matmul(o_ps[k % 2][:, 0:D], hT[k % 2][:, c, :], w2[:, bass.ds(e * NC + c, 1), :].rearrange("p a d -> p (a d)"),
                                       start=(c == 0), stop=(c == NC - 1))
                    mm.then_inc(o_done, 1)

                run(pe, [(2, turn_u), (1, up), (0, down), (1, turn_h)])

            @block.scalar
            def _(act):
                def take_u(j, k, m):
                    act.wait_ge(u_turned, j + 1)
                    act.activation(uT[k % 2][:, :], uT_ps[k % 2][:, 0:BLK], ACT.Copy).then_inc(uT_ready, 1)

                def take_h(j, k, m):
                    act.wait_ge(h_turned, j + 1)
                    act.activation(hT[k % 2][:, :, :].rearrange("p c t -> p (c t)"), hT_ps[k % 2][:, :], ACT.Relu).then_inc(hT_ready, 1)

                run(act, [(2, take_u), (1, take_h)])

            @block.vector
            def _(dve):
                dve.wait_ge(t["experts_loaded"], 64)

                def add1(j, k, m):
                    e = expert(dve, j)
                    dve.wait_ge(h_done, j + 1)
                    dve.tensor_tensor(hb[k % 2][:, :], h_ps[k % 2][:, :], b1[:, bass.ds(e * EH, EH)], ALU.add).then_inc(h_ready, 1)

                def add2(j, k, m):
                    e = expert(dve, j)
                    dve.wait_ge(o_done, j + 1)
                    dve.tensor_tensor(ob[:, :], o_ps[k % 2][:, 0:D], b2[:, bass.ds(e * D, D)], ALU.add).then_inc(o_ready, 1)
                    dve.wait_ge(o_ready, j + 1)
                    dve.tensor_tensor(gated[:, :], ob[:, :], t["gate"][:, bass.ds(j, 1)].to_broadcast([BLK, D]), ALU.mult)\
                       .then_inc(gated_ready, 1)
                    dve.wait_ge(gated_ready, j + 1)
                    before(dve, scattered[k % OB], 16 * (BODY // OB * m + k // OB))
                    dve.tensor_tensor(res[k % OB][:, :], gated[:, :], rows[k][:, D:2 * D], ALU.add).then_inc(res_ready, 1)

                run(dve, [(1, add1), (0, add2)])


def audio_tower(nc, io):
    with ExitStack() as ctx:
        def sb(name, shape, dt=F32):
            return ctx.enter_context(nc.sbuf_tensor(name, shape, dt))

        t = {"ident": sb("ident", [128, 128])}
        with nc.sbuf_tensor("rank_tok", [TT, NT, NG], F32) as rank_tok:
            t["rank_tok"] = rank_tok
            norms_and_ranks(nc, t, io)
            sequences(nc, t, io)
        t["z_set"] = ctx.enter_context(nc.semaphore("z_set"))
        t["experts_loaded"] = ctx.enter_context(nc.semaphore("experts_loaded"))
        t["w1"] = sb("w1", [D, E, EH])
        t["w2"] = sb("w2", [128, E * EH // 128, D])
        t["b1"] = sb("b1_rows", [128, E * EH])
        t["b2"] = sb("b2_rows", [128, E * D])
        t["logits"] = sb("logits", [TT, NTILE, E])
        t["row"] = sb("row", [BLK, NBLK], I32)
        t["dest"] = sb("dest", [BLK, NBLK], I32)
        t["gate"] = sb("gate", [BLK, NBLK])
        t["block_expert"] = sb("block_expert", [TT, NBLK], I32)
        tanh_attention(nc, t, io)
        route(nc, t, io)
        experts(nc, t, io)


def constants():
    slot_id = np.arange(NJ, dtype=np.float32)
    slot_id[K_TOP] = -1.0
    slot_id[K_TOP + 1] = -2.0
    return {
        "c_ident": np.eye(128, dtype=np.float32),
        "c_center": (np.eye(D) - 1.0 / D).astype(np.float32),
        "c_iota": np.arange(NJ, dtype=np.float32)[None],
        "c_slot_id": np.ascontiguousarray(slot_id.reshape(2, JT).T),
        "c_e_id": (E - np.arange(E, dtype=np.float32))[None],
        "c_upper": np.triu(np.ones((TT, TT), np.float32), 1),
        "c_blk": np.arange(NBLK, dtype=np.float32)[None],
        "c_slot_row": np.arange(BLK, dtype=np.float32)[None],
        "c_row_id": np.ascontiguousarray(1.0 + np.arange(NTILE * TT, dtype=np.float32).reshape(NTILE, TT).T),
    }


def kernel(**inputs):
    import concourse.bacc as _bacc
    from concourse.bass_utils import run_bass_kernel_spmd as _run

    nc = _bacc.Bacc("TRN2", target_bir_lowering=False, num_devices=1)
    laid = {k: np.ascontiguousarray(v) for k, v in inputs.items()}
    laid["conv_w"] = np.ascontiguousarray(laid.pop("L0_tok_conv_w").transpose(1, 2, 0))
    f1_b = laid.pop("L0_tok_f1_b").reshape(FF // 128, 128)
    laid["cols"] = np.ascontiguousarray(np.stack([laid.pop("L0_tok_" + n) for n in COLS[:7]] + list(f1_b), 1))
    laid.update(constants())
    arrays, io = {}, {}
    for name, a in laid.items():
        arrays[f"in_{name}"] = a
        io[name] = nc.dram_tensor(f"in_{name}", a.shape, mybir.dt.from_np(a.dtype), kind="ExternalInput").ap()
    io["out"] = nc.dram_tensor("out_0", (NB, S, D), F32, kind="ExternalOutput").ap()
    for name, shape, dt in (("q_rows", (NB, TT, NT * D), F32), ("rank_rows", (NG, L), BF16), ("h_rows", (NB, TT, ST * D), F32),
                            ("token_rows", (1 + NB * S, 2 * D), F32)):
        io[name] = nc.dram_tensor(name, shape, dt, kind="Internal").ap()
    audio_tower(nc, io)
    r = _run(nc, [arrays], core_ids=[0])
    return r.results[0]["out_0"]
```

```python
from contextlib import ExitStack

import concourse.bass as bass
from concourse import mybir
import numpy as np

F32 = mybir.dt.float32
BF16 = mybir.dt.bfloat16
I32 = mybir.dt.int32
ALU = mybir.AluOpType
ACT = mybir.ActivationFunctionType
AX = mybir.AxisListType

NB, L, D = 16, 750, 128
H = 8
HD = D // H
SCALE = float(HD) ** -0.5
K_TOP = max(1, int(L * 0.2))
EPS = 1e-5
FF = 512
TT = 125
NT = L // TT
HALF = L // 2
NG = NB * H
JT = 76
NJ = 2 * JT
PARTS = 6
KR = PARTS * HD
S = L // 2
ST = S // TT
NTILE = NB * ST
E = 8
EH = 512
BLK = 128
ROUNDER = 1.5 * 2.0 ** 23
CUTS = 4
NBLK = (NB * S) // BLK + E
assert NT * TT == L and ST * TT == S and K_TOP + 2 == NJ and NG == 128

COLS = ["o_b", "ln1_g", "ln1_b", "f2_b", "ln2_g", "ln2_b", "conv_b", "f1_b0", "f1_b1", "f1_b2", "f1_b3"]


def rounds(eng, steps, count, body, first):
    def round_of(r, i=0):
        for lead, step in steps:
            b = r + lead
            if not isinstance(i, int) or 0 <= b < count:
                step(body * i + b, b % body, i + b // body)
    leads = [lead for lead, _ in steps]
    loops = (count - max(leads) - first) // body
    for r in range(-max(leads), first):
        round_of(r)
    with eng.Fori(0, loops) as i:
        for r in range(first, first + body):
            round_of(r, i)
    for r in range(first + body * loops, count - min(leads)):
        round_of(r)


def wait_before(eng, semaphore, count):
    if not isinstance(count, int) or count > 0:
        eng.wait_ge(semaphore, count)


def stage3_tensors(sb):
    return {
        "wkv": sb("wkv", [D, 2 * D]),
        "kvb": sb("kvb_rows", [TT, 2 * D]),
        "wo": sb("wo", [D, D]),
        "f1": sb("f1", [D, FF]),
        "f2": sb("f2", [128, FF // 128, D]),
        "cw": sb("conv_taps", [D, 3, D]),
        "cols": sb("feature_cols", [D, len(COLS)]),
        "center": sb("center", [D, D]),
        "mean": sb("mean", [D, D]),
        "ident_bf": sb("ident_bf", [128, 128], BF16),
        "iota": sb("iota_f", [TT, NJ]),
        "iota_bf": sb("iota_bf", [TT, NJ], BF16),
        "slot_id": sb("slot_id", [JT, 2]),
        "eps": sb("eps", [D, 1]),
        "v_pad": sb("v_pad", [TT, NT, H, 32]),
        "kT": sb("kT", [KR + 3, H, L], BF16),
        "att": sb("att", [JT, 512]),
        "attp": sb("attp", [JT, 3, 512], BF16),
        "fu": sb("fu", [D, L + 2]),
    }


def stage3_loads(c, io):
    rows = {n: io[n].rearrange("(a n) -> a n", a=1).to_broadcast([TT, D]) for n in ("L0_tok_k_b", "L0_tok_v_b")}
    return [(c["wkv"][:, 0:D], io["L0_tok_k_w"]), (c["wkv"][:, D:2 * D], io["L0_tok_v_w"]),
            (c["kvb"][:, 0:D], rows["L0_tok_k_b"]), (c["kvb"][:, D:2 * D], rows["L0_tok_v_b"]),
            (c["wo"][:, :], io["L0_tok_o_w"]), (c["f1"][:, :], io["L0_tok_f1_w"]),
            (c["f2"][:, :, :], io["L0_tok_f2_w"].rearrange("(c p) d -> p c d", p=128)),
            (c["cw"][:, :, :], io["conv_w"]), (c["cols"][:, :], io["cols"]), (c["center"][:, :], io["c_center"]),
            (c["iota"][:, :], io["c_iota"].to_broadcast([TT, NJ])), (c["slot_id"][:, :], io["c_slot_id"])]


def norms_and_ranks(nc, t, io):
    BUFS = 4
    with ExitStack() as ctx:
        def sb(name, shape, dt=F32):
            return ctx.enter_context(nc.sbuf_tensor(name, shape, dt))

        def sem(name):
            return ctx.enter_context(nc.semaphore(name))

        wq = sb("wq", [D, D])
        qb = sb("qb_rows", [TT, D])
        x_in = [sb(f"x_in1{p}", [TT, NT, D]) for p in range(BUFS)]
        xT = [sb(f"xT1{p}", [D, L]) for p in range(2)]
        q_sb = [sb(f"q_sb{p}", [TT, NT * D]) for p in range(BUFS)]
        sq = [sb(f"sq{p}", [TT, NT * D]) for p in range(2)]
        qn_tok = sb("qn_tok", [TT, NT, NG])
        qn = sb("qn", [NG, L])
        top8 = sb("top8", [NG, 8])
        ones = sb("ones_row", [NG, L])
        count = sb("count", [NG, L])
        rank = sb("rank", [NG, L])
        rank_bf = sb("rank_bf", [NG, L], BF16)
        xT_ps = [ctx.enter_context(nc.psum_tensor(f"xT_ps{p}", [D, 2, 512], F32)) for p in range(2)]
        q_ps = [ctx.enter_context(nc.psum_tensor(f"q_ps{p}", [D, 2, 512], F32)) for p in range(2)]

        w_loaded = sem("w_loaded")
        const_loaded = sem("const_loaded")
        const_set = sem("const_set")
        x_loaded = [sem(f"x_loaded1{p}") for p in range(BUFS)]
        xT_done = sem("xT_done1")
        xT_ready = sem("xT_ready1")
        q_done = sem("q_done")
        q_ready = sem("q_ready")
        q_stored = [sem(f"q_stored{p}") for p in range(BUFS)]
        sq_ready = sem("sq_ready")
        norm_ready = sem("norm_ready")
        norms_turned = sem("norms_turned")
        top = sem("top_step")
        ranks_ready = sem("ranks_ready")
        ranks_turned = sem("ranks_turned")
        ranks_out = sem("ranks_out")
        x_v = io["x"].rearrange("b (n p) d -> b p n d", p=TT)

        with nc.Block() as block:
            @block.sync
            def _(sp):
                sp.dma_start(t["ident"][:, :], io["c_ident"]).then_inc(w_loaded, 16)
                sp.dma_start(wq[:, :], io["L0_tok_q_w"]).then_inc(w_loaded, 16)
                sp.dma_start(qb[:, :], io["L0_tok_q_b"].rearrange("(a n) -> a n", a=1).to_broadcast([TT, D])).then_inc(w_loaded, 16)

                def load(b, p, j):
                    wait_before(sp, xT_done, b - BUFS + 1)
                    sp.dma_start(x_in[p][:, :, :], x_v[bass.ds(b, 1), :, :, :].rearrange("b p n d -> (b p) n d")).then_inc(x_loaded[p], 16)

                rounds(sp, [(3, load)], NB, BUFS, 2)
                loads = stage3_loads(t["stage3"], io)
                for dst, src in loads:
                    sp.dma_start(dst, src).then_inc(const_loaded, 16)
                sp.wait_ge(const_loaded, 16 * len(loads))
                sp.wait_ge(ranks_ready, 1)
                sp.dma_start(io["rank_rows"], rank_bf[:, :]).then_inc(ranks_out, 16)
                sp.wait_ge(ranks_out, 16)

            @block.gpsimd
            def _(pool):
                c = t["stage3"]
                done = [0]

                def chain(ins):
                    done[0] += 1
                    ins.then_inc(const_set, 1)
                    pool.wait_ge(const_set, done[0])

                chain(pool.memset(c["mean"][:, :], 1.0 / D))
                chain(pool.memset(c["eps"][:, :], EPS))
                chain(pool.memset(c["v_pad"][:, :, :, :], 0.0))
                for odd in range(2):
                    chain(pool.memset(c["v_pad"][:, :, odd:H:2, HD * (1 - odd):HD * (1 - odd) + 1], 1.0))
                chain(pool.memset(c["kT"][KR:KR + 3, :, :], -1.0))
                chain(pool.memset(c["fu"][:, :], 0.0))
                for k in range(3):
                    chain(pool.memset(c["attp"][:, k, :], 0.0))
                chain(pool.memset(c["att"][:, :], 0.0))
                pool.wait_ge(const_loaded, 16 * len(stage3_loads(c, io)))
                chain(pool.tensor_copy(c["iota_bf"][:, :], c["iota"][:, :]))
                pool.wait_ge(w_loaded, 48)
                chain(pool.tensor_copy(c["ident_bf"][:, :], t["ident"][:, :]))

            @block.tensor
            def _(pe):
                pe.wait_ge(w_loaded, 48)

                def turn_x(b, p, j):
                    pe.wait_ge(x_loaded[p], 16 * j + 16)
                    for n in range(NT):
                        mm = pe.transpose(xT_ps[p % 2][:, n // 3, (n % 3) * TT:(n % 3 + 1) * TT],
                                          x_in[p][:, n, :], t["ident"][0:TT, 0:TT])
                    mm.then_inc(xT_done, 1)

                def project(b, p, j):
                    pe.wait_ge(xT_ready, b + 1)
                    wait_before(pe, q_ready, b - 1)
                    for n in range(NT):
                        mm = pe.matmul(q_ps[p % 2][0:TT, n // 3, (n % 3) * D:(n % 3 + 1) * D],
                                       xT[p % 2][:, n * TT:(n + 1) * TT], wq[:, :], start=True, stop=True)
                    mm.then_inc(q_done, 1)

                rounds(pe, [(1, turn_x), (0, project)], NB, BUFS, 2)
                pe.wait_ge(norm_ready, NB)
                for n in range(NT):
                    mm = pe.transpose(xT_ps[0][:, n // 3, (n % 3) * TT:(n % 3 + 1) * TT], qn_tok[:, n, :],
                                      t["ident"][0:TT, 0:TT])
                mm.then_inc(norms_turned, 1)
                pe.wait_ge(ranks_ready, 1)
                for n in range(NT):
                    mm = pe.transpose(q_ps[0][0:TT, n // 3, (n % 3) * NG:(n % 3 + 1) * NG], rank[:, n * TT:(n + 1) * TT],
                                      t["ident"][:, :])
                mm.then_inc(ranks_turned, 1)

            @block.scalar
            def _(act):
                act.preload_act_table_set("natural_log_exp_and_others")
                for p in range(BUFS):
                    act.sem_inc(q_stored[p], 16)

                def take_xT(b, p, j):
                    act.wait_ge(xT_done, b + 1)
                    act.activation(xT[p % 2][:, :].rearrange("p (a c) -> p a c", a=2), xT_ps[p % 2][:, :, 0:HALF],
                                   ACT.Copy).then_inc(xT_ready, 1)

                def square(b, p, j):
                    act.wait_ge(q_ready, b + 1)
                    wait_before(act, norm_ready, b - 1)
                    act.activation(sq[p % 2][:, :], q_sb[p][:, :], ACT.Square).then_inc(sq_ready, 1)
                    act.dma_start(io["q_rows"][bass.ds(b, 1), :, :].rearrange("b p n -> (b p) n"), q_sb[p][:, :]).then_inc(q_stored[p], 16)

                rounds(act, [(1, take_xT), (0, square)], NB, BUFS, 2)
                for p in range(BUFS):
                    act.wait_ge(q_stored[p], 16 * (NB // BUFS) + 16)

            @block.vector
            def _(dve):
                step = [0]

                def chain(ins):
                    step[0] += 1
                    ins.then_inc(top, 1)
                    dve.wait_ge(top, step[0])

                chain(dve.memset(ones[:, :], 1.0))
                dve.wait_ge(w_loaded, 48)

                def take_q(b, p, j):
                    dve.wait_ge(q_done, b + 1)
                    dve.wait_ge(q_stored[p], 16 * j + 16)
                    dve.tensor_tensor(
                        q_sb[p][:, :].rearrange("p (a n d) -> p a n d", a=2, n=3),
                        q_ps[p % 2][0:TT, :, 0:3 * D].rearrange("p a (n d) -> p a n d", n=3),
                        qb[:, :].unsqueeze(1).unsqueeze(1).to_broadcast([TT, 2, 3, D]), ALU.add).then_inc(q_ready, 1)

                def norms(b, p, j):
                    dve.wait_ge(sq_ready, b + 1)
                    dve.tensor_reduce(qn_tok[:, :, bass.ds(b * H, H)],
                                      sq[p % 2][:, :].rearrange("p (n h d) -> p n h d", n=NT, h=H), AX.X, ALU.add)\
                       .then_inc(norm_ready, 1)

                rounds(dve, [(0, take_q), (-1, norms)], NB, BUFS, 2)
                dve.wait_ge(norms_turned, 1)
                chain(dve.tensor_copy(qn[:, :].rearrange("p (a c) -> p a c", a=2), xT_ps[0][:, :, 0:HALF]))
                left = K_TOP
                while left > 0:
                    chain(dve.max(top8[:, :], qn[:, :]))
                    if left < 8:
                        chain(dve.memset(top8[:, left:8], -1.0))
                    chain(dve.match_replace(qn[:, :], top8[:, :], qn[:, :], -1.0))
                    left -= 8
                chain(dve.tensor_scalar(qn[:, :], qn[:, :], -1.0, None, ALU.is_equal))
                chain(dve.tensor_tensor_scan(count[:, :], ones[:, :], qn[:, :], 0.0, ALU.mult, ALU.add))
                chain(dve.tensor_tensor(count[:, :], count[:, :], qn[:, :], ALU.mult))
                chain(dve.tensor_scalar(rank[:, :], count[:, :], -1.0, None, ALU.add))
                dve.tensor_copy(rank_bf[:, :], rank[:, :]).then_inc(ranks_ready, 1)
                dve.wait_ge(ranks_turned, 1)
                dve.tensor_copy(t["rank_tok"][:, :, :].rearrange("p (a n) g -> p a n g", a=2),
                                q_ps[0][0:TT, :, 0:3 * NG].rearrange("p a (n g) -> p a n g", n=3))


def sequences(nc, t, io):
    P_TILES = ["xT", "k", "v"]
    A_ONLY = [f"kt{i}" for i in range(4)] + ["g0", "g1"] + [f"max{i}" for i in range(2 * H)] + ["mt"] + [f"s{h}" for h in range(H)]
    E_TILES = ["c2", "m2", "cv", "ht"]
    D_ONLY = ["sc", "o", "c1", "m1", "f0", "f1", "f2", "f3", "ff"]
    A_TILES = [step for part, step in order() if step in P_TILES + A_ONLY]
    D_TILES = [step for part, step in order() if step in E_TILES + D_ONLY]
    A_SLOTS = 2
    FIRST_A, FIRST_D = A_TILES.index("xT"), D_TILES.index("sc")
    EMPTY = [("P", name) for name in A_TILES[FIRST_A:] if name not in P_TILES] + [("ADE", "xT"), ("ADE", "k")] \
        + [("PAD", name) for name in D_TILES[FIRST_D:] if name in E_TILES] \
        + [("E", name) for name in D_TILES[:D_TILES.index("ht")] if name in D_ONLY]
    assert A_TILES[-1] == "v" and all(name[0] == "s" or name in ("ht", "xT", "k", "o") for parts, name in EMPTY)
    A_PER = len(A_TILES) // A_SLOTS
    D_PER = len(D_TILES)
    assert A_PER * A_SLOTS == len(A_TILES)
    c = t["stage3"]
    wkv, kvb, wo, f1, f2, cw, cols, center, mean, ident_bf, iota_bf, slot_id, eps = [
        c[n] for n in ("wkv", "kvb", "wo", "f1", "f2", "cw", "cols", "center", "mean", "ident_bf", "iota_bf", "slot_id", "eps")]

    with ExitStack() as ctx:
        def sb(name, shape, dt=F32):
            return ctx.enter_context(nc.sbuf_tensor(name, shape, dt))

        def sem(name):
            return ctx.enter_context(nc.semaphore(name))

        x_in = sb("x_in", [TT, NT, D])
        q_in = sb("q_in", [TT, NT * H, HD])
        xT = [sb(f"xT{p}", [D, L]) for p in range(2)]
        kf = sb("kf", [TT, NT * H, HD])
        q_rest = sb("q_rest", [TT, NT * H, HD])
        k_rest = sb("k_rest", [TT, NT * H, HD])
        qst = sb("qst", [TT, NT * H, PARTS, HD], BF16)
        kst = sb("kst", [TT, NT * H, PARTS, HD], BF16)
        v_pad = c["v_pad"]
        rank_cur = sb("rank_cur", [TT, NT, H])
        rank_bc = sb("rank_bc", [JT, H * L], BF16)
        G = sb("G", [TT, NT, H, NJ], BF16)
        GT = sb("GT", [JT, 2, H * L], BF16)
        kT = c["kT"]
        qT = sb("qT", [KR + 3, H * NJ], BF16)
        mx = sb("mx", [JT, 2 * H])
        mx_rest = sb("mx_rest", [JT, 2 * H])
        mx_rest2 = sb("mx_rest2", [JT, 2 * H])
        mxp = sb("mxp", [JT, 3, 2 * H], BF16)
        mxT = sb("mxT", [6 * H, JT], BF16)
        Pt = sb("Pt", [TT, H, NT * NJ])
        au = sb("au", [128, 2, NJ])
        rden = sb("rden", [JT, 4, 4])
        att, attp = c["att"], c["attp"]
        att_rest = sb("att_rest", [JT, 512])
        attT = sb("attT", [D, L])
        ao = sb("ao", [D, L])
        aob = sb("aob", [D, L])
        r = sb("r", [D, L])
        cS = sb("cS", [D, L])
        sq = sb("sqD", [D, L])
        h1 = sb("h1", [D, L])
        rl = sb("rl", [128, FF // 128, L])
        fu = c["fu"]
        hp = sb("hp", [D, S])
        hT = sb("hT", [D, S])
        h_sb = sb("h_sb", [TT, ST * D])

        a_ps = [ctx.enter_context(nc.psum_tensor(f"a_ps{s}", [128, 2, 512], F32)) for s in range(A_SLOTS)]
        d_ps = ctx.enter_context(nc.psum_tensor("d_ps", [128, 2, 512], F32))
        pv_ps = ctx.enter_context(nc.psum_tensor("pv_ps", [128, 512], F32))
        at_ps = ctx.enter_context(nc.psum_tensor("at_ps", [128, 512], F32))

        a_done = [sem(f"a_done{s}") for s in range(A_SLOTS)]
        a_free = [sem(f"a_free{s}") for s in range(A_SLOTS)]
        d_done = sem("d_done")
        d_free = sem("d_free")
        x_loaded = sem("x_loaded")
        q_loaded = sem("q_loaded")
        rank_loaded = sem("rank_loaded")
        rounded = {"q": sem("q_rounded"), "k": sem("k_rounded")}
        reduced = {"q": sem("q_reduced"), "k": sem("k_reduced")}
        copied = {"q": sem("q_copied"), "k": sem("k_copied")}
        cur_ready = sem("cur_ready")
        g_ready = sem("g_ready")
        gt_ready = sem("gt_ready")
        mx_step = sem("mx_step")
        mxp_ready = sem("mxp_ready")
        mxT_ready = sem("mxT_ready")
        mx_rows = sem("mx_rows")
        pv_done = [sem(f"pv_done{q}") for q in range(2)]
        au_ready = sem("au_ready")
        att_step = sem("att_step")
        attp_ready = sem("attp_ready")
        r_ready = sem("r_ready")
        aob_ready = sem("aob_ready")
        sq_ready = sem("sq_readyD")
        ln_step = sem("ln_step")
        rstd_ready = sem("rstd_ready")
        at_done = sem("at_done")
        h1_ready = sem("h1_ready")
        fu_ready = sem("fu_ready")
        hp_ready = sem("hp_ready")
        hT_ready = sem("hT_ready")
        h_ready = sem("h_ready")
        h_stored = sem("h_stored")
        gates = {eng: sem(f"gate_{n}") for n, eng in (("sp", nc.sync), ("pool", nc.gpsimd), ("pe", nc.tensor))}

        def a_slot(name):
            return A_TILES.index(name) % A_SLOTS

        def a_count(name, b):
            return A_PER * (b if name in P_TILES else b + 1) + A_TILES.index(name) // A_SLOTS + 1

        def credit(slot):
            return len([n for n in A_TILES[:FIRST_A] if a_slot(n) == slot])

        def a_tile(name):
            return a_ps[a_slot(name)]

        def d_count(name, b):
            return D_PER * (b + 1 if name in E_TILES else b) + D_TILES.index(name) + 1

        def await_a(eng, what, name, b):
            wait_before(eng, what[a_slot(name)], a_count(name, b))

        def col(name):
            return cols[:, COLS.index(name):COLS.index(name) + 1]

        def gate(eng):
            eng.sem_inc(gates[eng], 1)

        def two(ap):
            return ap.rearrange("p (a c) -> p a c", a=2)

        def two_of_three(ap, n):
            return ap[0:TT, :, 0:3 * n].rearrange("p a (t c) -> p a t c", t=3)

        KTS = TT + 1

        def turned_k(i):
            return a_tile(f"kt{i}")[0:KR, :, 0:NT * KTS // 2].bitcast(BF16).rearrange("p g (n c) -> p g n c", n=NT)[:, :, :, 0:TT]

        x_v = io["x"].rearrange("b (n p) d -> b p n d", p=TT)

        def run(eng, part_p, part_a, part_d, part_e, hand_on=None):
            SHARE = {"P": (part_p, 1), "A": (part_a, 0), "D": (part_d, -1), "E": (part_e, -2)}

            def round_of(b, pb, parts="PADE"):
                for part, step in ORDER:
                    steps, lead = SHARE[part]
                    if hand_on and (parts, step) in EMPTY:
                        hand_on(step, b + lead)
                    if part in parts and step in steps:
                        steps[step](b + lead, (pb + lead) % 2)
            round_of(-1, 1, "P")
            round_of(0, 0, "PA")
            round_of(1, 1, "PAD")
            with eng.Fori(0, NB // 2 - 2) as i:
                round_of(2 * i + 2, 0)
                round_of(2 * i + 3, 1)
            round_of(NB - 2, 0)
            round_of(NB - 1, 1, "ADE")
            round_of(NB, 0, "DE")
            round_of(NB + 1, 1, "E")

        ORDER = order()

        with nc.Block() as block:
            @block.sync
            def _(sp):
                sp.sem_inc(h_stored, 16)

                def load(b, pb):
                    await_a(sp, a_done, "xT", b - 1)
                    gate(sp)
                    sp.dma_start(x_in[:, :, :], x_v[bass.ds(b, 1), :, :, :].rearrange("b p n d -> (b p) n d")).then_inc(x_loaded, 16)
                    wait_before(sp, reduced["q"], 2 * b - 1)
                    gate(sp)
                    sp.dma_start(q_in[:, :, :].rearrange("p g d -> p (g d)"),
                                 io["q_rows"][bass.ds(b, 1), :, :].rearrange("b p n -> (b p) n")).then_inc(q_loaded, 16)

                def load_ranks(b, pb):
                    wait_before(sp, gt_ready, b)
                    gate(sp)
                    sp.dma_start(rank_bc[:, :], io["rank_rows"].rearrange("(b h) l -> b (h l)", h=H)[bass.ds(b, 1), :]
                                 .to_broadcast([JT, H * L])).then_inc(rank_loaded, 16)

                def max_rows(b, pb):
                    sp.wait_ge(mxT_ready, b + 1)
                    gate(sp)
                    for k in range(3):
                        sp.dma_start(qT[KR + k:KR + k + 1, :], mxT[2 * H * k:2 * H * (k + 1), :]).then_inc(mx_rows, 16)

                def store_h(b, pb):
                    sp.wait_ge(h_ready, b + 1)
                    gate(sp)
                    sp.dma_start(io["h_rows"][bass.ds(b, 1), :, :].rearrange("b p n -> (b p) n"), h_sb[:, :]).then_inc(h_stored, 16)

                run(sp, {"load": load, "ranks": load_ranks}, {"mt": max_rows}, {}, {"ht": store_h})
                sp.wait_ge(h_stored, 16 * NB + 16)

            @block.gpsimd
            def _(pool):
                def take_off(x, n, out, whole, part):
                    def go(b, pb):
                        pool.wait_ge(rounded[x], 2 * b + n)
                        pool.tensor_tensor(out, whole, part, ALU.subtract).then_inc(reduced[x], 1)
                    return go

                def copy_q(b, pb):
                    pool.wait_ge(rounded["q"], 2 * b + 2)
                    gate(pool)
                    for src, to in Q_COPIES:
                        ins = pool.tensor_copy(qst[:, :, to, :], qst[:, :, src, :])
                    ins.then_inc(copied["q"], 1)

                def residual_bias(b, pb):
                    pool.wait_ge(d_free, d_count("o", b))
                    gate(pool)
                    pool.tensor_scalar(aob[:, :], ao[:, :], col("ln2_b"), None, ALU.add).then_inc(aob_ready, 1)

                run(pool, {"q_rest": take_off("q", 1, q_rest[:, :, :], q_in[:, :, :], qst[:, :, 0, :]),
                           "q_third": take_off("q", 2, qst[:, :, 5, :], q_rest[:, :, :], qst[:, :, 3, :]),
                           "q_copy": copy_q,
                           "k_rest": take_off("k", 1, k_rest[:, :, :], kf[:, :, :], kst[:, :, 0, :]),
                           "k_third": take_off("k", 2, kst[:, :, 2, :], k_rest[:, :, :], kst[:, :, 1, :])},
                    {}, {"o": residual_bias}, {})

            @block.tensor
            def _(pe):
                for slot in range(A_SLOTS):
                    pe.sem_inc(a_done[slot], credit(slot))
                pe.sem_inc(d_done, FIRST_D)

                def taken(b, names, fill=None):
                    for slot in range(A_SLOTS):
                        counts = [a_count(n, 0) for n in names if a_slot(n) == slot]
                        if fill is not None and a_slot(fill) == slot:
                            counts.append(a_count(fill, 0) - 1)
                        if counts:
                            pe.wait_ge(a_free[slot], A_PER * b + max(counts))

                def fill_a(name, b, reads=()):
                    taken(b, reads, name)
                    return a_tile(name)

                def filled_a(mm, name):
                    mm.then_inc(a_done[a_slot(name)], 1)

                def fill_d(name, b):
                    pe.wait_ge(d_free, d_count(name, b) - 1)
                    return d_ps

                def turn_x(b, pb):
                    pe.wait_ge(x_loaded, 16 * b + 16)
                    ps = fill_a("xT", b)
                    for n in range(NT):
                        mm = pe.transpose(ps[:, n // 3, (n % 3) * TT:(n % 3 + 1) * TT], x_in[:, n, :], t["ident"][0:TT, 0:TT])
                    filled_a(mm, "xT")

                def project(name, w):
                    def go(b, pb):
                        ps = fill_a(name, b, ["xT"])
                        for n in range(NT):
                            mm = pe.matmul(ps[0:TT, n // 3, (n % 3) * D:(n % 3 + 1) * D], xT[pb][:, n * TT:(n + 1) * TT], w,
                                           start=True, stop=True)
                        filled_a(mm, name)
                    return go

                def turn_k(i):
                    def go(b, pb):
                        pe.wait_ge(copied["k"], b + 1)
                        pe.wait_ge(reduced["k"], 2 * b + 2)
                        ps = fill_a(f"kt{i}", b)
                        for g in range(2):
                            for n in range(NT):
                                mm = pe.transpose(ps[0:KR, g, :].bitcast(BF16)[:, n * KTS:n * KTS + TT],
                                                  kst[:, n * H + 2 * i + g, :, :].rearrange("p a d -> p (a d)"),
                                                  ident_bf[0:TT, 0:TT])
                        filled_a(mm, f"kt{i}")
                    return go

                def gather(i):
                    def go(b, pb):
                        pe.wait_ge(copied["q"], b + 1)
                        pe.wait_ge(reduced["q"], 2 * b + 2)
                        pe.wait_ge(g_ready, b + 1)
                        ps = fill_a(f"g{i}", b)
                        for g in range(4):
                            h = 4 * i + g
                            for n in range(NT):
                                mm = pe.matmul(ps[0:KR, g // 2, (g % 2) * NJ:(g % 2 + 1) * NJ],
                                               qst[:, n * H + h, :, :].rearrange("p a d -> p (a d)"), G[:, n, h, :],
                                               start=(n == 0), stop=(n == NT - 1))
                        filled_a(mm, f"g{i}")
                    return go

                def scores_for_max(i):
                    h, jt = i // 2, i % 2

                    def go(b, pb):
                        ps = fill_a(f"max{i}", b, [f"kt{h // 2}", f"g{h // 4}"])
                        for c in range(2):
                            mm = pe.matmul(ps[0:JT, c, 0:HALF], qT[0:KR, i * JT:(i + 1) * JT],
                                           kT[0:KR, h, c * HALF:(c + 1) * HALF], start=True, stop=True)
                        filled_a(mm, f"max{i}")
                    return go

                def turn_max(b, pb):
                    pe.wait_ge(mxp_ready, b + 1)
                    ps = fill_a("mt", b)
                    gate(pe)
                    filled_a(pe.transpose(ps[0:6 * H, 0, 0:JT // 2].bitcast(BF16), mxp[:, :, :].rearrange("p a s -> p (a s)"),
                                          ident_bf[0:JT, 0:JT]), "mt")

                def scores(h):
                    def go(b, pb):
                        pe.wait_ge(mx_rows, 48 * b + 48)
                        ps = fill_a(f"s{h}", b)
                        for n in range(NT):
                            mm = pe.matmul(ps[0:TT, n // 3, (n % 3) * NJ:(n % 3 + 1) * NJ], kT[:, h, n * TT:(n + 1) * TT],
                                           qT[:, h * NJ:(h + 1) * NJ], start=True, stop=True)
                        filled_a(mm, f"s{h}")
                    return go

                def values(q):
                    def go(b, pb):
                        taken(b, ["v"] + [f"s{4 * q + g}" for g in range(4)])
                        wait_before(pe, au_ready, b)
                        for n in range(NT):
                            for g in range(4):
                                mm = pe.matmul(pv_ps[32 * g:32 * g + 32, q * NJ:(q + 1) * NJ], v_pad[:, n, 4 * q + g, :],
                                               Pt[:, 4 * q + g, n * NJ:(n + 1) * NJ], start=(n == 0), stop=(n == NT - 1))
                        mm.then_inc(pv_done[q], 1)
                    return go

                def turn_att(b, pb):
                    pe.wait_ge(au_ready, b + 1)
                    for q in range(2):
                        for jt in range(2):
                            mm = pe.transpose(at_ps[0:JT, (2 * q + jt) * 128:(2 * q + jt + 1) * 128],
                                              au[:, q, jt * JT:(jt + 1) * JT], t["ident"][:, :])
                    mm.then_inc(at_done, 1)

                def scatter(step):
                    c, odd = step // 2, step % 2

                    def go(b, pb):
                        if step == 0:
                            pe.wait_ge(attp_ready, b + 1)
                            pe.wait_ge(gt_ready, b + 1)
                            fill_d("sc", b)
                        for k in range(3):
                            for jt in range(2):
                                for g in range(4):
                                    h = 2 * g + odd
                                    at = (2 * (h // 4) + jt) * 128 + 32 * (h % 4)
                                    mm = pe.matmul(d_ps[32 * g:32 * g + 32, c, 0:HALF], attp[:, k, at:at + 32],
                                                   GT[:, jt, h * L + c * HALF:h * L + (c + 1) * HALF],
                                                   start=(odd == 0 and k == 0 and jt == 0), stop=(odd == 1 and k == 2 and jt == 1))
                        if step == 3:
                            mm.then_inc(d_done, 1)
                    return go

                def dense(name, terms, waits):
                    def go(b, pb):
                        for w in waits:
                            w(b)
                        ps = fill_d(name, b)
                        for c in range(2):
                            for k, (w, data) in enumerate(terms):
                                mm = pe.matmul(ps[:, c, 0:HALF], w, data[:, c * HALF:(c + 1) * HALF],
                                               start=(k == 0), stop=(k == len(terms) - 1))
                        mm.then_inc(d_done, 1)
                    return go

                def convolve(c):
                    def go(b, pb):
                        if c == 0:
                            pe.wait_ge(fu_ready, b + 1)
                            fill_d("cv", b)
                        at, n = ((0, HALF + 1), (HALF + 1, HALF - 1))[c]
                        for tap in range(3):
                            mm = pe.matmul(d_ps[:, c, 0:n], cw[:, tap, :], fu[:, at + tap:at + tap + n],
                                           start=(tap == 0), stop=(tap == 2))
                        if c == 1:
                            mm.then_inc(d_done, 1)
                    return go

                def turn_h(b, pb):
                    pe.wait_ge(hT_ready, b + 1)
                    ps = fill_d("ht", b)
                    for n in range(ST):
                        mm = pe.transpose(ps[0:TT, 0, n * D:(n + 1) * D], hT[:, n * TT:(n + 1) * TT], t["ident"][:, :])
                    mm.then_inc(d_done, 1)

                part_p = {"xT": turn_x, "k": project("k", wkv[:, 0:D]), "v": project("v", wkv[:, D:2 * D])}
                part_a = {"mt": turn_max}
                for i in range(4):
                    part_a[f"kt{i}"] = turn_k(i)
                for i in range(2):
                    part_a[f"g{i}"] = gather(i)
                    part_a[f"pv{i}"] = values(i)
                for i in range(2 * H):
                    part_a[f"max{i}"] = scores_for_max(i)
                for h in range(H):
                    part_a[f"s{h}"] = scores(h)
                part_d = {"at": turn_att}
                for i, name in enumerate(["sc", "sc1", "sc2", "sc3"]):
                    part_d[name] = scatter(i)
                part_e = {"cv": convolve(0), "cv1": convolve(1), "ht": turn_h}
                part_d["o"] = dense("o", [(wo[:, :], attT[:, :])], [])
                part_d["c1"] = dense("c1", [(center[:, :], r[:, :])], [lambda b: pe.wait_ge(r_ready, 2 * b + 1)])
                part_d["m1"] = dense("m1", [(mean[:, :], sq[:, :])], [lambda b: pe.wait_ge(sq_ready, 2 * b + 1)])
                for i in range(4):
                    part_d[f"f{i}"] = dense(f"f{i}", [(f1[:, i * 128:(i + 1) * 128], h1[:, :])],
                                            [lambda b: pe.wait_ge(h1_ready, b + 1)])
                part_d["ff"] = dense("ff", [(f2[:, i, :], rl[:, i, :]) for i in range(4)],
                                     [])
                part_e["c2"] = dense("c2", [(center[:, :], r[:, :])], [lambda b: pe.wait_ge(r_ready, 2 * b + 2)])
                part_e["m2"] = dense("m2", [(mean[:, :], sq[:, :])], [lambda b: pe.wait_ge(sq_ready, 2 * b + 2)])
                def hand_on(name, b):
                    if name in A_TILES:
                        fill_a(name, b)
                        pe.sem_inc(a_done[a_slot(name)], 1)
                    else:
                        fill_d(name, b)
                        pe.sem_inc(d_done, 1)

                run(pe, part_p, part_a, part_d, part_e, hand_on)

            @block.scalar
            def _(act):
                act.preload_act_table_set("natural_log_exp_and_others")
                for slot in range(A_SLOTS):
                    act.sem_inc(a_free[slot], credit(slot))
                act.sem_inc(d_free, FIRST_D)

                def take_xT(b, pb):
                    await_a(act, a_done, "xT", b)
                    wait_before(act, r_ready, 2 * b - 3)
                    act.activation(two(xT[pb][:, :]), a_tile("xT")[:, :, 0:HALF], ACT.Copy).then_inc(a_free[a_slot("xT")], 1)

                def take_kT(i):
                    def go(b, pb):
                        await_a(act, a_done, f"kt{i}", b)
                        act.activation(kT[0:KR, 2 * i:2 * i + 2, :].rearrange("p g (n c) -> p g n c", n=NT), turned_k(i), ACT.Copy)\
                           .then_inc(a_free[a_slot(f"kt{i}")], 1)
                    return go

                def take_qT(i):
                    def go(b, pb):
                        await_a(act, a_done, f"g{i}", b)
                        act.activation(qT[0:KR, i * 4 * NJ:(i + 1) * 4 * NJ].rearrange("p (a c) -> p a c", a=2),
                                       a_tile(f"g{i}")[0:KR, :, 0:2 * NJ], ACT.Copy).then_inc(a_free[a_slot(f"g{i}")], 1)
                    return go

                def exps(h):
                    def go(b, pb):
                        await_a(act, a_done, f"s{h}", b)
                        act.activation(Pt[:, h, :].rearrange("p (a c) -> p a c", a=2), a_tile(f"s{h}")[0:TT, :, 0:3 * NJ],
                                       ACT.Exp, scale=SCALE).then_inc(a_free[a_slot(f"s{h}")], 1)
                    return go

                def round_part(x, n, out, whole, last_read):
                    def go(b, pb):
                        if n == 1:
                            x_there(b)[x]()
                            await_a(act, a_done, last_read, b - 1)
                        else:
                            act.wait_ge(reduced[x], 2 * b + 1)
                        act.activation(out, whole, ACT.Copy).then_inc(rounded[x], 1)
                    return go

                def x_there(b):
                    return {"q": lambda: act.wait_ge(q_loaded, 16 * b + 16), "k": lambda: await_a(act, a_free, "k", b)}

                def take_pv(b, pb):
                    act.wait_ge(pv_done[0], b + 1)
                    act.wait_ge(pv_done[1], b + 1)
                    act.activation(au[:, :, :].rearrange("p a c -> p (a c)"), pv_ps[:, 0:2 * NJ], ACT.Copy).then_inc(au_ready, 1)

                def take_sc(b, pb):
                    act.wait_ge(d_done, d_count("sc", b))
                    act.activation(two(attT[:, :]), d_ps[:, :, 0:HALF], ACT.Copy).then_inc(d_free, 1)

                def take_o(b, pb):
                    act.wait_ge(d_done, d_count("o", b))
                    act.activation(two(ao[:, :]), d_ps[:, :, 0:HALF], ACT.Identity, bias=col("o_b")).then_inc(d_free, 1)

                def take_c(i):
                    def go(b, pb):
                        act.wait_ge(d_done, d_count(f"c{i}", b))
                        act.activation(two(cS[:, :]), d_ps[:, :, 0:HALF], ACT.Copy)
                        act.activation(two(sq[:, :]), d_ps[:, :, 0:HALF], ACT.Square).then_inc(sq_ready, 1)
                        act.wait_ge(sq_ready, 2 * b + i)
                        act.sem_inc(d_free, 1)
                    return go

                def take_m(i):
                    def go(b, pb):
                        act.wait_ge(d_done, d_count(f"m{i}", b))
                        act.activation(two(sq[:, :]), d_ps[:, :, 0:HALF], ACT.Ln, bias=eps[:, :]).then_inc(d_free, 1)
                        act.wait_ge(d_free, d_count(f"m{i}", b))
                        act.activation(sq[:, :], sq[:, :], ACT.Exp, scale=-0.5).then_inc(rstd_ready, 1)
                    return go

                def take_f(i):
                    def go(b, pb):
                        act.wait_ge(d_done, d_count(f"f{i}", b))
                        act.activation(two(rl[:, i, :]), d_ps[:, :, 0:HALF], ACT.Relu, bias=col(f"f1_b{i}")).then_inc(d_free, 1)
                    return go

                def relu_h(b, pb):
                    act.wait_ge(hp_ready, 2 * b + 2)
                    act.activation(hT[:, :], hp[:, :], ACT.Relu, bias=col("conv_b")).then_inc(hT_ready, 1)

                def take_h(b, pb):
                    act.wait_ge(d_done, d_count("ht", b))
                    act.wait_ge(h_stored, 16 * b + 16)
                    act.activation(h_sb[:, :], d_ps[0:TT, 0, 0:ST * D], ACT.Copy).then_inc(h_ready, 1)
                    act.wait_ge(h_ready, b + 1)
                    act.sem_inc(d_free, 1)

                part_p = {"xT": take_xT,
                          "q_first": round_part("q", 1, qst[:, :, 0, :], q_in[:, :, :], "g1"),
                          "q_second": round_part("q", 2, qst[:, :, 3, :], q_rest[:, :, :], "g1"),
                          "k_first": round_part("k", 1, kst[:, :, 0, :], kf[:, :, :], "kt3"),
                          "k_second": round_part("k", 2, kst[:, :, 1, :], k_rest[:, :, :], "kt3")}
                part_a = {"g0": take_qT(0), "g1": take_qT(1), "au": take_pv}
                for i in ACT_KT:
                    part_a[f"kt{i}"] = take_kT(i)
                for h in range(H):
                    part_a[f"s{h}"] = exps(h)
                part_d = {"attT": take_sc, "o": take_o, "c1": take_c(1), "m1": take_m(1)}
                part_e = {"c2": take_c(2), "m2": take_m(2), "relu": relu_h, "ht": take_h}
                for i in ACT_F:
                    part_d[f"f{i}"] = take_f(i)
                def hand_on(name, b):
                    if name in D_TILES:
                        act.wait_ge(d_done, d_count(name, b))
                        act.sem_inc(d_free, 1)
                    elif name != "k":
                        await_a(act, a_done, name, b)
                        act.sem_inc(a_free[a_slot(name)], 1)

                run(act, part_p, part_a, part_d, part_e, hand_on)

            @block.vector
            def _(dve):
                def one_hots(part):
                    def go(b, pb):
                        if part == 0:
                            dve.tensor_copy(rank_cur[:, :, :], t["rank_tok"][:, :, bass.ds(b * H, H)]).then_inc(cur_ready, 1)
                            dve.wait_ge(cur_ready, b + 1)
                            await_a(dve, a_done, "g1", b - 1)
                        for h in range(H):
                            ins = dve.tensor_scalar(G[:, part, h, :], iota_bf[:, :], rank_cur[:, part, h:h + 1], None, ALU.is_equal)
                        if part == NT - 1:
                            ins.then_inc(g_ready, 1)
                    return go

                def slot_rows(b, pb):
                    dve.wait_ge(rank_loaded, 16 * b + 16)
                    wait_before(dve, d_done, d_count("sc", b - 1))
                    for jt in range(2):
                        ins = dve.tensor_scalar(GT[:, jt, :], rank_bc[:, :], slot_id[:, jt:jt + 1], None, ALU.is_equal)
                    ins.then_inc(gt_ready, 1)

                def take_k(b, pb):
                    await_a(dve, a_done, "k", b)
                    wait_before(dve, reduced["k"], 2 * b - 1)
                    dve.tensor_tensor(kf[:, :, :].rearrange("p (a n h) d -> p a n (h d)", a=2, n=3), two_of_three(a_tile("k"), D),
                                      kvb[:, 0:D].unsqueeze(1).unsqueeze(1).to_broadcast([TT, 2, 3, D]), ALU.add)\
                       .then_inc(a_free[a_slot("k")], 1)

                def take_v(b, pb):
                    await_a(dve, a_done, "v", b)
                    wait_before(dve, pv_done[1], b)
                    for a in range(2):
                        for odd in range(2):
                            ins = dve.tensor_tensor(
                                v_pad[:, 3 * a:3 * a + 3, odd:H:2, HD * odd:HD * odd + HD],
                                a_tile("v")[0:TT, a, 0:3 * D].rearrange("p (n h d) -> p n h d", n=3, h=H)[:, :, odd:H:2, :],
                                kvb[:, D:2 * D].rearrange("p (h d) -> p h d", h=H)[:, odd:H:2, :].unsqueeze(1)
                                .to_broadcast([TT, 3, H // 2, HD]), ALU.add)
                    ins.then_inc(a_free[a_slot("v")], 1)

                def take_kT(i):
                    def go(b, pb):
                        await_a(dve, a_done, f"kt{i}", b)
                        dve.tensor_copy(kT[0:KR, 2 * i:2 * i + 2, :].rearrange("p g (n c) -> p g n c", n=NT), turned_k(i))\
                           .then_inc(a_free[a_slot(f"kt{i}")], 1)
                    return go

                def take_max(i):
                    def go(b, pb):
                        await_a(dve, a_done, f"max{i}", b)
                        dve.tensor_reduce(mx[:, i:i + 1], a_tile(f"max{i}")[0:JT, :, 0:HALF], AX.XY, ALU.max)\
                           .then_inc(a_free[a_slot(f"max{i}")], 1)
                    return go

                def max_parts(b, pb):
                    await_a(dve, a_free, f"max{2 * H - 2}", b)
                    await_a(dve, a_free, f"max{2 * H - 1}", b)
                    dve.tensor_copy(mxp[:, 0, :], mx[:, :]).then_inc(mx_step, 1)
                    dve.wait_ge(mx_step, 3 * b + 1)
                    dve.tensor_tensor(mx_rest[:, :], mx[:, :], mxp[:, 0, :], ALU.subtract).then_inc(mx_step, 1)
                    dve.wait_ge(mx_step, 3 * b + 2)
                    dve.tensor_copy(mxp[:, 1, :], mx_rest[:, :]).then_inc(mx_step, 1)
                    dve.wait_ge(mx_step, 3 * b + 3)
                    dve.tensor_tensor(mxp[:, 2, :], mx_rest[:, :], mxp[:, 1, :], ALU.subtract).then_inc(mxp_ready, 1)

                def take_max_rows(b, pb):
                    await_a(dve, a_done, "mt", b)
                    dve.tensor_copy(mxT[:, :], a_tile("mt")[0:6 * H, 0, 0:JT // 2].bitcast(BF16)).then_inc(mxT_ready, 1)
                    dve.wait_ge(mxT_ready, b + 1)
                    dve.sem_inc(a_free[a_slot("mt")], 1)

                def take_att(b, pb):
                    dve.wait_ge(at_done, b + 1)
                    at = at_ps[0:JT, :].rearrange("p (s g d) -> p s g d", s=4, g=4)
                    to = att[:, :].rearrange("p (s g d) -> p s g d", s=4, g=4)
                    for odd in range(2):
                        dve.reciprocal(rden[:, :, odd:4:2], at[:, :, odd:4:2, HD * (1 - odd)]).then_inc(att_step, 1)
                    dve.wait_ge(att_step, 7 * b + 2)
                    for odd in range(2):
                        half = slice(HD * odd, HD * odd + HD)
                        dve.tensor_tensor(to[:, :, odd:4:2, half], at[:, :, odd:4:2, half],
                                          rden[:, :, odd:4:2].unsqueeze(3).to_broadcast([JT, 4, 2, HD]), ALU.mult)\
                           .then_inc(att_step, 1)
                    dve.wait_ge(att_step, 7 * b + 4)
                    dve.tensor_copy(attp[:, 0, :], att[:, :]).then_inc(att_step, 1)
                    dve.wait_ge(att_step, 7 * b + 5)
                    dve.tensor_tensor(att_rest[:, :], att[:, :], attp[:, 0, :], ALU.subtract).then_inc(att_step, 1)
                    dve.wait_ge(att_step, 7 * b + 6)
                    dve.tensor_copy(attp[:, 1, :], att_rest[:, :]).then_inc(att_step, 1)
                    dve.wait_ge(att_step, 7 * b + 7)
                    dve.tensor_tensor(attp[:, 2, :], att_rest[:, :], attp[:, 1, :], ALU.subtract).then_inc(attp_ready, 1)

                def copy_k(b, pb):
                    dve.wait_ge(rounded["k"], 2 * b + 2)
                    for src, to in K_COPIES:
                        ins = dve.tensor_copy(kst[:, :, to, :], kst[:, :, src, :])
                    ins.then_inc(copied["k"], 1)

                def residual1(b, pb):
                    dve.wait_ge(d_free, d_count("o", b))
                    dve.tensor_tensor(r[:, :], ao[:, :], xT[pb][:, :], ALU.add).then_inc(r_ready, 1)

                def norm1(b, pb):
                    dve.wait_ge(rstd_ready, 2 * b + 1)
                    dve.tensor_tensor(cS[:, :], cS[:, :], sq[:, :], ALU.mult).then_inc(ln_step, 1)
                    dve.wait_ge(ln_step, 2 * b + 1)
                    dve.tensor_scalar(h1[:, :], cS[:, :], col("ln1_g"), col("ln1_b"), ALU.mult, ALU.add).then_inc(h1_ready, 1)

                def take_f(i):
                    def go(b, pb):
                        dve.wait_ge(d_done, d_count(f"f{i}", b))
                        dve.tensor_scalar(two(rl[:, i, :]), d_ps[:, :, 0:HALF], col(f"f1_b{i}"), 0.0, ALU.add, ALU.max)\
                           .then_inc(d_free, 1)
                    return go

                def residual2(b, pb):
                    dve.wait_ge(d_done, d_count("ff", b))
                    dve.scalar_tensor_tensor(two(r[:, :]), d_ps[:, :, 0:HALF], col("f2_b"), two(h1[:, :]), ALU.add, ALU.add)\
                       .then_inc(d_free, 1)
                    dve.wait_ge(d_free, d_count("ff", b))
                    dve.sem_inc(r_ready, 1)

                def norm2(b, pb):
                    dve.wait_ge(rstd_ready, 2 * b + 2)
                    dve.tensor_tensor(cS[:, :], cS[:, :], sq[:, :], ALU.mult).then_inc(ln_step, 1)
                    dve.wait_ge(ln_step, 2 * b + 2)
                    dve.wait_ge(aob_ready, b + 1)
                    dve.scalar_tensor_tensor(fu[:, 1:L + 1], cS[:, :], col("ln2_g"), aob[:, :], ALU.mult, ALU.add)\
                       .then_inc(fu_ready, 1)

                def pool_pairs(b, pb):
                    dve.wait_ge(d_done, d_count("cv", b))
                    n = (HALF + 1) // 2
                    dve.tensor_reduce(hp[:, 0:n], d_ps[:, 0, 0:2 * n].rearrange("p (s w) -> p s w", w=2), AX.X, ALU.max)\
                       .then_inc(hp_ready, 1)
                    dve.tensor_reduce(hp[:, n:S], d_ps[:, 1, 0:2 * (S - n)].rearrange("p (s w) -> p s w", w=2), AX.X, ALU.max)\
                       .then_inc(hp_ready, 1)
                    dve.wait_ge(hp_ready, 2 * b + 2)
                    dve.sem_inc(d_free, 1)

                part_p = {"k": take_k, "v_pad": take_v, 
                          "k_copy": copy_k}
                for i in range(NT):
                    part_p[f"hot{i}"] = one_hots(i)
                part_a = {"gt": slot_rows, "mp": max_parts, "mt": take_max_rows}
                for i in range(4):
                    if i not in ACT_KT:
                        part_a[f"kt{i}"] = take_kT(i)
                for i in range(2 * H):
                    part_a[f"max{i}"] = take_max(i)
                part_d = {"at": take_att, "r1": residual1, "n1": norm1, "r2": residual2}
                part_e = {"n2": norm2, "pool": pool_pairs}
                for i in range(4):
                    if i not in ACT_F:
                        part_d[f"f{i}"] = take_f(i)
                def hand_on(name, b):
                    if name == "k":
                        await_a(dve, a_done, name, b)
                        dve.sem_inc(a_free[a_slot(name)], 1)

                run(dve, part_p, part_a, part_d, part_e, hand_on)


ACT_KT = ()
ACT_F = (0, 1, 2, 3)
K_COPIES = ((0, 3), (0, 5), (1, 4))
Q_COPIES = ((0, 1), (0, 2), (3, 4))


def order():
    text = """P.load A.kt0 A.kt1 E.c2 A.kt2 E.m2 A.kt3 A.g0 E.n2 D.at A.g1 P.q_rest A.max0 A.max1 E.relu
        P.q_first E.cv A.max2 P.q_second P.q_third P.q_copy A.max3 E.cv1 E.pool A.max4 A.max5 D.sc A.max6 A.max7
        D.sc1 A.max8 A.max9 D.sc2 A.max10 A.max11 D.sc3 D.attT A.max12 A.max13 E.ht A.max14 A.max15 D.o A.mp
        D.r1 A.mt D.c1 P.hot0 P.hot1 P.k_rest P.xT D.m1 P.k_first P.k D.n1 A.s0 A.s1 P.k_third P.hot_pool
        P.k_second D.f0 A.s2 P.hot2 A.s3 D.f1 P.hot3 P.k_copy A.s4 A.pv0 P.hot4 P.hot5 D.f2 A.s5 A.s6 D.f3 A.s7
        D.ff A.gt P.ranks A.pv1 P.v_pad A.au D.r2 P.v"""
    return [tuple(s.split(".")) for s in text.split()]


def tanh_attention(nc, t, io):
    BUFS = 4
    with ExitStack() as ctx:
        def sb(name, shape, dt=F32):
            return ctx.enter_context(nc.sbuf_tensor(name, shape, dt))

        def sem(name):
            return ctx.enter_context(nc.semaphore(name))

        aw = sb("attention_w", [D, D])
        wr = sb("router_w", [D, E])
        brc = sb("router_b_rows", [TT, E])
        minus_half = sb("minus_half", [TT, ST])
        h_in = [sb(f"h_in{p}", [TT, ST, D]) for p in range(BUFS)]
        z = [sb(f"z{p}", [TT, ST, D + 1]) for p in range(BUFS)]
        rows = [sb(f"rows{p}", [TT, ST, 2 * D]) for p in range(BUFS)]
        zero_row = sb("zero_row", [1, 2 * D])
        stats = [sb(f"ln_stats{k}", [TT, ST, 6]) for k in range(2)]
        mv = [sb(f"ln_mv{k}", [TT, ST, 2]) for k in range(2)]
        ve = [sb(f"ln_ve{k}", [TT, ST]) for k in range(2)]
        rs = [sb(f"ln_rs{k}", [TT, ST]) for k in range(2)]
        zT = [sb(f"zT{p}", [D, S]) for p in range(2)]
        pT = sb("pT", [D, S])
        th = sb("tanh_s", [TT, ST, S])
        ex = [sb(f"exp_s{p}", [TT, ST, S]) for p in range(2)]
        rden = sb("rden4", [TT, ST])
        uT = sb("uT4", [D, S])
        zT_ps = ctx.enter_context(nc.psum_tensor("zT_ps", [128, 512], F32))
        pT_ps = ctx.enter_context(nc.psum_tensor("pT_ps", [128, 512], F32))
        s_ps = ctx.enter_context(nc.psum_tensor("s_ps", [128, ST, 512], F32))
        o_ps = ctx.enter_context(nc.psum_tensor("o_ps4", [128, 512], F32))
        uT_ps = ctx.enter_context(nc.psum_tensor("uT_ps", [128, 512], F32))
        l_ps = ctx.enter_context(nc.psum_tensor("l_ps", [128, 512], F32))

        names = ["w4", "set4", "zT_done", "zT_ready", "pT_done", "pT_ready", "s_done", "th_ready", "ex_ready", "o_done",
                 "rden_ready", "hh_ready", "uT_done", "uT_ready", "l_done", "l_ready"]
        w4, set4, zT_done, zT_ready, pT_done, pT_ready, s_done, th_ready, ex_ready, o_done, rden_ready, hh_ready, uT_done, \
            uT_ready, l_done, l_ready = [sem(n) for n in names]
        gate4 = sem("gate4")
        h_loaded = [sem(f"h_loaded4{p}") for p in range(BUFS)]
        st_ready = [sem(f"st_ready{k}") for k in range(2)]
        mv_ready = [sem(f"mv_ready{k}") for k in range(2)]
        ve_ready = [sem(f"ve_ready{k}") for k in range(2)]
        rs_ready = [sem(f"rs_ready{k}") for k in range(2)]
        n_ready = [sem(f"n_ready4{k}") for k in range(2)]
        rows_stored = [sem(f"rows_stored{p}") for p in range(BUFS)]
        zero_made = sem("zero_made")
        logits = t["logits"]
        rows_v = io["token_rows"][1:1 + NB * S, :].rearrange("(b n p) d -> b p n d", n=ST, p=TT)

        def run(eng, steps):
            rounds(eng, steps, NB, BUFS, 2)

        with nc.Block() as block:
            @block.sync
            def _(sp):
                sp.dma_start(aw[:, :], io["L0_attn_attention_weights"]).then_inc(w4, 16)
                sp.dma_start(wr[:, :], io["L0_ffn_Wr"]).then_inc(w4, 16)
                sp.dma_start(brc[:, :], io["L0_ffn_br"].rearrange("(a n) -> a n", a=1).to_broadcast([TT, E])).then_inc(w4, 16)

                def load(b, p, j):
                    wait_before(sp, hh_ready, ST * (b - BUFS + 1))
                    sp.dma_start(h_in[p][:, :, :].rearrange("p n d -> p (n d)"),
                                 io["h_rows"][bass.ds(b, 1), :, :].rearrange("b p n -> (b p) n")).then_inc(h_loaded[p], 16)

                def store(b, p, j):
                    sp.wait_ge(n_ready[1], b + 1)
                    sp.dma_start(rows_v[bass.ds(b, 1), :, :, :].rearrange("b p n d -> (b p) n d"), rows[p][:, :, :]).then_inc(rows_stored[p], 16)

                def load_expert(b, p, j):
                    assert BUFS == 4 and NB == 2 * E
                    e = 2 * j + p // 2
                    if p % 2 == 0:
                        pieces = [(t["w1"][:, bass.ds(e, 1), :].rearrange("d e h -> d (e h)"),
                                   io["L0_ffn_W1"][bass.ds(e, 1), :, :].rearrange("e d h -> (e d) h")),
                                  (t["b1"][:, bass.ds(e * EH, EH)], io["L0_ffn_b1"][bass.ds(e, 1), :].to_broadcast([128, EH]))]
                    else:
                        pieces = [(t["w2"][:, bass.ds(e * (EH // 128), EH // 128), :],
                                   io["L0_ffn_W2"][bass.ds(e, 1), :, :].rearrange("e (c p) d -> p (e c) d", p=128)),
                                  (t["b2"][:, bass.ds(e * D, D)], io["L0_ffn_b2"][bass.ds(e, 1), :].to_broadcast([128, D]))]
                    for dst, src in pieces:
                        sp.dma_start(dst, src).then_inc(t["experts_loaded"], 16)

                sp.wait_ge(zero_made, 1)
                sp.dma_start(io["token_rows"][0:1, :], zero_row[:, :]).then_inc(zero_made, 16)
                for p in range(BUFS):
                    sp.sem_inc(rows_stored[p], 16)
                run(sp, [(4, load), (0, load_expert), (-1, store)])
                sp.wait_ge(zero_made, 17)
                for p in range(BUFS):
                    sp.wait_ge(rows_stored[p], 16 * (NB // BUFS) + 16)

            @block.gpsimd
            def _(pool):
                pool.memset(zero_row[:, :], 0.0).then_inc(zero_made, 1)
                pool.memset(minus_half[:, :], -0.5).then_inc(set4, 1)
                pool.wait_ge(set4, 1)

                def power(k):
                    def go(b, p, j):
                        pool.wait_ge(ve_ready[k], b + 1)
                        pool.tensor_tensor(rs[k][:, :], ve[k][:, :], minus_half[:, :], ALU.pow).then_inc(rs_ready[k], 1)
                    return go

                run(pool, [(3, power(0)), (0, power(1))])

            @block.tensor
            def _(pe):
                pe.wait_ge(w4, 48)

                def turn_z(b, p, j):
                    pe.wait_ge(n_ready[0], b + 1)
                    for n in range(ST):
                        mm = pe.transpose(zT_ps[:, n * TT:(n + 1) * TT], z[p][:, n, 0:D], t["ident"][0:TT, 0:TT])
                    mm.then_inc(zT_done, 1)

                def project(b, p, j):
                    pe.wait_ge(zT_ready, b + 1)
                    pe.matmul(pT_ps[:, 0:S], aw[:, :], zT[p % 2][:, :], start=True, stop=True).then_inc(pT_done, 1)

                def scores(b, p, j):
                    pe.wait_ge(pT_ready, b + 1)
                    wait_before(pe, th_ready, b)
                    for n in range(ST):
                        mm = pe.matmul(s_ps[0:TT, n, 0:S], zT[p % 2][:, n * TT:(n + 1) * TT], pT[:, :], start=True, stop=True)
                    mm.then_inc(s_done, 1)

                def attend(b, p, j):
                    pe.wait_ge(ex_ready, b + 1)
                    wait_before(pe, hh_ready, ST * b)
                    for m in range(ST):
                        for n in range(ST):
                            mm = pe.matmul(o_ps[0:TT, m * (D + 1):(m + 1) * (D + 1)], ex[p % 2][:, n, m * TT:(m + 1) * TT],
                                           z[p][:, n, :], start=(n == 0), stop=(n == ST - 1))
                    mm.then_inc(o_done, 1)

                def turn_u(b, p, j):
                    pe.wait_ge(n_ready[1], b + 1)
                    for n in range(ST):
                        mm = pe.transpose(uT_ps[:, n * TT:(n + 1) * TT], rows[p][:, n, 0:D], t["ident"][0:TT, 0:TT])
                    mm.then_inc(uT_done, 1)

                def router(b, p, j):
                    pe.wait_ge(uT_ready, b + 1)
                    pe.wait_ge(l_ready, b + 1)
                    for n in range(ST):
                        mm = pe.matmul(l_ps[0:TT, n * E:(n + 1) * E], uT[:, n * TT:(n + 1) * TT], wr[:, :], start=True, stop=True)
                    mm.then_inc(l_done, 1)

                run(pe, [(1, project), (2, turn_z), (-2, turn_u), (0, attend), (1, scores), (-2, router)])

            @block.scalar
            def _(act):
                def take_z(b, p, j):
                    act.wait_ge(zT_done, b + 1)
                    act.activation(zT[p % 2][:, :], zT_ps[:, 0:S], ACT.Copy).then_inc(zT_ready, 1)

                def exps(b, p, j):
                    act.wait_ge(s_done, b + 1)
                    act.activation(th[:, :, :], s_ps[0:TT, :, 0:S], ACT.Tanh).then_inc(th_ready, 1)
                    act.wait_ge(th_ready, b + 1)
                    act.activation(ex[p % 2][:, :, :], th[:, :, :], ACT.Exp).then_inc(ex_ready, 1)

                def take_u(b, p, j):
                    act.wait_ge(uT_done, b + 1)
                    act.activation(uT[:, :], uT_ps[:, 0:S], ACT.Copy).then_inc(uT_ready, 1)

                run(act, [(2, take_z), (-2, take_u), (1, exps)])

            @block.vector
            def _(dve):
                for p in range(BUFS):
                    dve.memset(z[p][:, :, D:D + 1], 1.0).then_inc(t["z_set"], 1)
                dve.sem_inc(l_ready, 1)
                dve.wait_ge(t["z_set"], BUFS)
                dve.wait_ge(w4, 48)

                def variance(k, src, b):
                    for n in range(ST):
                        dve.bn_stats(stats[k][:, n, :], src(n)).then_inc(st_ready[k], 1)
                    dve.wait_ge(st_ready[k], ST * b + ST)
                    dve.sem_inc(gate4, 1)
                    for n in range(ST):
                        dve.bn_aggr(mv[k][:, n, :], stats[k][:, n, :]).then_inc(mv_ready[k], 1)
                    dve.wait_ge(mv_ready[k], ST * b + ST)
                    dve.tensor_scalar(ve[k][:, :], mv[k][:, :, 1], EPS, None, ALU.add).then_inc(ve_ready[k], 1)

                def normalize(k, src, dst, b):
                    dve.wait_ge(rs_ready[k], b + 1)
                    for n in range(ST):
                        ins = dve.tensor_scalar(dst(n), src(n), mv[k][:, n, 0:1], rs[k][:, n:n + 1], ALU.subtract, ALU.mult)
                    ins.then_inc(n_ready[k], 1)

                def h_variance(b, p, j):
                    dve.wait_ge(h_loaded[p], 16 * j + 16)
                    variance(0, lambda n: h_in[p][:, n, :], b)

                def z_rows(b, p, j):
                    normalize(0, lambda n: h_in[p][:, n, :], lambda n: z[p][:, n, 0:D], b)

                def take_p(b, p, j):
                    dve.wait_ge(pT_done, b + 1)
                    dve.tensor_copy(pT[:, :], pT_ps[:, 0:S]).then_inc(pT_ready, 1)

                def residual(b, p, j):
                    dve.wait_ge(o_done, b + 1)
                    o = o_ps[0:TT, 0:ST * (D + 1)].rearrange("p (n d) -> p n d", n=ST)
                    dve.reciprocal(rden[:, :], o[:, :, D]).then_inc(rden_ready, 1)
                    dve.wait_ge(rden_ready, b + 1)
                    dve.wait_ge(rows_stored[p], 16 * j + 16)
                    for n in range(ST):
                        dve.scalar_tensor_tensor(rows[p][:, n, D:2 * D], o[:, n, 0:D], rden[:, n:n + 1], h_in[p][:, n, :], ALU.mult, ALU.add)\
                            .then_inc(hh_ready, 1)
                    dve.wait_ge(hh_ready, ST * b + ST)
                    variance(1, lambda n: rows[p][:, n, D:2 * D], b)

                def u_rows(b, p, j):
                    normalize(1, lambda n: rows[p][:, n, D:2 * D], lambda n: rows[p][:, n, 0:D], b)

                def take_logits(b, p, j):
                    dve.wait_ge(l_done, b + 1)
                    dve.tensor_tensor(logits[:, bass.ds(b * ST, ST), :], l_ps[0:TT, 0:ST * E].rearrange("p (n e) -> p n e", n=ST),
                                      brc[:, :].unsqueeze(1).to_broadcast([TT, ST, E]), ALU.add).then_inc(l_ready, 1)

                run(dve, [(1, take_p), (-1, u_rows), (3, h_variance), (0, residual), (3, z_rows), (-2, take_logits)])


def route(nc, t, io):
    with ExitStack() as ctx:
        def sb(name, shape, dt=F32):
            return ctx.enter_context(nc.sbuf_tensor(name, shape, dt))

        def sem(name):
            return ctx.enter_context(nc.semaphore(name))

        top = sb("top_logit", [TT, NTILE])
        hot = sb("hot", [TT, NTILE, E])
        pick = sb("pick", [TT, NTILE, E])
        best = sb("best", [TT, NTILE])
        e_id = sb("e_id", [TT, E])
        upper = sb("upper", [TT, TT])
        ones = sb("ones5", [TT, TT])
        ones_t = sb("ones_t", [TT, NTILE])
        total = sb("total", [TT, NTILE, E])
        cum = sb("cum", [TT, E, NTILE])
        blk_row = sb("blk_row", [TT, NBLK])
        full = sb("full", [TT, E, NBLK])
        nblk = sb("nblk", [TT, E])
        bend = sb("bend", [TT, E])
        bstart = sb("bstart", [TT, E])
        past = sb("past", [TT, NBLK, E])
        owner = sb("owner", [TT, NBLK])
        slot = sb("slot_f", [TT, NTILE])
        first = sb("first_slot", [TT, NTILE])
        slot_row = sb("slot_row", [TT, BLK])
        row_id = sb("row_id", [TT, NTILE])
        is_slot = sb("is_slot", [TT, NTILE, BLK])
        in_block = sb("in_block", [TT, NTILE, 2, NBLK])
        rows_f = sb("rows_f", [BLK, NBLK])
        dest_f = sb("dest_f", [BLK, NBLK])
        gate = sb("gate_tok", [TT, NTILE])
        i_ps = ctx.enter_context(nc.psum_tensor("i_ps", [128, 512], F32))
        p_ps = ctx.enter_context(nc.psum_tensor("p_ps", [128, 512], F32))
        t_ps = ctx.enter_context(nc.psum_tensor("t_ps", [128, 512], F32))
        const5 = sem("const5")
        hot_ready = sem("hot_ready")
        counted = sem("counted")
        diff_ready = sem("diff_ready")
        gate_exp = sem("gate_exp")
        step5 = sem("step5")
        hot_slots = sem("hot_slots")
        inverted = sem("inverted")

        with nc.Block() as block:
            @block.sync
            def _(sp):
                sp.dma_start(e_id[:, :], io["c_e_id"].to_broadcast([TT, E])).then_inc(const5, 16)
                sp.dma_start(upper[:, :], io["c_upper"]).then_inc(const5, 16)
                sp.dma_start(blk_row[:, :], io["c_blk"].to_broadcast([TT, NBLK])).then_inc(const5, 16)
                sp.dma_start(slot_row[:, :], io["c_slot_row"].to_broadcast([TT, BLK])).then_inc(const5, 16)
                sp.dma_start(row_id[:, :], io["c_row_id"]).then_inc(const5, 16)

            @block.scalar
            def _(act):
                act.wait_ge(diff_ready, 1)
                act.activation(gate[:, :], best[:, :], ACT.Exp).then_inc(gate_exp, 1)

            @block.tensor
            def _(pe):
                pe.wait_ge(const5, 80)
                pe.wait_ge(hot_ready, 1)
                m = hot[:, :, :].rearrange("p t e -> p (t e)")
                pe.matmul(p_ps[0:TT, 0:NTILE * E], upper[:, :], m, start=True, stop=True)
                pe.matmul(t_ps[0:TT, 0:NTILE * E], ones[:, :], m, start=True, stop=True).then_inc(counted, 1)
                for n in range(NTILE):
                    if n % (NTILE // CUTS) == 0:
                        pe.wait_ge(hot_slots, n // (NTILE // CUTS) + 1)
                    mm = pe.matmul(i_ps[0:BLK, 0:2 * NBLK], is_slot[:, n, :], in_block[:, n, :, :].rearrange("p a j -> p (a j)"),
                                   start=(n == 0), stop=(n == NTILE - 1))
                mm.then_inc(inverted, 1)

            @block.vector
            def _(dve):
                n_step = [0]

                def chain(ins):
                    n_step[0] += 1
                    ins.then_inc(step5, 1)
                    dve.wait_ge(step5, n_step[0])

                def tiles(ap):
                    return ap.unsqueeze(2).to_broadcast([TT, NTILE, E])

                def experts(ap, n=NTILE):
                    return ap.unsqueeze(1).to_broadcast([TT, n, E])

                chain(dve.memset(ones[:, :], 1.0))
                chain(dve.memset(ones_t[:, :], 1.0))
                dve.wait_ge(const5, 80)
                chain(dve.tensor_reduce(top[:, :], t["logits"][:, :, :], AX.X, ALU.max))
                dve.tensor_tensor(best[:, :], top[:, :], top[:, :], ALU.subtract).then_inc(diff_ready, 1)
                dve.wait_ge(gate_exp, 1)
                chain(dve.reciprocal(best[:, :], gate[:, :]))
                chain(dve.tensor_tensor(gate[:, :], gate[:, :], best[:, :], ALU.mult))
                chain(dve.tensor_tensor(pick[:, :, :], t["logits"][:, :, :], tiles(top[:, :]), ALU.is_equal))
                chain(dve.tensor_tensor(pick[:, :, :], pick[:, :, :], experts(e_id[:, :]), ALU.mult))
                chain(dve.tensor_reduce(best[:, :], pick[:, :, :], AX.X, ALU.max))
                dve.tensor_tensor(hot[:, :, :], experts(e_id[:, :]), tiles(best[:, :]), ALU.is_equal).then_inc(hot_ready, 1)
                dve.wait_ge(counted, 1)
                chain(dve.tensor_copy(total[:, :, :].rearrange("p t e -> p (t e)"), t_ps[0:TT, 0:NTILE * E]))
                for e in range(E):
                    chain(dve.tensor_tensor_scan(cum[:, e, :], ones_t[:, :], total[:, :, e], 0.0, ALU.mult, ALU.add))
                chain(dve.tensor_scalar(full[:, 0, :], blk_row[:, :], float(BLK), None, ALU.mult))
                chain(dve.tensor_copy(owner[:, :], full[:, 0, :]))
                chain(dve.tensor_tensor(full[:, :, :], cum[:, :, NTILE - 1:NTILE].to_broadcast([TT, E, NBLK]),
                                        owner[:, :].unsqueeze(1).to_broadcast([TT, E, NBLK]), ALU.is_gt))
                chain(dve.tensor_reduce(nblk[:, :], full[:, :, :], AX.X, ALU.add))
                chain(dve.tensor_tensor_scan(bend[:, :], ones_t[:, 0:E], nblk[:, :], 0.0, ALU.mult, ALU.add))
                chain(dve.tensor_tensor(bstart[:, :], bend[:, :], nblk[:, :], ALU.subtract))
                chain(dve.tensor_scalar(bstart[:, :], bstart[:, :], float(BLK), None, ALU.mult))
                chain(dve.tensor_tensor(past[:, :, :], blk_row[:, :].unsqueeze(2).to_broadcast([TT, NBLK, E]),
                                        experts(bend[:, :], NBLK), ALU.is_ge))
                chain(dve.tensor_reduce(owner[:, :], past[:, :, :], AX.X, ALU.add))
                chain(dve.tensor_scalar(t["block_expert"][:, :], owner[:, :], float(E - 1), None, ALU.min))
                chain(dve.tensor_tensor(pick[:, :, :], cum[:, :, :].rearrange("p e t -> p t e"), total[:, :, :], ALU.subtract))
                chain(dve.tensor_tensor(pick[:, :, :], pick[:, :, :], experts(bstart[:, :]), ALU.add))
                chain(dve.tensor_tensor(pick[:, :, :], pick[:, :, :], p_ps[0:TT, 0:NTILE * E].rearrange("p (t e) -> p t e", e=E),
                                        ALU.add))
                chain(dve.tensor_tensor(pick[:, :, :], pick[:, :, :], hot[:, :, :], ALU.mult))
                chain(dve.tensor_reduce(slot[:, :], pick[:, :, :], AX.X, ALU.add))
                chain(dve.tensor_scalar(first[:, :], slot[:, :], 1.0 / BLK, -0.5 + 0.5 / BLK, ALU.mult, ALU.add))
                chain(dve.tensor_scalar(first[:, :], first[:, :], ROUNDER, None, ALU.add))
                chain(dve.tensor_scalar(first[:, :], first[:, :], -ROUNDER, float(BLK), ALU.add, ALU.mult))
                chain(dve.tensor_tensor(slot[:, :], slot[:, :], first[:, :], ALU.subtract))
                chain(dve.tensor_scalar(blk_row[:, :], blk_row[:, :], float(BLK), None, ALU.mult))
                for c in range(CUTS):
                    n = NTILE // CUTS
                    at = slice(c * n, (c + 1) * n)
                    dve.tensor_tensor(is_slot[:, at, :], slot_row[:, :].unsqueeze(1).to_broadcast([TT, n, BLK]),
                                      slot[:, at].unsqueeze(2).to_broadcast([TT, n, BLK]), ALU.is_equal)
                    chain(dve.tensor_tensor(in_block[:, at, 0, :], blk_row[:, :].unsqueeze(1).to_broadcast([TT, n, NBLK]),
                                            first[:, at].unsqueeze(2).to_broadcast([TT, n, NBLK]), ALU.is_equal))
                    dve.tensor_tensor(in_block[:, at, 1, :], in_block[:, at, 0, :],
                                      gate[:, at].unsqueeze(2).to_broadcast([TT, n, NBLK]), ALU.mult)
                    dve.tensor_tensor(in_block[:, at, 0, :], in_block[:, at, 0, :],
                                      row_id[:, at].unsqueeze(2).to_broadcast([TT, n, NBLK]), ALU.mult).then_inc(hot_slots, 1)
                dve.wait_ge(inverted, 1)
                chain(dve.tensor_copy(rows_f[:, :], i_ps[0:BLK, 0:NBLK]))
                dve.tensor_copy(t["gate"][:, :], i_ps[0:BLK, NBLK:2 * NBLK])
                dve.tensor_copy(t["row"][:, :], rows_f[:, :])
                chain(dve.tensor_scalar(dest_f[:, :], rows_f[:, :], 0.0, float(2 * NB * S), ALU.is_equal, ALU.mult))
                chain(dve.tensor_tensor(dest_f[:, :], dest_f[:, :], rows_f[:, :], ALU.add))
                dve.tensor_scalar(t["dest"][:, :], dest_f[:, :], -1.0, None, ALU.add)


def experts(nc, t, io):
    NC = EH // 128
    BODY = 6
    UB, OB = BODY, 3
    AHEAD = 4
    assert NBLK % BODY == 0
    with ExitStack() as ctx:
        def sb(name, shape, dt=F32):
            return ctx.enter_context(nc.sbuf_tensor(name, shape, dt))

        def sem(name):
            return ctx.enter_context(nc.semaphore(name))

        w1, w2, b1, b2 = t["w1"], t["w2"], t["b1"], t["b2"]
        rows = [sb(f"block_rows{p}", [BLK, 2 * D]) for p in range(UB)]
        uT = [sb(f"uT_block{p}", [D, BLK]) for p in range(2)]
        hb = [sb(f"h_block{p}", [BLK, EH]) for p in range(2)]
        hT = [sb(f"hT_block{p}", [128, NC, BLK]) for p in range(2)]
        ob = sb("o_block", [BLK, D])
        gated = sb("gated_block", [BLK, D])
        res = [sb(f"result{p}", [BLK, D]) for p in range(OB)]
        uT_ps = [ctx.enter_context(nc.psum_tensor(f"uTb_ps{p}", [128, 512], F32)) for p in range(2)]
        h_ps = [ctx.enter_context(nc.psum_tensor(f"h_ps{p}", [128, 512], F32)) for p in range(2)]
        hT_ps = [ctx.enter_context(nc.psum_tensor(f"hT_ps{p}", [128, 512], F32)) for p in range(2)]
        o_ps = [ctx.enter_context(nc.psum_tensor(f"ob_ps{p}", [128, 512], F32)) for p in range(2)]
        gathered = [sem(f"gathered{p}") for p in range(UB)]
        u_turned = sem("u_turned6")
        uT_ready = sem("uT_ready6")
        h_done = sem("h_done6")
        h_ready = sem("h_ready6")
        h_turned = sem("h_turned6")
        hT_ready = sem("hT_ready6")
        o_done = sem("o_done6")
        o_ready = sem("o_ready6")
        gated_ready = sem("gated_ready6")
        res_ready = sem("res_ready6")
        scattered = [sem(f"scattered{p}") for p in range(OB)]

        def run(eng, steps):
            rounds(eng, steps, NBLK, BODY, OB)

        def first_use(eng, held, j, m):
            e = eng.value_load(t["block_expert"][0:1, bass.ds(j, 1)], min_val=0, max_val=E - 1)
            held.append((isinstance(m, int), e))
            return e

        def second_use(eng, held, j, m):
            straight, e = held.pop(0)
            if straight != isinstance(m, int):
                e = eng.value_load(t["block_expert"][0:1, bass.ds(j, 1)], min_val=0, max_val=E - 1)
            return e

        out_rows = io["out"].rearrange("b s d -> (b s) d")

        with nc.Block() as block:
            @block.gpsimd
            def _(pool):
                for r in range(-AHEAD, NBLK):
                    j = r + AHEAD
                    if j < NBLK:
                        wait_before(pool, res_ready, j - UB + 1)
                        pool.indirect_dma_start(out=rows[j % UB][:, :], out_offset=None, in_=io["token_rows"],
                                                in_offset=bass.IndirectOffsetOnAxis(ap=t["row"][:, j:j + 1], axis=0))\
                            .then_inc(gathered[j % UB], 16)
                    if r >= 0:
                        pool.wait_ge(res_ready, r + 1)
                        pool.indirect_dma_start(out=out_rows, out_offset=bass.IndirectOffsetOnAxis(ap=t["dest"][:, r:r + 1], axis=0),
                                                in_=res[r % OB][:, :], in_offset=None, bounds_check=NB * S - 1, oob_is_err=False)\
                            .then_inc(scattered[r % OB], 16)
                for p in range(OB):
                    pool.wait_ge(scattered[p], 16 * (NBLK // OB))

            @block.tensor
            def _(pe):
                pe.wait_ge(t["experts_loaded"], 16 * 4 * E)
                held = []

                def turn_u(j, k, m):
                    pe.wait_ge(gathered[k], 16 * m + 16)
                    pe.transpose(uT_ps[k % 2][:, 0:BLK], rows[k][:, 0:D], t["ident"][:, :]).then_inc(u_turned, 1)

                def up(j, k, m):
                    e = first_use(pe, held, j, m)
                    pe.wait_ge(uT_ready, j + 1)
                    pe.matmul(h_ps[k % 2][:, :], uT[k % 2][:, :], w1[:, bass.ds(e, 1), :].rearrange("p a h -> p (a h)"),
                              start=True, stop=True).then_inc(h_done, 1)

                def turn_h(j, k, m):
                    pe.wait_ge(h_ready, j + 1)
                    for c in range(NC):
                        mm = pe.transpose(hT_ps[k % 2][:, c * BLK:(c + 1) * BLK], hb[k % 2][:, c * 128:(c + 1) * 128], t["ident"][:, :])
                    mm.then_inc(h_turned, 1)

                def down(j, k, m):
                    e = second_use(pe, held, j, m)
                    pe.wait_ge(hT_ready, j + 1)
                    wait_before(pe, o_ready, j - 1)
                    for c in range(NC):
                        mm = pe.matmul(o_ps[k % 2][:, 0:D], hT[k % 2][:, c, :], w2[:, bass.ds(e * NC + c, 1), :].rearrange("p a d -> p (a d)"),
                                       start=(c == 0), stop=(c == NC - 1))
                    mm.then_inc(o_done, 1)

                run(pe, [(1, up), (0, down), (2, turn_u), (1, turn_h)])

            @block.scalar
            def _(act):
                def take_u(j, k, m):
                    act.wait_ge(u_turned, j + 1)
                    act.activation(uT[k % 2][:, :], uT_ps[k % 2][:, 0:BLK], ACT.Copy).then_inc(uT_ready, 1)

                def take_h(j, k, m):
                    act.wait_ge(h_turned, j + 1)
                    act.activation(hT[k % 2][:, :, :].rearrange("p c t -> p (c t)"), hT_ps[k % 2][:, :], ACT.Relu).then_inc(hT_ready, 1)

                run(act, [(2, take_u), (1, take_h)])

            @block.vector
            def _(dve):
                dve.wait_ge(t["experts_loaded"], 16 * 4 * E)
                held = []

                def add1(j, k, m):
                    e = first_use(dve, held, j, m)
                    dve.wait_ge(h_done, j + 1)
                    dve.tensor_tensor(hb[k % 2][:, :], h_ps[k % 2][:, :], b1[:, bass.ds(e * EH, EH)], ALU.add).then_inc(h_ready, 1)

                def add2(j, k, m):
                    e = second_use(dve, held, j, m)
                    dve.wait_ge(o_done, j + 1)
                    dve.tensor_tensor(ob[:, :], o_ps[k % 2][:, 0:D], b2[:, bass.ds(e * D, D)], ALU.add).then_inc(o_ready, 1)
                    dve.wait_ge(o_ready, j + 1)
                    dve.tensor_tensor(gated[:, :], ob[:, :], t["gate"][:, bass.ds(j, 1)].to_broadcast([BLK, D]), ALU.mult)\
                       .then_inc(gated_ready, 1)
                    dve.wait_ge(gated_ready, j + 1)
                    wait_before(dve, scattered[k % OB], 16 * (BODY // OB * m + k // OB))
                    dve.tensor_tensor(res[k % OB][:, :], gated[:, :], rows[k][:, D:2 * D], ALU.add).then_inc(res_ready, 1)

                run(dve, [(1, add1), (0, add2)])


def audio_tower(nc, io):
    with ExitStack() as ctx:
        def sb(name, shape, dt=F32):
            return ctx.enter_context(nc.sbuf_tensor(name, shape, dt))

        t = {"ident": sb("ident", [128, 128])}
        with nc.sbuf_tensor("rank_tok", [TT, NT, NG], F32) as rank_tok:
            t["rank_tok"] = rank_tok
            with ExitStack() as inner:
                t["stage3"] = stage3_tensors(lambda name, shape, dt=F32: inner.enter_context(nc.sbuf_tensor(name, shape, dt)))
                norms_and_ranks(nc, t, io)
                sequences(nc, t, io)
        t["z_set"] = ctx.enter_context(nc.semaphore("z_set"))
        t["experts_loaded"] = ctx.enter_context(nc.semaphore("experts_loaded"))
        t["w1"] = sb("w1", [D, E, EH])
        t["w2"] = sb("w2", [128, E * EH // 128, D])
        t["b1"] = sb("b1_rows", [128, E * EH])
        t["b2"] = sb("b2_rows", [128, E * D])
        t["logits"] = sb("logits", [TT, NTILE, E])
        t["row"] = sb("row", [BLK, NBLK], I32)
        t["dest"] = sb("dest", [BLK, NBLK], I32)
        t["gate"] = sb("gate", [BLK, NBLK])
        t["block_expert"] = sb("block_expert", [TT, NBLK], I32)
        tanh_attention(nc, t, io)
        route(nc, t, io)
        experts(nc, t, io)


def constants():
    slot_id = np.arange(NJ, dtype=np.float32)
    slot_id[K_TOP] = -1.0
    slot_id[K_TOP + 1] = -2.0
    return {
        "c_ident": np.eye(128, dtype=np.float32),
        "c_center": (np.eye(D) - 1.0 / D).astype(np.float32),
        "c_iota": np.arange(NJ, dtype=np.float32)[None],
        "c_slot_id": np.ascontiguousarray(slot_id.reshape(2, JT).T),
        "c_e_id": (E - np.arange(E, dtype=np.float32))[None],
        "c_upper": np.triu(np.ones((TT, TT), np.float32), 1),
        "c_blk": np.arange(NBLK, dtype=np.float32)[None],
        "c_slot_row": np.arange(BLK, dtype=np.float32)[None],
        "c_row_id": np.ascontiguousarray(1.0 + np.arange(NTILE * TT, dtype=np.float32).reshape(NTILE, TT).T),
    }


def kernel(**inputs):
    import concourse.bacc as _bacc
    from concourse.bass_utils import run_bass_kernel_spmd as _run

    nc = _bacc.Bacc("TRN2", target_bir_lowering=False, num_devices=1)
    laid = {k: np.ascontiguousarray(v) for k, v in inputs.items()}
    laid["conv_w"] = np.ascontiguousarray(laid.pop("L0_tok_conv_w").transpose(1, 2, 0))
    f1_b = laid.pop("L0_tok_f1_b").reshape(FF // 128, 128)
    laid["cols"] = np.ascontiguousarray(np.stack([laid.pop("L0_tok_" + n) for n in COLS[:7]] + list(f1_b), 1))
    laid.update(constants())
    arrays, io = {}, {}
    for name, a in laid.items():
        arrays[f"in_{name}"] = a
        io[name] = nc.dram_tensor(f"in_{name}", a.shape, mybir.dt.from_np(a.dtype), kind="ExternalInput").ap()
    io["out"] = nc.dram_tensor("out_0", (NB, S, D), F32, kind="ExternalOutput").ap()
    for name, shape, dt in (("q_rows", (NB, TT, NT * D), F32), ("rank_rows", (NG, L), BF16), ("h_rows", (NB, TT, ST * D), F32),
                            ("token_rows", (1 + NB * S, 2 * D), F32)):
        io[name] = nc.dram_tensor(name, shape, dt, kind="Internal").ap()
    audio_tower(nc, io)
    r = _run(nc, [arrays], core_ids=[0])
    return r.results[0]["out_0"]
```
